# Optimizing a Trainium2 kernel written in Bass

```python
import numpy as np
import jax
import jax.numpy as jnp

def _softmax(x, axis=-1):
    return jax.nn.softmax(x, axis=axis)

def _gelu(x):
    return jax.nn.gelu(x, approximate=True)

def _silu(x):
    return jax.nn.silu(x)

def _sigmoid(x):
    return jax.nn.sigmoid(x)

def _layernorm(x, axis=-1, eps=1e-05):
    m = jnp.mean(x, axis=axis, keepdims=True)
    v = jnp.var(x, axis=axis, keepdims=True)
    return (x - m) / jnp.sqrt(v + eps)

def _scatter_add(tgt, idx, src, axis=0):
    return tgt.at[idx].add(src)

def _segment_sum(src, seg, n):
    return jax.ops.segment_sum(src, seg, n)
kernel_name = 'mk_gps_d2_gnn_r8_3cc87e'

def setup_inputs(seed: int=0):
    np.random.seed(seed)
    _w = jnp.asarray

    def _rec_inputs():
        import jax
        import jax.numpy as jnp
        _gk = jax.random.key(seed)
        x = -0.0003713 + 1 * jax.random.normal(jax.random.fold_in(_gk, 1), (6250, 256), jnp.float32)
        src = jax.random.randint(jax.random.fold_in(_gk, 2), (100000,), 0, 6250, jnp.int32)
        dst = jnp.minimum((6250 * jax.random.uniform(jax.random.fold_in(_gk, 3), (100000,)) ** 2.0).astype(jnp.int32), 49999)
        _o = jnp.argsort(dst, stable=True)
        src = src[_o]
        dst = dst[_o]
        return (x, src, dst)
    x, src, dst = _rec_inputs()

    def _L0_gnn_setup():
        import jax, jax.numpy as jnp
        import numpy as np
        N = 6250
        E = 100000
        DIN = 256
        DOUT = 64
        H = 4
        NEG_SLOPE = 0.01
        key = jax.random.key(seed)
        k0, k1, k2, k3, k4 = jax.random.split(key, 5)
        h = jax.random.normal(k0, (N, DIN), dtype=jnp.float32)
        src = jax.random.randint(k1, (E,), 0, N)
        dst = jax.random.randint(k2, (E,), 0, N)
        W = jax.random.normal(k3, (H, DOUT, DIN), dtype=jnp.float32) * np.float32(np.sqrt(2.0) * np.sqrt(2.0 / (DIN + DOUT)))
        att = jax.random.normal(k4, (H, 2 * DOUT), dtype=jnp.float32) * np.float32(np.sqrt(2.0) * np.sqrt(2.0 / (2 * DOUT + 1)))
        return {'h': h, 'src': src, 'dst': dst, 'W': W, 'att': att}
    _L0_gnn_all = _L0_gnn_setup()
    _L0_gnn_in = {k: v for k, v in _L0_gnn_all.items() if k in ('W', 'att')}
    del _L0_gnn_all

    def _L0_mix_setup():
        import jax, jax.numpy as jnp
        import numpy as np
        N, F, C, H = (32, 512, 256, 8)
        D = C // H
        EPS_ATTN = 1e-06
        EPS_LN = 1e-05

        def layer_norm(x, g, b):
            mu = jnp.mean(x, axis=-1, keepdims=True)
            var = jnp.var(x, axis=-1, keepdims=True)
            return (x - mu) * jax.lax.rsqrt(var + EPS_LN) * g + b
        key = jax.random.key(seed)
        ks = jax.random.split(key, 8)
        s = 1.0 / np.sqrt(C)
        return {'x': jax.random.normal(ks[0], (N, F, C), jnp.float32), 'Wqkv': jax.random.uniform(ks[1], (3 * C, C), jnp.float32, -s, s), 'ln1_g': jnp.ones((C,), jnp.float32), 'ln1_b': jnp.zeros((C,), jnp.float32), 'W1': jax.random.uniform(ks[2], (C, C), jnp.float32, -s, s), 'b1': jax.random.uniform(ks[3], (C,), jnp.float32, -s, s), 'W2': jax.random.uniform(ks[4], (C, C), jnp.float32, -s, s), 'b2': jax.random.uniform(ks[5], (C,), jnp.float32, -s, s), 'ln2_g': jnp.ones((C,), jnp.float32), 'ln2_b': jnp.zeros((C,), jnp.float32)}
    _L0_mix_all = _L0_mix_setup()
    _L0_mix_in = {k: v for k, v in _L0_mix_all.items() if k in ('Wqkv', 'ln1_g', 'ln1_b', 'W1', 'b1', 'W2', 'b2', 'ln2_g', 'ln2_b')}
    del _L0_mix_all

    def _L0_ffn_setup():
        import math
        import jax, jax.numpy as jnp
        import numpy as np
        CAPACITY_FACTOR = 1.25
        key = jax.random.key(seed)
        ks = jax.random.split(key, 5)
        B, L, D, F, E = (8, 1024, 256, 1024, 8)
        h = jax.random.normal(ks[0], (B, L, D), dtype=jnp.float32)
        gate_w = jax.random.normal(ks[1], (D, E), dtype=jnp.float32) * 0.02
        gate_b = jnp.zeros((E,), dtype=jnp.float32)
        w1 = jax.random.normal(ks[2], (E, D, F), dtype=jnp.float32) * (1.0 / math.sqrt(D))
        b1 = jnp.zeros((E, F), dtype=jnp.float32)
        w2 = jax.random.normal(ks[3], (E, F, D), dtype=jnp.float32) * (1.0 / math.sqrt(F))
        b2 = jnp.zeros((E, D), dtype=jnp.float32)
        return {'h': h, 'gate_w': gate_w, 'gate_b': gate_b, 'w1': w1, 'b1': b1, 'w2': w2, 'b2': b2}
    _L0_ffn_all = _L0_ffn_setup()
    _L0_ffn_in = {k: v for k, v in _L0_ffn_all.items() if k in ('gate_w', 'gate_b', 'w1', 'b1', 'w2', 'b2')}
    del _L0_ffn_all

    def _L1_gnn_setup():
        import jax, jax.numpy as jnp
        import numpy as np
        N_NODES = 6250
        N_EDGES = 100000
        IN_F = 256
        HEADS = 4
        OUT_F = 64
        NEG_SLOPE = 0.2
        key = jax.random.key(seed)
        k1, k2, k3, k4, k5 = jax.random.split(key, 5)
        x = jax.random.normal(k1, (N_NODES, IN_F), dtype=jnp.float32)
        edge_index = jax.random.randint(k2, (2, N_EDGES), 0, N_NODES, dtype=jnp.int64)
        W = jax.random.normal(k3, (IN_F, HEADS * OUT_F), dtype=jnp.float32) * (1.0 / np.sqrt(IN_F))
        att_src = jax.random.normal(k4, (1, HEADS, OUT_F), dtype=jnp.float32) * (1.0 / np.sqrt(OUT_F))
        att_dst = jax.random.normal(k5, (1, HEADS, OUT_F), dtype=jnp.float32) * (1.0 / np.sqrt(OUT_F))
        bias = jnp.zeros((HEADS * OUT_F,), dtype=jnp.float32)
        return {'x': x, 'edge_index': edge_index, 'W': W, 'att_src': att_src, 'att_dst': att_dst, 'bias': bias}
    _L1_gnn_all = _L1_gnn_setup()
    _L1_gnn_in = {k: v for k, v in _L1_gnn_all.items() if k in ('W', 'att_src', 'att_dst', 'bias')}
    del _L1_gnn_all

    def _L1_mix_setup():
        import jax, jax.numpy as jnp
        import numpy as np
        BN_EPS = 1e-05
        key = jax.random.key(seed)
        ks = jax.random.split(key, 4)
        B, N, D = (8, 1024, 256)
        outD = 256
        s = 1.0 / np.sqrt(D)
        return {'feature': jax.random.normal(ks[0], (B, N, D), dtype=jnp.float32), 'W_qk': jax.random.normal(ks[1], (2, D, D), dtype=jnp.float32) * s, 'b_qk': jnp.zeros((2, D), dtype=jnp.float32), 'W_v': jax.random.normal(ks[2], (D, outD), dtype=jnp.float32) * s, 'b_v': jnp.zeros((outD,), dtype=jnp.float32), 'gamma': jnp.ones((D,), dtype=jnp.float32), 'beta': jnp.zeros((D,), dtype=jnp.float32)}
    _L1_mix_all = _L1_mix_setup()
    _L1_mix_in = {k: v for k, v in _L1_mix_all.items() if k in ('W_qk', 'b_qk', 'W_v', 'b_v', 'gamma', 'beta')}
    del _L1_mix_all

    def _L1_ffn_setup():
        import math
        import jax, jax.numpy as jnp
        import numpy as np
        CAPACITY_FACTOR = 1.25
        TOP_K = 2
        LN_EPS = 1e-05

        def _layer_norm(x, gamma, beta):
            mu = jnp.mean(x, axis=-1, keepdims=True)
            var = jnp.var(x, axis=-1, keepdims=True)
            return (x - mu) * jax.lax.rsqrt(var + LN_EPS) * gamma + beta
        key = jax.random.key(seed)
        ks = jax.random.split(key, 4)
        B, S, D, F, E = (8, 512, 256, 512, 8)
        x = jax.random.normal(ks[0], (B, S, D), dtype=jnp.float32)
        Wr = jax.random.normal(ks[1], (D, E), dtype=jnp.float32) / np.sqrt(D)
        br = jnp.zeros((E,), jnp.float32)
        W1 = jax.random.normal(ks[2], (E, D, F), dtype=jnp.float32) / np.sqrt(D)
        b1 = jnp.zeros((E, F), jnp.float32)
        W2 = jax.random.normal(ks[3], (E, F, D), dtype=jnp.float32) / np.sqrt(F)
        b2 = jnp.zeros((E, D), jnp.float32)
        gamma = jnp.ones((D,), jnp.float32)
        beta = jnp.zeros((D,), jnp.float32)
        return {'x': x, 'Wr': Wr, 'br': br, 'W1': W1, 'b1': b1, 'W2': W2, 'b2': b2, 'gamma': gamma, 'beta': beta}
    _L1_ffn_all = _L1_ffn_setup()
    _L1_ffn_in = {k: v for k, v in _L1_ffn_all.items() if k in ('Wr', 'br', 'W1', 'b1', 'W2', 'b2', 'gamma', 'beta')}
    del _L1_ffn_all
    return {'x': x, 'src': src, 'dst': dst, 'L0_gnn_W': _L0_gnn_in['W'], 'L0_gnn_att': _L0_gnn_in['att'], 'L0_mix_Wqkv': _L0_mix_in['Wqkv'], 'L0_mix_ln1_g': _L0_mix_in['ln1_g'], 'L0_mix_ln1_b': _L0_mix_in['ln1_b'], 'L0_mix_W1': _L0_mix_in['W1'], 'L0_mix_b1': _L0_mix_in['b1'], 'L0_mix_W2': _L0_mix_in['W2'], 'L0_mix_b2': _L0_mix_in['b2'], 'L0_mix_ln2_g': _L0_mix_in['ln2_g'], 'L0_mix_ln2_b': _L0_mix_in['ln2_b'], 'L0_ffn_gate_w': _L0_ffn_in['gate_w'], 'L0_ffn_gate_b': _L0_ffn_in['gate_b'], 'L0_ffn_w1': _L0_ffn_in['w1'], 'L0_ffn_b1': _L0_ffn_in['b1'], 'L0_ffn_w2': _L0_ffn_in['w2'], 'L0_ffn_b2': _L0_ffn_in['b2'], 'L1_gnn_W': _L1_gnn_in['W'], 'L1_gnn_att_src': _L1_gnn_in['att_src'], 'L1_gnn_att_dst': _L1_gnn_in['att_dst'], 'L1_gnn_bias': _L1_gnn_in['bias'], 'L1_mix_W_qk': _L1_mix_in['W_qk'], 'L1_mix_b_qk': _L1_mix_in['b_qk'], 'L1_mix_W_v': _L1_mix_in['W_v'], 'L1_mix_b_v': _L1_mix_in['b_v'], 'L1_mix_gamma': _L1_mix_in['gamma'], 'L1_mix_beta': _L1_mix_in['beta'], 'L1_ffn_Wr': _L1_ffn_in['Wr'], 'L1_ffn_br': _L1_ffn_in['br'], 'L1_ffn_W1': _L1_ffn_in['W1'], 'L1_ffn_b1': _L1_ffn_in['b1'], 'L1_ffn_W2': _L1_ffn_in['W2'], 'L1_ffn_b2': _L1_ffn_in['b2'], 'L1_ffn_gamma': _L1_ffn_in['gamma'], 'L1_ffn_beta': _L1_ffn_in['beta']}

def reference(x, src, dst, L0_gnn_W, L0_gnn_att, L0_mix_Wqkv, L0_mix_ln1_g, L0_mix_ln1_b, L0_mix_W1, L0_mix_b1, L0_mix_W2, L0_mix_b2, L0_mix_ln2_g, L0_mix_ln2_b, L0_ffn_gate_w, L0_ffn_gate_b, L0_ffn_w1, L0_ffn_b1, L0_ffn_w2, L0_ffn_b2, L1_gnn_W, L1_gnn_att_src, L1_gnn_att_dst, L1_gnn_bias, L1_mix_W_qk, L1_mix_b_qk, L1_mix_W_v, L1_mix_b_v, L1_mix_gamma, L1_mix_beta, L1_ffn_Wr, L1_ffn_br, L1_ffn_W1, L1_ffn_b1, L1_ffn_W2, L1_ffn_b2, L1_ffn_gamma, L1_ffn_beta):
    import jax
    import jax.numpy as jnp

    def _L0_gnn_ref(h, src, dst, W, att):
        import jax, jax.numpy as jnp
        import numpy as np
        N = 6250
        E = 100000
        DIN = 256
        DOUT = 64
        H = 4
        NEG_SLOPE = 0.01
        z = jnp.einsum('ni,hoi->hno', h, W)
        a_src, a_dst = (att[:, :DOUT], att[:, DOUT:])
        e_src = jnp.einsum('hno,ho->hn', z, a_src)
        e_dst = jnp.einsum('hno,ho->hn', z, a_dst)
        e = e_src[:, src] + e_dst[:, dst]
        e = jnp.where(e > 0, e, NEG_SLOPE * e)

        def per_head(e_h, z_h):
            m = jax.ops.segment_max(e_h, dst, num_segments=N)
            m = jnp.where(jnp.isfinite(m), m, 0.0)
            ex = jnp.exp(e_h - m[dst])
            den = jax.ops.segment_sum(ex, dst, num_segments=N)
            alpha = ex / jnp.maximum(den[dst], jnp.float32(1e-16))
            return jax.ops.segment_sum(alpha[:, None] * z_h[src], dst, num_segments=N)
        out = jax.vmap(per_head)(e, z)
        return jnp.transpose(out, (1, 0, 2)).reshape(N, H * DOUT)

    def _L0_mix_ref(x, Wqkv, ln1_g, ln1_b, W1, b1, W2, b2, ln2_g, ln2_b):
        import jax, jax.numpy as jnp
        import numpy as np
        N, F, C, H = (32, 512, 256, 8)
        D = C // H
        EPS_ATTN = 1e-06
        EPS_LN = 1e-05

        def layer_norm(x, g, b):
            mu = jnp.mean(x, axis=-1, keepdims=True)
            var = jnp.var(x, axis=-1, keepdims=True)
            return (x - mu) * jax.lax.rsqrt(var + EPS_LN) * g + b
        n, f, c = x.shape
        qkv = jnp.einsum('nfc,oc->nfo', x, Wqkv)
        q, k, v = jnp.split(qkv, 3, axis=-1)
        q = q.reshape(n, f, H, D)
        k = k.reshape(n, f, H, D)
        v = v.reshape(n, f, H, D)
        q = jax.nn.elu(q) + 1.0
        k = jax.nn.elu(k) + 1.0
        kv = jnp.einsum('nshd,nshm->nhmd', k, v)
        ksum = jnp.sum(k, axis=1)
        z = 1.0 / (jnp.einsum('nlhd,nhd->nlh', q, ksum) + EPS_ATTN)
        t = jnp.einsum('nlhd,nhmd,nlh->nlhm', q, kv, z)
        t = t.reshape(n, f, c)
        x1 = layer_norm(t + x, ln1_g, ln1_b)
        h = jax.nn.gelu(jnp.einsum('nfc,oc->nfo', x1, W1) + b1, approximate=False)
        y = jnp.einsum('nfc,oc->nfo', h, W2) + b2
        return layer_norm(y + x1, ln2_g, ln2_b)

    def _L0_ffn_ref(h, gate_w, gate_b, w1, b1, w2, b2):
        import math
        import jax, jax.numpy as jnp
        import numpy as np
        CAPACITY_FACTOR = 1.25
        B, L, D = h.shape
        E = gate_w.shape[1]
        T = B * L
        C = max(1, math.ceil(CAPACITY_FACTOR * T / E))
        x = h.reshape(T, D)
        logits = x @ gate_w + gate_b
        probs = jax.nn.softmax(logits, axis=-1)
        idx = jnp.argmax(probs, axis=-1)
        prb = jnp.take_along_axis(probs, idx[:, None], axis=1)[:, 0]
        one_hot = jax.nn.one_hot(idx, E, dtype=jnp.float32)
        pos = (jnp.cumsum(one_hot, axis=0) * one_hot).sum(-1).astype(jnp.int32) - 1
        kept = pos < C
        pos_safe = jnp.where(kept, pos, C)
        buf = jnp.zeros((E, C, D), dtype=h.dtype).at[idx, pos_safe].set(x, mode='drop')
        hmid = jax.nn.relu(jnp.einsum('ecd,edf->ecf', buf, w1) + b1[:, None, :])
        ybuf = jnp.einsum('ecf,efd->ecd', hmid, w2) + b2[:, None, :]
        pos_g = jnp.minimum(pos, C - 1)
        y_tok = ybuf[idx, pos_g] * (prb * kept)[:, None]
        y = y_tok.reshape(B, L, D)
        y = jnp.nan_to_num(y, nan=0.0, posinf=10000.0, neginf=-10000.0)
        return y

    def _L1_gnn_ref(x, edge_index, W, att_src, att_dst, bias):
        import jax, jax.numpy as jnp
        import numpy as np
        N_NODES = 6250
        N_EDGES = 100000
        IN_F = 256
        HEADS = 4
        OUT_F = 64
        NEG_SLOPE = 0.2
        N = x.shape[0]
        h = (x @ W).reshape(N, HEADS, OUT_F)
        a_src = jnp.sum(h * att_src, axis=-1)
        a_dst = jnp.sum(h * att_dst, axis=-1)
        loop = jnp.arange(N, dtype=edge_index.dtype)
        src = jnp.concatenate([edge_index[0], loop])
        dst = jnp.concatenate([edge_index[1], loop])
        e = jax.nn.leaky_relu(a_src[src] + a_dst[dst], negative_slope=NEG_SLOPE)
        e_max = jax.lax.stop_gradient(jax.ops.segment_max(e, dst, num_segments=N))
        e_max = jnp.where(jnp.isfinite(e_max), e_max, 0.0)
        ex = jnp.exp(e - e_max[dst])
        denom = jax.ops.segment_sum(ex, dst, num_segments=N)
        alpha = ex / denom[dst]
        msg = h[src] * alpha[..., None]
        out = jax.ops.segment_sum(msg, dst, num_segments=N)
        return out.reshape(N, HEADS * OUT_F) + bias

    def _L1_mix_ref(feature, W_qk, b_qk, W_v, b_v, gamma, beta):
        import jax, jax.numpy as jnp
        import numpy as np
        BN_EPS = 1e-05
        QK = jnp.einsum('bnd,kde->bkne', feature, W_qk) + b_qk[None, :, None, :]
        value = jnp.einsum('bnd,de->bne', feature, W_v) + b_v
        query = QK[:, 0]
        key = QK[:, 1]
        sm = jax.nn.softmax(key, axis=1)
        lam = jnp.einsum('bnd,bne->bde', sm, value)
        mean = jnp.mean(lam, axis=(0, 2), keepdims=True)
        var = jnp.var(lam, axis=(0, 2), keepdims=True)
        bn = (lam - mean) * jax.lax.rsqrt(var + BN_EPS)
        bn = bn * gamma[None, :, None] + beta[None, :, None]
        return jnp.einsum('bnd,bde->bne', query, bn)

    def _L1_ffn_ref(x, Wr, br, W1, b1, W2, b2, gamma, beta):
        import math
        import jax, jax.numpy as jnp
        import numpy as np
        CAPACITY_FACTOR = 1.25
        TOP_K = 2
        LN_EPS = 1e-05

        def _layer_norm(x, gamma, beta):
            mu = jnp.mean(x, axis=-1, keepdims=True)
            var = jnp.var(x, axis=-1, keepdims=True)
            return (x - mu) * jax.lax.rsqrt(var + LN_EPS) * gamma + beta
        B, S, D = x.shape
        E = Wr.shape[1]
        N = B * S
        K = TOP_K
        logits = jnp.mean(x, axis=1) @ Wr + br
        routing_weights = jax.nn.softmax(logits, axis=-1)
        capacity = float(math.ceil(N * CAPACITY_FACTOR / E))
        expected_loads = routing_weights.sum(axis=0) * (N / B)
        scale = jnp.where(expected_loads > capacity, capacity / expected_loads, 1.0)
        routing_weights = jax.nn.softmax(routing_weights * scale, axis=-1)
        rw_tok = jnp.broadcast_to(routing_weights[:, None, :], (B, S, E)).reshape(N, E)
        top_w, top_i = jax.lax.top_k(rw_tok, K)
        top_w = jax.nn.softmax(top_w, axis=-1)
        xf = x.reshape(N, D)
        h = jax.nn.gelu(jnp.einsum('nd,edf->enf', xf, W1) + b1[:, None, :], approximate=False)
        y = jnp.einsum('enf,efd->end', h, W2) + b2[:, None, :]
        w_dense = jnp.zeros((N, E), x.dtype).at[jnp.arange(N)[:, None], top_i].add(top_w)
        out = jnp.einsum('ne,end->nd', w_dense, y).reshape(B, S, D)
        out = _layer_norm(out + x, gamma, beta)
        return out
    edge_index = jnp.stack([src, dst])
    xn = _layernorm(x, axis=-1)
    x = x + _L0_gnn_ref(xn, src, dst, L0_gnn_W, L0_gnn_att) + _L0_mix_ref(xn[None], L0_mix_Wqkv, L0_mix_ln1_g, L0_mix_ln1_b, L0_mix_W1, L0_mix_b1, L0_mix_W2, L0_mix_b2, L0_mix_ln2_g, L0_mix_ln2_b)[0]
    x = x + _L0_ffn_ref(_layernorm(x, axis=-1)[None], L0_ffn_gate_w, L0_ffn_gate_b, L0_ffn_w1, L0_ffn_b1, L0_ffn_w2, L0_ffn_b2)[0]
    xn = _layernorm(x, axis=-1)
    x = x + _L1_gnn_ref(xn, edge_index, L1_gnn_W, L1_gnn_att_src, L1_gnn_att_dst, L1_gnn_bias) + _L1_mix_ref(xn[None], L1_mix_W_qk, L1_mix_b_qk, L1_mix_W_v, L1_mix_b_v, L1_mix_gamma, L1_mix_beta)[0]
    x = x + _L1_ffn_ref(_layernorm(x, axis=-1)[None], L1_ffn_Wr, L1_ffn_br, L1_ffn_W1, L1_ffn_b1, L1_ffn_W2, L1_ffn_b2, L1_ffn_gamma, L1_ffn_beta)[0]
    return x

_drawn_inputs = setup_inputs


def setup_inputs(seed=0):
    import zlib

    import numpy as np

    out = dict(_drawn_inputs(seed))
    spreads = {'L0_mix_ln1_g': (1.0, 0.2),
     'L0_mix_ln1_b': (0.0, 0.1),
     'L0_mix_ln2_g': (1.0, 0.2),
     'L0_mix_ln2_b': (0.0, 0.1),
     'L0_ffn_gate_b': (0.0, 0.1),
     'L0_ffn_b1': (0.0, 0.8),
     'L0_ffn_b2': (0.0, 0.552),
     'L1_gnn_bias': (0.0, 0.8),
     'L1_mix_b_qk': (0.0, 0.1),
     'L1_mix_b_v': (0.0, 0.1),
     'L1_mix_gamma': (1.0, 0.2),
     'L1_mix_beta': (0.0, 0.1),
     'L1_ffn_br': (0.0, 0.8),
     'L1_ffn_b1': (0.0, 0.8),
     'L1_ffn_b2': (0.0, 0.8),
     'L1_ffn_gamma': (1.0, 0.6),
     'L1_ffn_beta': (0.0, 0.8)}
    factors = {'L0_mix_Wqkv': 2.806, 'L1_gnn_att_src': 4.413, 'L1_gnn_att_dst': 8.0}
    for name, (base, spread) in spreads.items():
        noise = np.random.default_rng([zlib.crc32(name.encode()), seed]).standard_normal(out[name].shape)
        drawn = base * np.exp(spread * noise) if base else spread * noise
        out[name] = jnp.asarray(drawn.astype(out[name].dtype))
    for name, factor in factors.items():
        out[name] = (out[name] * factor).astype(out[name].dtype)
    return out
```

```python
import concourse.bass as bass
from concourse import mybir
from contextlib import ExitStack

F32 = mybir.dt.float32
BF16 = mybir.dt.bfloat16
I32 = mybir.dt.int32
ALU = mybir.AluOpType
ACT = mybir.ActivationFunctionType
AX = mybir.AxisListType

N, E, D = 6250, 100000, 256
P, T = 125, 50
J = 125
C = E // J
CP, CK = 100, 8
BC = 40
NB = C // BC
GC = 10
NG = BC // GC
HEADS, DO = 4, 64
ZW = D + HEADS
GW = D + 2 * HEADS
BIG = 1e38
OOB = 200000.0
ROUND = 12582912.0


class Count:

    def __init__(self, e, sem):
        self.e, self.sem, self.n = e, sem, 0

    def next(self):
        self.n += 1
        return self.n

    def reset(self):
        if self.n:
            self.e.sem_inc(self.sem, -self.n)
            self.n = 0


def steps(e, n, body):
    with e.Fori(0, n // 2) as i:
        body(i * 2, 0)
        body(i * 2 + 1, 1)
    if n % 2:
        body(n - 1, 0)


class Mem:

    def __init__(self, nc, stage):
        self.nc, self.stage, self.ctx, self.sems = nc, stage, ExitStack(), []

    def __enter__(self):
        return self

    def __exit__(self, *a):
        if self.sems:
            self.nc.clear_and_free_semaphores(self.sems)
            self.nc.all_engine_barrier()
        self.ctx.close()

    def sb(self, name, shape, dt=F32):
        return self.ctx.enter_context(self.nc.sbuf_tensor(f"{self.stage}_{name}", shape, dt))

    def ps(self, name, shape=(128, 512), dt=F32):
        return self.ctx.enter_context(self.nc.psum_tensor(f"{self.stage}_{name}", list(shape), dt))

    def sem(self, name):
        self.sems.append(self.nc.alloc_semaphore(f"{self.stage}_{name}"))
        return self.sems[-1]

    def counter(self, name):
        return self.nc.alloc_semaphore(f"{self.stage}_{name}")


class Edges:

    def __init__(self, m):
        self.gT = m.sb("gT", [P, C])
        self.srcT = m.sb("srcT", [P, C + BC], I32)
        self.start = m.sb("start", [BC, NB * J])
        self.main_row = m.sb("main_row", [P, T], I32)
        self.extra_row = m.sb("extra_row", [P, T], I32)
        self.edge_row = m.sb("edge_row", [P, T], I32)
        self.first_node = m.sb("first_node", [CP, CK], I32)
        self.first_nodef = m.sb("first_nodef", [CP, CK])
        self.first_row = m.sb("first_row", [CP, CK], I32)
        self.cont = m.sb("cont", [CP, CK])
        self.first_all = m.sb("first_all", [CP, C])
        self.group_mask = m.sb("group_mask", [HEADS, C + 1])


def edge_tables(nc, ed, const, src, dst, start_dram):
    ident, tri, iota, rowbase = const.ident, const.tri, const.iota, const.rowbase
    W = CK * J
    with Mem(nc, "et") as m:
        srcn = m.sb("srcn", [CP, W], I32)
        dstx = m.sb("dstx", [CP, W + 1], I32)
        dstf = m.sb("dstf", [CP, W + 1])
        start = m.sb("start", [CP, W])
        ones = m.sb("ones", [CP, W])
        seg = m.sb("seg", [CP, W])
        t1 = m.sb("t1", [CP, W])
        t2 = m.sb("t2", [CP, W])
        hi = m.sb("hi", [CP, W])
        lo = m.sb("lo", [CP, W])
        srcf = m.sb("srcf", [CP, W])
        hiT = m.sb("hiT", [P, C])
        loT = m.sb("loT", [P, C])
        ohi = m.sb("ohi", [P, 2, GC, P], BF16)
        olo = m.sb("olo", [P, 2, GC, T], BF16)
        cnt = m.sb("cnt", [P, T])
        ncum = m.sb("ncum", [P, 2, T])
        nb = m.sb("nb", [P, 8, T])
        tot = m.sb("tot", [P, 2])
        frow = m.sb("frow", [1, C], I32)
        frowf = m.sb("frowf", [1, C])
        pst = m.ps("pst", [128, 2, 4, 128])
        pcnt = m.ps("pcnt")
        poff = m.ps("poff")
        pfa = m.ps("pfa", [128, 2, 512])
        loaded = m.sem("loaded")
        loaded2 = m.sem("loaded2")
        floaded = m.sem("floaded")
        ch = m.sem("ch")
        ready = m.sem("ready")
        tr_done = m.sem("tr_done")
        tr_free = m.sem("tr_free")
        totals = m.sem("totals")
        offs = m.sem("offs")
        oh_ready = [m.sem("oh_ready0"), m.sem("oh_ready1")]
        oh_free = [m.sem("oh_free0"), m.sem("oh_free1")]
        counted = m.sem("counted")
        ntot = m.sem("ntot")
        noff = m.sem("noff")
        fready = m.sem("fready")
        fall = m.sem("fall")
        stored = m.sem("stored")
        st_ready = m.sem("st_ready")
        st_loaded = m.sem("st_loaded")
        with nc.Block() as block:

            @block.sync
            def _(e):
                e.dma_start(srcn[:, :], src.rearrange("(p w) -> p w", p=CP)).then_inc(loaded, 16)
                e.wait_ge(loaded, 16)
                e.sem_inc(loaded, -16)
                e.dma_start(dstx[:, 1:W + 1], dst.rearrange("(p w) -> p w", p=CP)).then_inc(loaded, 16)
                e.wait_ge(loaded, 16)
                e.sem_inc(loaded, -16)
                with nc.allow_non_contiguous_dma(reason="99 single elements"):
                    e.dma_start(dstx[1:CP, 0:1], dst.rearrange("(p w) -> p w", p=CP)[0:CP - 1, W - 1:W]).then_inc(loaded, 16)
                    e.wait_ge(loaded, 16)
                    e.sem_inc(loaded, -16)
                    e.dma_start(frow[:, :], dst.rearrange("(a c j) -> a c j", a=1, j=J)[:, :, 0]).then_inc(floaded, 16)
                e.sem_inc(loaded2, 1)
                e.wait_ge(st_ready, 1)
                e.sem_inc(st_ready, -1)
                e.dma_start(start_dram.rearrange("(p k) j -> p (k j)", p=CP), start[:, :]).then_inc(stored, 16)
                e.wait_ge(stored, 16)
                e.sem_inc(stored, -16)
                e.dma_start(ed.start[:, :].rearrange("k (b j) -> k b j", j=J), start_dram.rearrange("(b k) j -> k b j", k=BC)).then_inc(st_loaded, 16)

            @block.vector
            def _(e):
                v = nc.vector
                c = Count(e, ch)
                v.memset(dstx[0:1, 0:1], -1).then_inc(ch, 1)
                e.wait_ge(ch, c.next())
                v.memset(ones[:, :], 1.0).then_inc(ch, 1)
                e.wait_ge(ch, c.next())
                v.memset(ed.srcT[:, C:C + BC], 0).then_inc(ch, 1)
                e.wait_ge(ch, c.next())
                e.wait_ge(loaded2, 1)
                e.sem_inc(loaded2, -1)
                v.tensor_copy(srcf[:, :], srcn[:, :])
                v.tensor_copy(dstf[:, :], dstx[:, :]).then_inc(ch, 1)
                e.wait_ge(ch, c.next())
                v.tensor_tensor(out=start[:, :], in0=dstf[:, 1:W + 1], in1=dstf[:, 0:W], op=ALU.not_equal).then_inc(ch, 1)
                e.wait_ge(ch, c.next())
                e.sem_inc(st_ready, 1)
                v.tensor_tensor_scan(out=seg[:, :], data0=ones[:, :], data1=start[:, :], initial=0.0,
                                     op0=ALU.mult, op1=ALU.add).then_inc(ch, 1)
                e.wait_ge(ch, c.next())
                v.tensor_copy(tot[:CP, 0:1], seg[:, W - 1:W]).then_inc(totals, 1)
                v.tensor_scalar(t1[:, :], dstf[:, 1:W + 1], 0.5, 1.0 / T, ALU.add, ALU.mult).then_inc(ch, 1)
                e.wait_ge(ch, c.next())
                v.tensor_scalar(t1[:, :], t1[:, :], -0.5, ROUND, ALU.add, ALU.add).then_inc(ch, 1)
                e.wait_ge(ch, c.next())
                v.tensor_scalar(hi[:, :], t1[:, :], -ROUND, None, ALU.add).then_inc(ch, 1)
                e.wait_ge(ch, c.next())
                v.scalar_tensor_tensor(lo[:, :], hi[:, :], -float(T), dstf[:, 1:W + 1], ALU.mult, ALU.add).then_inc(ch, 1)
                e.wait_ge(ch, c.next())
                e.wait_ge(offs, 1)
                e.sem_inc(offs, -1)
                v.tensor_scalar(seg[:, :], seg[:, :], poff[:CP, 0:1], -1.0, ALU.add, ALU.add).then_inc(ch, 1)
                e.wait_ge(ch, c.next())
                v.tensor_scalar(t1[:, :], seg[:, :], 0.5, 1.0 / J, ALU.add, ALU.mult).then_inc(ch, 1)
                e.wait_ge(ch, c.next())
                v.tensor_scalar(t1[:, :], t1[:, :], -0.5, ROUND, ALU.add, ALU.add).then_inc(ch, 1)
                e.wait_ge(ch, c.next())
                v.tensor_scalar(t1[:, :], t1[:, :], -ROUND, None, ALU.add).then_inc(ch, 1)
                e.wait_ge(ch, c.next())
                v.scalar_tensor_tensor(t2[:, :], t1[:, :], -float(J), seg[:, :], ALU.mult, ALU.add).then_inc(ch, 1)
                e.wait_ge(ch, c.next())
                e.sem_inc(ready, 1)
                for k in range(CK):
                    e.wait_ge(tr_done, 1)
                    e.sem_inc(tr_done, -1)
                    for n, tab in enumerate((ed.gT, ed.srcT, hiT, loT)):
                        ins = v.tensor_copy(tab[:, 0:C].rearrange("j (p k) -> j p k", k=CK)[:, :, k], pst[:J, k % 2, n, :CP])
                    ins.then_inc(tr_free, 1)
                sv = start[:, :].rearrange("p (k j) -> p k j", j=J)[:, :, 0]
                v.tensor_scalar(ed.cont[:, :], sv, -1.0, 1.0, ALU.mult, ALU.add).then_inc(ch, 1)
                e.wait_ge(ch, c.next())
                v.tensor_copy(ed.first_nodef[:, :], dstf[:, 1:W + 1].rearrange("p (k j) -> p k j", j=J)[:, :, 0]).then_inc(ch, 1)
                e.wait_ge(ch, c.next())
                v.tensor_copy(ed.first_node[:, :], ed.first_nodef[:, :]).then_inc(ch, 1)
                e.wait_ge(ch, c.next())
                v.scalar_tensor_tensor(t1[:, 0:CK], t2[:, :].rearrange("p (k j) -> p k j", j=J)[:, :, 0], float(BC),
                                       rowbase[:CP, :], ALU.mult, ALU.add).then_inc(ch, 1)
                e.wait_ge(ch, c.next())
                v.tensor_copy(ed.first_row[:, :], t1[:, 0:CK]).then_inc(ch, 1)
                e.wait_ge(ch, c.next())
                e.sem_inc(oh_free[0], 1)
                e.sem_inc(oh_free[1], 1)
                c.reset()

                def body(g, par):
                    e.wait_ge(oh_free[par], 1)
                    e.sem_inc(oh_free[par], -1)
                    v.tensor_tensor(out=ohi[:, par], in0=iota[:P, 0:P].unsqueeze(1).to_broadcast([P, GC, P]),
                                    in1=hiT[:, bass.ds(g * GC, GC)].unsqueeze(2).to_broadcast([P, GC, P]),
                                    op=ALU.is_equal)
                    v.tensor_tensor(out=olo[:, par], in0=iota[:P, 0:T].unsqueeze(1).to_broadcast([P, GC, T]),
                                    in1=loT[:, bass.ds(g * GC, GC)].unsqueeze(2).to_broadcast([P, GC, T]),
                                    op=ALU.is_equal).then_inc(oh_ready[par], 1)
                steps(e, C // GC, body)
                e.wait_ge(counted, 1)
                e.sem_inc(counted, -1)
                v.tensor_copy(cnt[:, :], pcnt[:P, 0:T]).then_inc(ch, 1)
                e.wait_ge(ch, c.next())
                v.tensor_scalar(nb[:, 0, :], cnt[:, :], 0.0, None, ALU.is_gt).then_inc(ch, 1)
                e.wait_ge(ch, c.next())
                v.tensor_tensor_scan(out=ncum[:, 0, :], data0=iota[:P, 1:2].to_broadcast([P, T]), data1=cnt[:, :], initial=0.0,
                                     op0=ALU.mult, op1=ALU.add).then_inc(ch, 1)
                e.wait_ge(ch, c.next())
                v.tensor_tensor_scan(out=ncum[:, 1, :], data0=iota[:P, 1:2].to_broadcast([P, T]), data1=nb[:, 0, :], initial=0.0,
                                     op0=ALU.mult, op1=ALU.add).then_inc(ch, 1)
                e.wait_ge(ch, c.next())
                v.tensor_copy(tot[:, 0:2], ncum[:, :, T - 1]).then_inc(ntot, 1)
                e.wait_ge(noff, 1)
                e.sem_inc(noff, -1)
                v.tensor_scalar(ncum[:, 0, :], ncum[:, 0, :], poff[:P, 4:5], None, ALU.add).then_inc(ch, 1)
                e.wait_ge(ch, c.next())
                v.tensor_scalar(ncum[:, 1, :], ncum[:, 1, :], poff[:P, 5:6], None, ALU.add).then_inc(ch, 1)
                e.wait_ge(ch, c.next())
                v.tensor_tensor(out=nb[:, 1, :], in0=ncum[:, 0, :], in1=cnt[:, :], op=ALU.subtract).then_inc(ch, 1)
                e.wait_ge(ch, c.next())
                v.tensor_tensor(out=nb[:, 2, :], in0=ncum[:, 1, :], in1=nb[:, 0, :], op=ALU.subtract).then_inc(ch, 1)
                e.wait_ge(ch, c.next())

                def floordiv(dst_, src_, d):
                    v.tensor_scalar(dst_, src_, 0.5, 1.0 / d, ALU.add, ALU.mult).then_inc(ch, 1)
                    e.wait_ge(ch, c.next())
                    v.tensor_scalar(dst_, dst_, -0.5, ROUND, ALU.add, ALU.add).then_inc(ch, 1)
                    e.wait_ge(ch, c.next())
                    v.tensor_scalar(dst_, dst_, -ROUND, None, ALU.add).then_inc(ch, 1)
                    e.wait_ge(ch, c.next())

                floordiv(nb[:, 3, :], nb[:, 1, :], J)
                floordiv(nb[:, 4, :], nb[:, 2, :], J)
                v.scalar_tensor_tensor(nb[:, 2, :], nb[:, 4, :], -float(J), nb[:, 2, :], ALU.mult, ALU.add).then_inc(ch, 1)
                e.wait_ge(ch, c.next())
                floordiv(nb[:, 4, :], nb[:, 3, :], BC)
                v.scalar_tensor_tensor(nb[:, 5, :], nb[:, 4, :], float(P * BC - BC), nb[:, 3, :], ALU.mult, ALU.add).then_inc(ch, 1)
                e.wait_ge(ch, c.next())
                v.scalar_tensor_tensor(nb[:, 5, :], nb[:, 2, :], float(BC), nb[:, 5, :], ALU.mult, ALU.add).then_inc(ch, 1)
                e.wait_ge(ch, c.next())
                v.tensor_scalar(nb[:, 6, :], nb[:, 0, :], -OOB, OOB, ALU.mult, ALU.add).then_inc(ch, 1)
                e.wait_ge(ch, c.next())
                v.tensor_tensor(out=nb[:, 5, :], in0=nb[:, 5, :], in1=nb[:, 6, :], op=ALU.add).then_inc(ch, 1)
                e.wait_ge(ch, c.next())
                v.tensor_copy(ed.main_row[:, :], nb[:, 5, :]).then_inc(ch, 1)
                e.wait_ge(ch, c.next())
                v.tensor_tensor(out=nb[:, 5, :], in0=nb[:, 1, :], in1=nb[:, 6, :], op=ALU.add).then_inc(ch, 1)
                e.wait_ge(ch, c.next())
                v.tensor_copy(ed.edge_row[:, :], nb[:, 5, :]).then_inc(ch, 1)
                e.wait_ge(ch, c.next())
                v.tensor_scalar(nb[:, 3, :], nb[:, 3, :], 1.0, None, ALU.add).then_inc(ch, 1)
                e.wait_ge(ch, c.next())
                v.tensor_scalar(nb[:, 4, :], nb[:, 3, :], float(J), None, ALU.mult).then_inc(ch, 1)
                e.wait_ge(ch, c.next())
                v.tensor_tensor(out=nb[:, 4, :], in0=ncum[:, 0, :], in1=nb[:, 4, :], op=ALU.is_le).then_inc(ch, 1)
                e.wait_ge(ch, c.next())
                v.scalar_tensor_tensor(nb[:, 5, :], nb[:, 4, :], OOB, nb[:, 3, :], ALU.mult, ALU.add).then_inc(ch, 1)
                e.wait_ge(ch, c.next())
                v.tensor_tensor(out=nb[:, 5, :], in0=nb[:, 5, :], in1=nb[:, 6, :], op=ALU.add).then_inc(ch, 1)
                e.wait_ge(ch, c.next())
                v.tensor_copy(ed.extra_row[:, :], nb[:, 5, :]).then_inc(ch, 1)
                e.wait_ge(ch, c.next())
                e.wait_ge(floaded, 16)
                e.sem_inc(floaded, -16)
                v.tensor_copy(frowf[:, :], frow[:, :]).then_inc(ch, 1)
                e.wait_ge(ch, c.next())
                e.sem_inc(fready, 1)
                e.wait_ge(fall, 1)
                e.sem_inc(fall, -1)
                v.tensor_copy(ed.first_all[:, :].rearrange("p (a c) -> p a c", a=2), pfa[:CP, :, 0:C // 2]).then_inc(ch, 1)
                e.wait_ge(ch, c.next())
                v.memset(ed.group_mask[:, :], -BIG).then_inc(ch, 1)
                e.wait_ge(ch, c.next())
                v.tensor_tensor(out=ed.group_mask[:, 1:C], in0=ed.first_all[0:HEADS, 1:C], in1=ed.first_all[0:HEADS, 0:C - 1],
                                op=ALU.is_equal).then_inc(ch, 1)
                e.wait_ge(ch, c.next())
                v.tensor_scalar(ed.group_mask[:, 1:C], ed.group_mask[:, 1:C], 2 * BIG, -BIG, ALU.mult, ALU.add).then_inc(ch, 1)
                e.wait_ge(ch, c.next())
                e.wait_ge(st_loaded, 16)
                e.sem_inc(st_loaded, -16)
                v.memset(ed.start[:, :].rearrange("k (b j) -> k b j", j=J)[:, :, 0:1], 1.0).then_inc(ch, 1)
                e.wait_ge(ch, c.next())
                c.reset()

            @block.tensor
            def _(e):
                t = nc.tensor
                e.wait_ge(totals, 1)
                e.sem_inc(totals, -1)
                t.matmul(poff[:CP, 0:1], tri[:CP, :CP], tot[:CP, 0:1], start=True, stop=True).then_inc(offs, 1)
                e.wait_ge(ready, 1)
                e.sem_inc(ready, -1)
                e.sem_inc(tr_free, 2)
                for k in range(CK):
                    e.wait_ge(tr_free, 1)
                    e.sem_inc(tr_free, -1)
                    for n, tab in enumerate((t2, srcf, hi, lo)):
                        ins = t.transpose(pst[:J, k % 2, n, :CP], tab[:, k * J:(k + 1) * J], ident[:CP, :CP])
                    ins.then_inc(tr_done, 1)

                def group(par, first=False, last=False):
                    e.wait_ge(oh_ready[par], 1)
                    e.sem_inc(oh_ready[par], -1)
                    for k in range(GC):
                        ins = t.matmul(pcnt[:P, 0:T], ohi[:, par, k, :], olo[:, par, k, :], start=first and k == 0,
                                       stop=last and k == GC - 1)
                    if last:
                        ins.then_inc(counted, 1)
                    else:
                        ins.then_inc(oh_free[par], 1)
                group(0, first=True)
                with e.Fori(0, C // GC // 2 - 1) as i:
                    group(1)
                    group(0)
                group(1, last=True)
                e.wait_ge(ntot, 1)
                e.sem_inc(ntot, -1)
                t.matmul(poff[:P, 4:6], tri[:P, :P], tot[:, 0:2], start=True, stop=True).then_inc(noff, 1)
                e.wait_ge(fready, 1)
                e.sem_inc(fready, -1)
                for a in range(2):
                    ins = t.matmul(pfa[:CP, a, 0:C // 2], const.ones[0:1, :CP], frowf[0:1, a * (C // 2):(a + 1) * (C // 2)],
                                   start=True, stop=True)
                ins.then_inc(fall, 1)



def norm_stats(nc, stage, X, mean, rstd, eps):
    with Mem(nc, stage) as m:
        st = m.sb("st", [P, T * 6])
        dd = m.sb("dd", [P, 2, T])
        ch, var_ready, sd_ready = m.sem("ch"), m.sem("var_ready"), m.sem("sd_ready")
        with nc.Block() as block:

            @block.vector
            def _(e):
                v = nc.vector
                c = Count(e, ch)
                with e.Fori(0, T // 10) as i:
                    for k in range(10):
                        v.bn_stats(out=st[:, bass.ds(i * 60 + k * 6, 6)], in_=X[:, bass.ds(i * (10 * D) + k * D, D)])
                v.memset(dd[:, :, :], 0.0).then_inc(ch, 1)
                e.wait_ge(ch, c.next())
                s = st[:, :].rearrange("p (t s) -> p s t", s=6)
                v.tensor_tensor(out=mean[:, :], in0=s[:, 1, :], in1=s[:, 4, :], op=ALU.add).then_inc(ch, 1)
                e.wait_ge(ch, c.next())
                v.tensor_scalar(mean[:, :], mean[:, :], 0.5, None, ALU.mult).then_inc(ch, 1)
                e.wait_ge(ch, c.next())
                v.tensor_tensor(out=dd[:, 0, :], in0=s[:, 1, :], in1=s[:, 4, :], op=ALU.subtract).then_inc(ch, 1)
                e.wait_ge(ch, c.next())
                v.tensor_tensor(out=dd[:, 0, :], in0=dd[:, 0, :], in1=dd[:, 0, :], op=ALU.mult).then_inc(ch, 1)
                e.wait_ge(ch, c.next())
                v.tensor_tensor(out=dd[:, 1, :], in0=s[:, 2, :], in1=s[:, 5, :], op=ALU.add).then_inc(ch, 1)
                e.wait_ge(ch, c.next())
                v.tensor_scalar(dd[:, 1, :], dd[:, 1, :], 1.0 / D, eps, ALU.mult, ALU.add).then_inc(ch, 1)
                e.wait_ge(ch, c.next())
                v.scalar_tensor_tensor(dd[:, 1, :], dd[:, 0, :], 0.25, dd[:, 1, :], ALU.mult, ALU.add).then_inc(ch, 1)
                e.wait_ge(ch, c.next())
                e.sem_inc(var_ready, 1)
                e.wait_ge(sd_ready, 1)
                e.sem_inc(sd_ready, -1)
                v.reciprocal(rstd[:, :], dd[:, 0, :]).then_inc(ch, 1)
                e.wait_ge(ch, c.next())
                c.reset()

            @block.scalar
            def _(e):
                e.wait_ge(var_ready, 1)
                e.sem_inc(var_ready, -1)
                nc.scalar.activation(dd[:, 0, :], dd[:, 1, :], ACT.Sqrt).then_inc(sd_ready, 1)


def gat_weights(nc, stage, w_in, w_out, att, wz):
    with Mem(nc, stage) as m:
        wo = m.sb("wo", [DO, HEADS, D])
        at = m.sb("at", [DO, 2 * HEADS])
        pw = m.ps("pw")
        ld, done = m.sem("ld"), m.sem("done")
        with nc.Block() as block:

            @block.sync
            def _(e):
                e.dma_start(wo[:, :, :], w_out).then_inc(ld, 16)
                e.dma_start(at[:, :], att).then_inc(ld, 16)
                e.dma_start(wz[:, :, 0:D], w_in.rearrange("(b i) o -> i b o", b=2)).then_inc(ld, 16)

            @block.tensor
            def _(e):
                e.wait_ge(ld, 48)
                e.sem_inc(ld, -48)
                for b in range(2):
                    for h in range(HEADS):
                        for s in range(2):
                            ins = nc.tensor.matmul(pw[:, (b * 8 + s * 4 + h):(b * 8 + s * 4 + h) + 1], wo[:, h, b * 128:(b + 1) * 128],
                                                   at[:, s * 4 + h:s * 4 + h + 1], start=True, stop=True)
                ins.then_inc(done, 1)

            @block.vector
            def _(e):
                e.wait_ge(done, 1)
                e.sem_inc(done, -1)
                nc.vector.tensor_copy(wz[:, :, D:D + 8], pw[:, 0:16].rearrange("p (b s) -> p b s", b=2))


def fill(nc, stage, jobs):
    with Mem(nc, stage) as m:
        z = m.sb("z", [128, 1024])
        s, ld = m.sem("s"), m.sem("ld")
        with nc.Block() as block:

            @block.vector
            def _(e):
                nc.vector.memset(z[:, :], 0.0).then_inc(s, 1)

            @block.sync
            def _(e):
                e.wait_ge(s, 1)
                e.sem_inc(s, -1)
                for view in jobs:
                    p, r, w = view.shape
                    for i in range(r):
                        e.dma_start(view[:, i, :], z[:p, 0:w]).then_inc(ld, 16)
                    e.wait_ge(ld, 16 * r)
                    e.sem_inc(ld, -(16 * r))


def dense0(nc, const, ed, X, mean, rstd, wz, wkv, wq, zt, edt, edn, edge_ed, qT, kv):
    with Mem(nc, "d0") as m:
        xn = m.sb("xn", [P, 2, D])
        xT = m.sb("xT", [128, 2, 2, P])
        zr = m.sb("zr", [P, 2, ZW + HEADS])
        ke, kr = m.sb("ke", [P, 2, D]), m.sb("kr", [P, 2, D])
        qe, qr = m.sb("qe", [128, 2, 2 * P]), m.sb("qr", [128, 2, 2 * P])
        kk = m.sb("kk", [P, 2, D])
        vv = m.sb("vv", [P, 2, 2, 129])
        pT = m.ps("pT")
        pz = m.ps("pz")
        pkv = [m.ps("pkv0"), m.ps("pkv1")]
        pq = [m.ps("pq0"), m.ps("pq1")]
        pacc = [m.ps("pacc0"), m.ps("pacc1")]
        ch = m.sem("ch")
        S = {n: [m.sem(n + "0"), m.sem(n + "1")] for n in
             ("xn_ready", "xn_free", "zr_ready", "zr_free", "zr_stored", "exps_ready", "exps_free", "k_ready", "k_free",
              "pkv_ready", "pkv_free", "pq_ready", "pq_free")}
        pT_ready, xT_ready = m.sem("pT_ready"), m.sem("xT_ready")
        pz_ready, pz_free = m.sem("pz_ready"), m.sem("pz_free")
        acc_ready = m.sem("acc_ready")
        edst = m.sem("edst")
        ed_done = m.sem("ed_done")
        row_ready, scattered = m.sem("row_ready"), m.counter("scattered")
        zt_v = zt.rearrange("(p t) w -> p (t w)", t=T)
        with nc.Block() as block:

            @block.vector
            def _(e):
                v = nc.vector
                c = Count(e, ch)
                v.memset(vv[:, :, :, :], 1.0).then_inc(ch, 1)
                e.wait_ge(ch, c.next())
                c.reset()
                for par in range(2):
                    e.sem_inc(S["xn_free"][par], 1)
                    e.sem_inc(S["k_free"][par], 1)
                    e.sem_inc(S["exps_free"][par], 1)

                def norm(t, par):
                    e.wait_ge(S["xn_free"][par], 1)
                    e.sem_inc(S["xn_free"][par], -1)
                    v.tensor_scalar(xn[:, par, :], X[:, bass.ds(t * D, D)], mean[:, bass.ds(t, 1)], rstd[:, bass.ds(t, 1)],
                                    ALU.subtract, ALU.mult).then_inc(S["xn_ready"][par], 1)

                def body(t, par):
                    e.wait_ge(S["exps_ready"][par], 1)
                    e.sem_inc(S["exps_ready"][par], -1)
                    v.scalar_tensor_tensor(kk[:, par, :], ke[:, par, :], 1.0, kr[:, par, :], ALU.min, ALU.add).then_inc(S["k_ready"][par], 1)
                    v.scalar_tensor_tensor(qT[:, bass.ds(t * 2 * P, 2 * P)], qe[:, par, :], 1.0, qr[:, par, :], ALU.min, ALU.add).then_inc(S["exps_free"][par], 1)
                norm(0, 0)
                norm(1, 1)
                with e.Fori(0, T // 2 - 1) as i:
                    for par in range(2):
                        norm(i * 2 + par + 2, par)
                        body(i * 2 + par, par)
                body(T - 2, 0)
                body(T - 1, 1)
                v.memset(kv[:, :], 0.0).then_inc(ch, 1)
                e.wait_ge(ch, c.next())
                e.wait_ge(acc_ready, 1)
                e.sem_inc(acc_ready, -1)
                for b in range(2):
                    for g in range(4):
                        r = slice(32 * g, 32 * g + 32)
                        o = b * 132
                        v.tensor_copy(kv[r, o + 32 * g:o + 32 * g + 32], pacc[b][r, 32 * g:32 * g + 32])
                        v.tensor_copy(kv[r, o + 128 + g:o + 129 + g], pacc[b][r, 128:129])
                c.reset()

            @block.scalar
            def _(e):
                a = nc.scalar

                def transposed(par):
                    e.wait_ge(pT_ready, 1)
                    e.sem_inc(pT_ready, -1)
                    e.sem_inc(S["xn_free"][par], 1)
                    a.activation(xT[:, par, :, :], pT[:, 0:2 * P].rearrange("p (b n) -> p b n", b=2), ACT.Copy).then_inc(xT_ready, 1)

                def body(t, par, last=False):
                    if not last:
                        transposed(1 - par)
                    e.wait_ge(pz_ready, 1)
                    e.sem_inc(pz_ready, -1)
                    e.wait_ge(S["zr_free"][par], 1)
                    e.sem_inc(S["zr_free"][par], -1)
                    a.activation(zr[:, par, :], pz[:P, 0:ZW + HEADS], ACT.Copy).then_inc(S["zr_ready"][par], 1)
                    a.activation(edn[:, bass.ds(t * HEADS, HEADS)], pz[:P, ZW:ZW + HEADS], ACT.Copy).then_inc(pz_free, 1)
                    e.drain().then_inc(row_ready, 1)
                    e.wait_ge(S["pkv_ready"][par], 1)
                    e.sem_inc(S["pkv_ready"][par], -1)
                    e.wait_ge(S["k_free"][par], 1)
                    e.sem_inc(S["k_free"][par], -1)
                    e.wait_ge(S["exps_free"][par], 1)
                    e.sem_inc(S["exps_free"][par], -1)
                    a.activation(ke[:, par, :], pkv[par][:P, 0:D], ACT.Exp)
                    a.activation(kr[:, par, :], pkv[par][:P, 0:D], ACT.Relu)
                    a.activation(vv[:, par, :, 0:128], pkv[par][:P, D:2 * D].rearrange("p (a b) -> p a b", a=2), ACT.Copy).then_inc(S["pkv_free"][par], 1)
                    e.wait_ge(S["pq_ready"][par], 1)
                    e.sem_inc(S["pq_ready"][par], -1)
                    a.activation(qe[:, par, :], pq[par][:, 0:2 * P], ACT.Exp)
                    a.activation(qr[:, par, :], pq[par][:, 0:2 * P], ACT.Relu).then_inc(S["pq_free"][par], 1)
                    e.drain().then_inc(S["exps_ready"][par], 1)
                for par in range(2):
                    e.sem_inc(S["zr_free"][par], 1)
                transposed(0)
                with e.Fori(0, T // 2 - 1) as i:
                    body(i * 2, 0)
                    body(i * 2 + 1, 1)
                body(T - 2, 0)
                body(T - 1, 1, last=True)
                e.drain().then_inc(ed_done, 1)

            @block.gpsimd
            def _(e):
                scatter_edge_inputs(e, ed, edn, edge_ed, row_ready, scattered)

            @block.sync
            def _(e):
                def body(t, par):
                    e.wait_ge(S["zr_ready"][par], 1)
                    e.sem_inc(S["zr_ready"][par], -1)
                    e.dma_start(zt_v[:, bass.ds(t * ZW, ZW)], zr[:, par, 0:ZW]).then_inc(S["zr_stored"][par], 16)
                    e.wait_ge(S["zr_stored"][par], 16)
                    e.sem_inc(S["zr_stored"][par], -(16))
                    e.sem_inc(S["zr_free"][par], 1)
                steps(e, T, body)
                e.wait_ge(ed_done, 1)
                e.sem_inc(ed_done, -1)
                e.dma_start(edt.rearrange("(p t) w -> p (t w)", t=T), edn[:, :]).then_inc(edst, 16)
                e.wait_ge(edst, 16)
                e.sem_inc(edst, -16)

            @block.tensor
            def _(e):
                t_ = nc.tensor
                e.sem_inc(pz_free, 1)
                for par in range(2):
                    e.sem_inc(S["pkv_free"][par], 1)
                    e.sem_inc(S["pq_free"][par], 1)

                def transposes(par):
                    e.wait_ge(S["xn_ready"][par], 1)
                    e.sem_inc(S["xn_ready"][par], -1)
                    for b in range(2):
                        ins = t_.transpose(pT[:, b * P:(b + 1) * P], xn[:, par, b * 128:(b + 1) * 128], const.ident[:P, :P])
                    ins.then_inc(pT_ready, 1)

                def accumulate(par, first=False, last=False):
                    e.wait_ge(S["k_ready"][par], 1)
                    e.sem_inc(S["k_ready"][par], -1)
                    for b in range(2):
                        ins = t_.matmul(pacc[b][:, 0:129], kk[:, par, b * 128:(b + 1) * 128], vv[:, par, b, :], start=first, stop=last)
                    ins.then_inc(acc_ready if last else S["k_free"][par], 1)

                def body(par, last=False):
                    e.wait_ge(xT_ready, 1)
                    e.sem_inc(xT_ready, -1)
                    if not last:
                        transposes(1 - par)
                    e.wait_ge(pz_free, 1)
                    e.sem_inc(pz_free, -1)
                    for b in range(2):
                        ins = t_.matmul(pz[:P, 0:ZW + HEADS], xT[:, par, b, :], wz[:, b, :], start=b == 0, stop=b == 1)
                    ins.then_inc(pz_ready, 1)
                    e.wait_ge(S["pkv_free"][par], 1)
                    e.sem_inc(S["pkv_free"][par], -1)
                    for b in range(2):
                        ins = t_.matmul(pkv[par][:P, 0:2 * D], xT[:, par, b, :], wkv[:, b, :], start=b == 0, stop=b == 1)
                    ins.then_inc(S["pkv_ready"][par], 1)
                    e.wait_ge(S["pq_free"][par], 1)
                    e.sem_inc(S["pq_free"][par], -1)
                    for o in range(2):
                        for b in range(2):
                            ins = t_.matmul(pq[par][:, o * P:(o + 1) * P], wq[:, b, o * 128:(o + 1) * 128], xT[:, par, b, :], start=b == 0, stop=b == 1)
                    ins.then_inc(S["pq_ready"][par], 1)
                transposes(0)
                body(0)
                body(1)
                accumulate(0, first=True)
                with e.Fori(0, T // 2 - 2) as i:
                    body(0)
                    accumulate(1)
                    body(1)
                    accumulate(0)
                body(0)
                accumulate(1)
                body(1, last=True)
                accumulate(0)
                accumulate(1, last=True)


def scatter_edge_inputs(e, ed, edn, edge_ed, row_ready, scattered):
    for t in range(T):
        e.wait_ge(row_ready, 1)
        e.sem_inc(row_ready, -1)
        e.indirect_dma_start(out=edge_ed[:, :], out_offset=bass.IndirectOffsetOnAxis(ap=ed.edge_row[:, t:t + 1], axis=0),
                             in_=edn[:, t * HEADS:(t + 1) * HEADS], in_offset=None,
                             bounds_check=E - 1, oob_is_err=False).then_inc(scattered, 16)
    e.wait_ge(scattered, 16 * T)


def chunk_edge_inputs(nc, stage, ed, edt, edge_ed):
    with Mem(nc, stage) as m:
        fe = m.sb("fe", [CP, CK, HEADS])
        gathered, stored = m.counter("gathered"), m.sem("stored")
        with nc.Block() as block:

            @block.gpsimd
            def _(e):
                for k in range(CK):
                    e.indirect_dma_start(out=fe[:, k, :], out_offset=None, in_=edt[:, :],
                                         in_offset=bass.IndirectOffsetOnAxis(ap=ed.first_node[:, k:k + 1], axis=0)).then_inc(gathered, 16)

            @block.sync
            def _(e):
                e.wait_ge(gathered, 16 * CK)
                e.dma_start(edge_ed[0:E, :].rearrange("(p k j) h -> p k (j h)", k=CK, j=J)[:, :, 0:HEADS], fe[:, :, :]).then_inc(stored, 16)
                e.wait_ge(stored, 16)
                e.sem_inc(stored, -16)


def gat_edges(nc, stage, const, ed, zt, edge_ed, sums, slope):
    HW = J + 1
    W4 = HEADS * HW
    with Mem(nc, stage) as m:
        Z = m.sb("Z", [P, 2 * BC * GW])
        onehot = m.sb("onehot", [P, 2, GC * J])
        sumrow = m.sb("sumrow", [P, 2, GC * GW])
        idx = m.sb("idx", [P, 2, BC], I32)
        edv = m.sb("edv", [BC, 2, J * HEADS])
        vs = m.sb("vs", [BC, W4])
        cm = m.sb("cm", [BC, W4])
        mk = m.sb("mk", [BC, W4 + 1])
        edf = m.sb("edf", [BC, W4])
        ev = m.sb("ev", [BC, W4])
        fw = m.sb("fw", [BC, W4])
        bw, ex, ms = edf, cm, vs
        pes = m.ps("pes")
        pex = m.ps("pex")
        NPO = 5
        po = [m.ps(f"po{i}") for i in range(NPO)]
        ch = m.sem("ch")
        S = {n: [m.sem(n + "0"), m.sem(n + "1")] for n in
             ("slot_free", "staged", "edv_ld", "edv_ready", "edv_free", "grp_ready", "oh_free", "out_ready", "out_free", "stored")}
        S["gathered"] = [m.counter("gathered0"), m.counter("gathered1")]
        es_ready, es_free = m.sem("es_ready"), m.sem("es_free")
        d_ready, ex_ready, ms_ready = m.sem("d_ready"), m.sem("ex_ready"), m.sem("ms_ready")
        pex_ready, pex_free = m.sem("pex_ready"), m.sem("pex_free")
        po_ready = [m.sem(f"po_ready{i}") for i in range(NPO)]
        po_free = [m.sem(f"po_free{i}") for i in range(NPO)]
        zv = [Z[:, b * BC * GW:(b + 1) * BC * GW].rearrange("p (k w) -> p k w", w=GW) for b in range(2)]
        h4 = lambda x: x[:, 0:W4].rearrange("k (h j) -> k h j", h=HEADS)[:, :, 0:J]
        sums_v = sums.rearrange("(x k) w -> x (k w)", k=BC)
        ed_v = edge_ed.rearrange("(c j) h -> c (j h)", j=J)
        with nc.Block() as block:

            @block.gpsimd
            def _(e):
                e.sem_inc(S["slot_free"][0], 1)
                e.sem_inc(S["slot_free"][1], 1)
                with e.Fori(0, NB // 2) as i:
                    for b in range(2):
                        e.wait_ge(S["slot_free"][b], 1)
                        e.sem_inc(S["slot_free"][b], -1)
                        e.wait_ge(S["staged"][b], 1)
                        e.sem_inc(S["staged"][b], -1)
                        for k in range(BC):
                            e.indirect_dma_start(out=zv[b][:, k, 0:ZW], out_offset=None, in_=zt[:, :],
                                                 in_offset=bass.IndirectOffsetOnAxis(ap=idx[:, b, k:k + 1], axis=0)).then_inc(S["gathered"][b], 16)

            @block.sync
            def _(e):
                def load(B, b):
                    e.wait_ge(S["edv_free"][b], 1)
                    e.sem_inc(S["edv_free"][b], -1)
                    e.dma_start(edv[:, b, :], ed_v[bass.ds(B * BC, BC), :]).then_inc(S["edv_ld"][b], 16)
                    e.wait_ge(S["edv_ld"][b], 16)
                    e.sem_inc(S["edv_ld"][b], -16)
                    e.sem_inc(S["edv_ready"][b], 1)
                e.sem_inc(S["edv_free"][0], 1)
                e.sem_inc(S["edv_free"][1], 1)
                load(0, 0)
                with e.Fori(0, NB // 2) as i:
                    for b in range(2):
                        load(i * 2 + b + 1, 1 - b)
                        for q in range(NG):
                            e.wait_ge(S["out_ready"][q % 2], 1)
                            e.sem_inc(S["out_ready"][q % 2], -1)
                            e.dma_start(sums_v[bass.ds((i * 2 + b) * P, P), q * GC * GW:(q + 1) * GC * GW], sumrow[:, q % 2, :]).then_inc(S["stored"][q % 2], 16)
                            e.wait_ge(S["stored"][q % 2], 16)
                            e.sem_inc(S["stored"][q % 2], -16)
                            e.sem_inc(S["out_free"][q % 2], 1)

            @block.vector
            def _(e):
                v = nc.vector
                c = Count(e, ch)
                for x in (vs, cm, edf, ev):
                    v.memset(x[:, :], 0.0)
                v.memset(mk[:, :], -BIG).then_inc(ch, 1)
                e.wait_ge(ch, c.next())
                v.tensor_copy(idx[:, 0, :], ed.srcT[:, 0:BC]).then_inc(ch, 1)
                e.wait_ge(ch, c.next())
                e.sem_inc(S["staged"][0], 1)
                c.reset()
                with e.Fori(0, NB // 2) as i:
                    for b in range(2):
                        B = i * 2 + b
                        st = ed.start[:, bass.ds(B * J, J)].unsqueeze(1).to_broadcast([BC, HEADS, J])
                        v.tensor_scalar(h4(cm), st, -1.0, 1.0, ALU.mult, ALU.add)
                        v.tensor_scalar(h4(mk), st, -2 * BIG, BIG, ALU.mult, ALU.add)
                        e.wait_ge(S["edv_ready"][b], 1)
                        e.sem_inc(S["edv_ready"][b], -1)
                        v.tensor_tensor(out=h4(vs), in0=edv[:, b, :].rearrange("k (j h) -> k h j", h=HEADS), in1=st, op=ALU.mult).then_inc(ch, 1)
                        e.wait_ge(ch, c.next())
                        e.sem_inc(S["edv_free"][b], 1)
                        v.tensor_tensor_scan(out=edf[:, :], data0=cm[:, :], data1=vs[:, :], initial=0.0, op0=ALU.mult, op1=ALU.add).then_inc(ch, 1)
                        e.wait_ge(ch, c.next())
                        e.wait_ge(S["gathered"][b], i * (16 * BC) + 16 * BC)
                        v.tensor_copy(idx[:, 1 - b, :], ed.srcT[:, bass.ds(B * BC + BC, BC)]).then_inc(S["staged"][1 - b], 1)
                        e.wait_ge(es_ready, 1)
                        e.sem_inc(es_ready, -1)
                        v.tensor_tensor(out=h4(ev), in0=pes[:BC, :].rearrange("k (h j) -> k h j", h=HEADS)[:, :, 0:J], in1=h4(edf), op=ALU.add).then_inc(ch, 1)
                        e.wait_ge(ch, c.next())
                        e.sem_inc(es_free, 1)
                        v.scalar_tensor_tensor(ev[:, :], ev[:, :], slope, ev[:, :], ALU.mult, ALU.max).then_inc(ch, 1)
                        e.wait_ge(ch, c.next())
                        v.tensor_tensor_scan(out=fw[:, :], data0=mk[:, 0:W4], data1=ev[:, :], initial=-BIG, op0=ALU.min, op1=ALU.max)
                        v.tensor_tensor_scan(out=bw[:, ::-1], data0=mk[:, W4:0:-1], data1=ev[:, ::-1], initial=-BIG, op0=ALU.min, op1=ALU.max).then_inc(ch, 1)
                        e.wait_ge(ch, c.next())
                        v.tensor_tensor(out=fw[:, :], in0=fw[:, :], in1=bw[:, :], op=ALU.max).then_inc(ch, 1)
                        e.wait_ge(ch, c.next())
                        v.tensor_tensor(out=ev[:, :], in0=ev[:, :], in1=fw[:, :], op=ALU.subtract).then_inc(d_ready, 1)
                        v.tensor_tensor(out=h4(ms), in0=h4(fw), in1=st, op=ALU.mult).then_inc(ms_ready, 1)
                        e.wait_ge(pex_ready, 1)
                        e.sem_inc(pex_ready, -1)
                        v.tensor_copy(zv[b].rearrange("p k w -> p w k")[:, D:GW, :], pex[:P, 0:8 * BC].rearrange("p (w k) -> p w k", w=8)).then_inc(ch, 1)
                        e.wait_ge(ch, c.next())
                        e.sem_inc(pex_free, 1)
                        c.reset()
                        with e.Fori(0, NG // 2) as g:
                            for par in range(2):
                                e.wait_ge(S["oh_free"][par], 1)
                                e.sem_inc(S["oh_free"][par], -1)
                                zg = Z[:, bass.ds(g * (2 * GC * GW) + (b * BC + par * GC) * GW, GC * GW)].rearrange("p (k w) -> p k w", w=GW)
                                v.tensor_tensor(out=zg[:, :, 0:D].rearrange("p k (h o) -> p k h o", h=HEADS),
                                                in0=zg[:, :, 0:D].rearrange("p k (h o) -> p k h o", h=HEADS),
                                                in1=zg[:, :, D:D + HEADS].unsqueeze(3).to_broadcast([P, GC, HEADS, DO]), op=ALU.mult)
                                v.tensor_tensor(out=onehot[:, par, :].rearrange("p (k j) -> p k j", k=GC),
                                                in0=const.iota[:P, 0:J].unsqueeze(1).to_broadcast([P, GC, J]),
                                                in1=ed.gT[:, bass.ds(i * (2 * BC) + g * (2 * GC) + (b * BC + par * GC), GC)].unsqueeze(2).to_broadcast([P, GC, J]),
                                                op=ALU.is_equal).then_inc(S["grp_ready"][par], 1)

            @block.scalar
            def _(e):
                a = nc.scalar
                e.sem_inc(S["out_free"][0], 1)
                e.sem_inc(S["out_free"][1], 1)
                with e.Fori(0, NB // 2) as i:
                    for b in range(2):
                        e.wait_ge(d_ready, 1)
                        e.sem_inc(d_ready, -1)
                        a.activation(ex[:, :], ev[:, :], ACT.Exp).then_inc(ex_ready, 1)
                        with e.Fori(0, NG // 2) as g:
                            for par in range(2):
                                e.wait_ge(S["out_free"][par], 1)
                                e.sem_inc(S["out_free"][par], -1)
                                for k in range(GC):
                                    e.wait_ge(po_ready[k % NPO], 1)
                                    e.sem_inc(po_ready[k % NPO], -1)
                                    if k == GC - 1:
                                        e.sem_inc(S["oh_free"][par], 1)
                                    a.activation(sumrow[:, par, k * GW:(k + 1) * GW], po[k % NPO][:P, 0:GW], ACT.Copy).then_inc(po_free[k % NPO], 1)
                                e.drain().then_inc(S["out_ready"][par], 1)
                        e.sem_inc(S["slot_free"][b], 1)

            @block.tensor
            def _(e):
                t = nc.tensor
                for s in [es_free, pex_free, S["oh_free"][0], S["oh_free"][1]] + po_free:
                    e.sem_inc(s, 1)
                with e.Fori(0, NB // 2) as i:
                    for b in range(2):
                        e.wait_ge(S["gathered"][b], i * (16 * BC) + 16 * BC)
                        e.wait_ge(es_free, 1)
                        e.sem_inc(es_free, -1)
                        for h in range(HEADS):
                            ins = t.transpose(pes[:BC, h * 128:h * 128 + J], zv[b][:, :, D + h], const.ident[:P, :P])
                        ins.then_inc(es_ready, 1)
                        e.wait_ge(ex_ready, 1)
                        e.sem_inc(ex_ready, -1)
                        e.wait_ge(ms_ready, 1)
                        e.sem_inc(ms_ready, -1)
                        e.wait_ge(pex_free, 1)
                        e.sem_inc(pex_free, -1)
                        for n in range(2 * HEADS):
                            x, h = (ex, ms)[n // HEADS], n % HEADS
                            ins = t.transpose(pex[:P, n * BC:(n + 1) * BC], x[:, h * HW:h * HW + J], const.ident[:BC, :BC])
                        ins.then_inc(pex_ready, 1)
                        with e.Fori(0, NG // 2) as g:
                            for par in range(2):
                                e.wait_ge(S["grp_ready"][par], 1)
                                e.sem_inc(S["grp_ready"][par], -1)
                                for k in range(GC):
                                    e.wait_ge(po_free[k % NPO], 1)
                                    e.sem_inc(po_free[k % NPO], -1)
                                    ins = t.matmul(po[k % NPO][:P, 0:GW], onehot[:, par, k * J:(k + 1) * J],
                                                   Z[:, bass.ds(g * (2 * GC * GW) + (b * BC + par * GC + k) * GW, GW)], start=True, stop=True)
                                    ins.then_inc(po_ready[k % NPO], 1)


def gat_extras(nc, stage, const, ed, sums, extras):
    with Mem(nc, stage) as m:
        R = m.sb("R", [CP, CK * GW])
        same = m.sb("same", [CP, 2, C])
        mt = m.sb("mt", [HEADS, C])
        fw = m.sb("fw", [HEADS, C])
        bw = m.sb("bw", [HEADS, C])
        mc = m.sb("mc", [CP, CK])
        df = m.sb("df", [CP, CK * HEADS])
        fac = m.sb("fac", [CP, CK * HEADS])
        mg = m.sb("mg", [CP, CK * HEADS])
        tot = m.sb("tot", [CP, CK * GW])
        pm = [m.ps("pm0"), m.ps("pm1")]
        pb = m.ps("pb")
        po = [m.ps(f"po{k}") for k in range(4)]
        ga = m.counter("ga")
        ch, m_ready, mt_ready, mg_ready, back = (m.sem(x) for x in ("ch", "m_ready", "mt_ready", "mg_ready", "back"))
        df_ready, fac_ready, po_ready, po_free, tot_ready, st = (m.sem(x) for x in ("df_ready", "fac_ready", "po_ready", "po_free", "tot_ready", "st"))
        eq_ready = [m.sem("eq_ready0"), m.sem("eq_ready1")]
        eq_free = [m.sem("eq_free0"), m.sem("eq_free1")]
        r3 = R[:, :].rearrange("p (k w) -> p k w", w=GW)
        t3 = tot[:, :].rearrange("p (k w) -> p k w", w=GW)
        kh = lambda x: x[:, :].rearrange("p (k h) -> p k h", h=HEADS)
        with nc.Block() as block:

            @block.gpsimd
            def _(e):
                for k in range(CK):
                    e.indirect_dma_start(out=R[:, k * GW:(k + 1) * GW], out_offset=None, in_=sums[:, :],
                                         in_offset=bass.IndirectOffsetOnAxis(ap=ed.first_row[:, k:k + 1], axis=0)).then_inc(ga, 16)

            @block.vector
            def _(e):
                v = nc.vector
                c = Count(e, ch)
                v.tensor_scalar(mc[:, :], ed.cont[:, :], BIG, -BIG, ALU.mult, ALU.add).then_inc(ch, 1)
                e.wait_ge(ch, c.next())
                e.wait_ge(ga, 16 * CK)
                v.tensor_tensor(out=r3[:, :, :], in0=r3[:, :, :], in1=ed.cont[:, :].unsqueeze(2).to_broadcast([CP, CK, GW]), op=ALU.mult).then_inc(ch, 1)
                e.wait_ge(ch, c.next())
                v.tensor_tensor(out=r3[:, :, ZW:GW], in0=r3[:, :, ZW:GW], in1=mc[:, :].unsqueeze(2).to_broadcast([CP, CK, HEADS]), op=ALU.add).then_inc(ch, 1)
                e.wait_ge(ch, c.next())
                e.sem_inc(m_ready, 1)
                e.wait_ge(mt_ready, 1)
                e.sem_inc(mt_ready, -1)
                mv = mt[:, :].rearrange("h (p k) -> h k p", k=CK)
                for a in range(2):
                    v.tensor_copy(mv[:, 4 * a:4 * a + 4, :], pm[a][:HEADS, :].rearrange("h (k p) -> h k p", k=4)[:, :, 0:CP]).then_inc(ch, 1)
                    e.wait_ge(ch, c.next())
                v.tensor_tensor_scan(out=fw[:, :], data0=ed.group_mask[:, 0:C], data1=mt[:, :], initial=-BIG, op0=ALU.min, op1=ALU.max).then_inc(ch, 1)
                e.wait_ge(ch, c.next())
                v.tensor_tensor_scan(out=bw[:, ::-1], data0=ed.group_mask[:, C:0:-1], data1=mt[:, ::-1], initial=-BIG, op0=ALU.min, op1=ALU.max).then_inc(ch, 1)
                e.wait_ge(ch, c.next())
                v.tensor_tensor(out=fw[:, :], in0=fw[:, :], in1=bw[:, :], op=ALU.max).then_inc(ch, 1)
                e.wait_ge(ch, c.next())
                e.sem_inc(mg_ready, 1)
                e.wait_ge(back, 1)
                e.sem_inc(back, -1)
                v.tensor_copy(mg[:, :], pb[:CP, 0:CK * HEADS]).then_inc(ch, 1)
                e.wait_ge(ch, c.next())
                v.tensor_tensor(out=kh(df), in0=r3[:, :, ZW:GW], in1=kh(mg), op=ALU.subtract).then_inc(ch, 1)
                e.wait_ge(ch, c.next())
                e.sem_inc(df_ready, 1)
                e.wait_ge(fac_ready, 1)
                e.sem_inc(fac_ready, -1)
                v.tensor_tensor(out=r3[:, :, D:ZW], in0=r3[:, :, D:ZW], in1=kh(fac), op=ALU.mult).then_inc(ch, 1)
                e.wait_ge(ch, c.next())
                v.tensor_tensor(out=r3[:, :, 0:D].rearrange("p k (h o) -> p k h o", h=HEADS),
                                in0=r3[:, :, 0:D].rearrange("p k (h o) -> p k h o", h=HEADS),
                                in1=kh(fac).unsqueeze(3).to_broadcast([CP, CK, HEADS, DO]), op=ALU.mult).then_inc(ch, 1)
                e.wait_ge(ch, c.next())
                v.tensor_copy(t3[:, :, ZW:GW], kh(mg)).then_inc(ch, 1)
                e.wait_ge(ch, c.next())
                for half in range(2):
                    for k in range(CK):
                        if half or k >= 2:
                            e.wait_ge(eq_free[k % 2], 1)
                            e.sem_inc(eq_free[k % 2], -1)
                        v.tensor_scalar(same[:, k % 2, :], ed.first_all[:, :], ed.first_nodef[:, k:k + 1], None, ALU.is_equal).then_inc(eq_ready[k % 2], 1)
                    e.wait_ge(po_ready, 1)
                    e.sem_inc(po_ready, -1)
                    for q in range(4):
                        v.tensor_copy(t3[:, half * 4 + q, 0:ZW], po[q][:CP, 0:ZW]).then_inc(ch, 1)
                        e.wait_ge(ch, c.next())
                    e.sem_inc(po_free, 1)
                e.sem_inc(tot_ready, 1)
                c.reset()

            @block.scalar
            def _(e):
                e.wait_ge(df_ready, 1)
                e.sem_inc(df_ready, -1)
                nc.scalar.activation(fac[:, :], df[:, :], ACT.Exp).then_inc(fac_ready, 1)

            @block.tensor
            def _(e):
                t = nc.tensor
                e.wait_ge(m_ready, 1)
                e.sem_inc(m_ready, -1)
                for k in range(CK):
                    ins = t.transpose(pm[k // 4][:HEADS, (k % 4) * 128:(k % 4) * 128 + CP], r3[:, k, ZW:GW], const.ident[:CP, :CP])
                ins.then_inc(mt_ready, 1)
                e.wait_ge(mg_ready, 1)
                e.sem_inc(mg_ready, -1)
                gv = fw[:, :].rearrange("h (p k) -> h k p", k=CK)
                for k in range(CK):
                    ins = t.transpose(pb[:CP, k * HEADS:(k + 1) * HEADS], gv[:, k, :], const.ident[:HEADS, :HEADS])
                ins.then_inc(back, 1)
                for half in range(2):
                    if half:
                        e.wait_ge(po_free, 1)
                        e.sem_inc(po_free, -1)
                    for k in range(CK):
                        e.wait_ge(eq_ready[k % 2], 1)
                        e.sem_inc(eq_ready[k % 2], -1)
                        sv = same[:, k % 2, :].rearrange("p (c k) -> p k c", k=CK)
                        for q in range(4):
                            ins = t.matmul(po[q][:CP, 0:ZW], sv[:, half * 4 + q, :], r3[:, k, 0:ZW], start=k == 0, stop=k == CK - 1)
                        if k == CK - 1:
                            ins.then_inc(po_ready, 1)
                        elif not (half and k >= CK - 2):
                            ins.then_inc(eq_free[k % 2], 1)
                    if not half:
                        e.sem_inc(eq_free[1], 1)

            @block.sync
            def _(e):
                e.wait_ge(tot_ready, 1)
                e.sem_inc(tot_ready, -1)
                e.dma_start(extras.rearrange("(p k) w -> p (k w)", k=CK), tot[:, :]).then_inc(st, 16)
                e.wait_ge(st, 16)
                e.sem_inc(st, -16)


def gat_merge(nc, stage, ed, X, sums, extras, zt=None, edn=None, bias=None, slope=None):
    G = 5
    NP = 3 if zt is not None else 2
    with Mem(nc, stage) as m:
        part = [m.sb(f"part{i}", [P, 2, G * GW]) for i in range(NP)]
        mx = m.sb("mx", [P, G * HEADS])
        df = m.sb("df", [P, 2, NP, G * HEADS])
        fac = m.sb("fac", [P, 2, NP, G * HEADS])
        den = m.sb("den", [P, G * HEADS])
        idx = m.sb("idx", [P, 2, 2, G], I32)
        bs = m.sb("bs", [P, D])
        ch, df_ready, fac_ready, bld = m.sem("ch"), m.sem("df_ready"), m.sem("fac_ready"), m.sem("bld")
        S = {n: [m.sem(n + "0"), m.sem(n + "1")] for n in ("ready", "self_ld", "self_free")}
        S["ga"] = [m.counter("ga0"), m.counter("ga1")]
        h4 = lambda x: x.rearrange("p (k w) -> p k w", w=GW)
        gh = lambda x: x.rearrange("p (k h) -> p k h", h=HEADS)
        n_steps = T // G
        with nc.Block() as block:

            @block.gpsimd
            def _(e):
                with e.Fori(0, n_steps // 2) as i:
                    for b in range(2):
                        e.wait_ge(S["ready"][b], 1)
                        e.sem_inc(S["ready"][b], -1)
                        for s, table, rows in ((0, sums, NB * P * BC), (1, extras, C)):
                            for k in range(G):
                                e.indirect_dma_start(out=part[s][:, b, k * GW:(k + 1) * GW], out_offset=None, in_=table[:, :],
                                                     in_offset=bass.IndirectOffsetOnAxis(ap=idx[:, b, s, k:k + 1], axis=0),
                                                     bounds_check=rows - 1, oob_is_err=False).then_inc(S["ga"][b], 16)

            if zt is not None:
                @block.sync
                def _(e):
                    zt_v = zt.rearrange("(p t) w -> p t w", t=T)
                    e.dma_start(bs[:, :], bias.partition_broadcast(P)).then_inc(bld, 16)
                    for b in range(2):
                        e.sem_inc(S["self_free"][b], 1)
                    with e.Fori(0, n_steps // 2) as i:
                        for b in range(2):
                            e.wait_ge(S["self_free"][b], 1)
                            e.sem_inc(S["self_free"][b], -1)
                            e.dma_start(h4(part[2][:, b, :])[:, :, 0:ZW], zt_v[:, bass.ds(i * (2 * G) + b * G, G), :]).then_inc(S["self_ld"][b], 16)

            @block.scalar
            def _(e):
                with e.Fori(0, n_steps // 2) as i:
                    for b in range(2):
                        e.wait_ge(df_ready, 1)
                        e.sem_inc(df_ready, -1)
                        nc.scalar.activation(fac[:, b, :, :], df[:, b, :, :], ACT.Exp).then_inc(fac_ready, 1)

            @block.vector
            def _(e):
                v = nc.vector
                c = Count(e, ch)

                def prefill(s, b):
                    for n in range(2):
                        p3 = h4(part[n][:, b, :])
                        v.memset(p3[:, :, 0:ZW], 0.0)
                        v.memset(p3[:, :, ZW:GW], -BIG)
                    v.tensor_copy(idx[:, b, 0, :], ed.main_row[:, bass.ds(s * G, G)])
                    v.tensor_copy(idx[:, b, 1, :], ed.extra_row[:, bass.ds(s * G, G)]).then_inc(S["ready"][b], 1)
                prefill(0, 0)
                if zt is not None:
                    e.wait_ge(bld, 16)
                    e.sem_inc(bld, -16)

                def body(i, b, last):
                    s = i * 2 + b
                    if not last:
                        prefill(s + 1, 1 - b)
                    e.wait_ge(S["ga"][b], i * (16 * 2 * G) + 16 * 2 * G)
                    p3 = [h4(part[n][:, b, :]) for n in range(NP)]
                    M = gh(mx[:, :])
                    v.tensor_tensor(out=M, in0=p3[0][:, :, ZW:GW], in1=p3[1][:, :, ZW:GW], op=ALU.max).then_inc(ch, 1)
                    e.wait_ge(ch, c.next())
                    if zt is not None:
                        e.wait_ge(S["self_ld"][b], 16)
                        e.sem_inc(S["self_ld"][b], -16)
                        v.tensor_tensor(out=p3[2][:, :, ZW:GW], in0=p3[2][:, :, D:ZW], in1=gh(edn[:, bass.ds(s * (G * HEADS), G * HEADS)]), op=ALU.add).then_inc(ch, 1)
                        e.wait_ge(ch, c.next())
                        v.scalar_tensor_tensor(p3[2][:, :, ZW:GW], p3[2][:, :, ZW:GW], slope, p3[2][:, :, ZW:GW], ALU.mult, ALU.max).then_inc(ch, 1)
                        e.wait_ge(ch, c.next())
                        v.tensor_tensor(out=M, in0=M, in1=p3[2][:, :, ZW:GW], op=ALU.max).then_inc(ch, 1)
                        e.wait_ge(ch, c.next())
                    for n in range(NP):
                        v.tensor_tensor(out=gh(df[:, b, n, :]), in0=p3[n][:, :, ZW:GW], in1=M, op=ALU.subtract).then_inc(ch, 1)
                        e.wait_ge(ch, c.next())
                    e.sem_inc(df_ready, 1)
                    e.wait_ge(fac_ready, 1)
                    e.sem_inc(fac_ready, -1)
                    for n in range(2):
                        v.tensor_tensor(out=p3[n][:, :, D:ZW], in0=p3[n][:, :, D:ZW], in1=gh(fac[:, b, n, :]), op=ALU.mult).then_inc(ch, 1)
                        e.wait_ge(ch, c.next())
                    v.tensor_tensor(out=gh(den[:, :]), in0=p3[0][:, :, D:ZW], in1=p3[1][:, :, D:ZW], op=ALU.add).then_inc(ch, 1)
                    e.wait_ge(ch, c.next())
                    if NP == 3:
                        v.tensor_tensor(out=den[:, :], in0=den[:, :], in1=fac[:, b, 2, :], op=ALU.add).then_inc(ch, 1)
                        e.wait_ge(ch, c.next())
                    v.tensor_scalar(den[:, :], den[:, :], 1e-16, None, ALU.max).then_inc(ch, 1)
                    e.wait_ge(ch, c.next())
                    v.reciprocal(den[:, :], den[:, :]).then_inc(ch, 1)
                    e.wait_ge(ch, c.next())
                    acc = p3[0][:, :, 0:D].rearrange("p k (h o) -> p k h o", h=HEADS)
                    for n in range(NP):
                        pn = p3[n][:, :, 0:D].rearrange("p k (h o) -> p k h o", h=HEADS)
                        v.tensor_tensor(out=gh(fac[:, b, n, :]), in0=gh(fac[:, b, n, :]), in1=gh(den[:, :]), op=ALU.mult).then_inc(ch, 1)
                        e.wait_ge(ch, c.next())
                        v.tensor_tensor(out=pn, in0=pn, in1=gh(fac[:, b, n, :]).unsqueeze(3).to_broadcast([P, G, HEADS, DO]), op=ALU.mult).then_inc(ch, 1)
                        e.wait_ge(ch, c.next())
                        if n:
                            v.tensor_tensor(out=p3[0][:, :, 0:D], in0=p3[0][:, :, 0:D], in1=p3[n][:, :, 0:D], op=ALU.add).then_inc(ch, 1)
                            e.wait_ge(ch, c.next())
                    if bias is not None:
                        v.tensor_tensor(out=p3[0][:, :, 0:D], in0=p3[0][:, :, 0:D], in1=bs[:, :].unsqueeze(1).to_broadcast([P, G, D]), op=ALU.add).then_inc(ch, 1)
                        e.wait_ge(ch, c.next())
                    xs = X[:, bass.ds(s * (G * D), G * D)].rearrange("p (k w) -> p k w", w=D)
                    v.tensor_tensor(out=xs, in0=xs, in1=p3[0][:, :, 0:D], op=ALU.add).then_inc(ch, 1)
                    e.wait_ge(ch, c.next())
                    if zt is not None:
                        e.sem_inc(S["self_free"][b], 1)
                    c.reset()
                with e.Fori(0, n_steps // 2 - 1) as i:
                    body(i, 0, False)
                    body(i, 1, False)
                body(n_steps // 2 - 1, 0, False)
                body(n_steps // 2 - 1, 1, True)


def mix0(nc, const, X, mean, rstd, qT, kv, a):
    Q = 2
    NS = T // Q
    with Mem(nc, "m0") as m:
        w1 = m.sb("w1", [128, 2, D])
        w2 = m.sb("w2", [128, 2, D])
        b1 = m.sb("b1", [128, 2])
        gb = m.sb("gb", [P, 5, D])
        nmean = m.sb("nmean", [P, T])
        qs = m.sb("qs", [128, 2, Q * 2 * P])
        xc = m.sb("xc", [P, 2, Q, D])
        xn = m.sb("xn", [P, 2, Q, D])
        at = m.sb("at", [P, Q, D])
        u = m.sb("u", [P, Q, D])
        u2 = m.sb("u2", [P, Q, D])
        x1 = m.sb("x1", [P, 2, Q, D])
        x1b = m.sb("x1b", [P, 2, Q, D])
        xT = m.sb("xT", [128, 2, Q * P])
        hT = m.sb("hT", [128, 2, 2, Q * P])
        den = m.sb("den", [P, Q, 8])
        stat = m.sb("stat", [P, 2, Q, 6])
        ms = m.sb("ms", [P, 2, Q, 3])
        half = m.sb("half", [P, Q])
        pt = m.ps("pt", [128, Q, 512])
        pT = m.ps("pT")
        ph = m.ps("ph")
        py = m.ps("py")
        names = ("nm_ready", "pt_ready", "pt_free", "x1_ready", "x1_for_sum", "x1b_ready", "xb_ready", "pT_ready", "xT_ready", "ph_ready", "hT_ready",
                 "py_ready", "ch", "act_ch", "pool_ch", "ld")
        s = {n: m.sem(n) for n in names}
        S = {n: [m.sem(n + "0"), m.sem(n + "1")] for n in ("qs_ready", "qs_free", "xn_ready", "xn_free", "var_ready", "rstd_ready")}
        with nc.Block() as block:

            @block.sync
            def _(e):
                e.dma_start(w1[:, :, :], a["mix_w1"].rearrange("(b i) o -> i b o", b=2)).then_inc(s["ld"], 16)
                e.dma_start(w2[:, :, :], a["mix_w2"].rearrange("(b i) o -> i b o", b=2)).then_inc(s["ld"], 16)
                e.dma_start(b1[:, :], a["mix_b1"]).then_inc(s["ld"], 16)
                for n, name in enumerate(("L0_mix_ln1_g", "L0_mix_ln1_b", "L0_mix_b2", "L0_mix_ln2_g", "L0_mix_ln2_b")):
                    e.dma_start(gb[:, n, :], a[name].partition_broadcast(P)).then_inc(s["ld"], 16)
                e.wait_ge(s["ld"], 128)
                e.sem_inc(s["ld"], -(128))
        both = lambda n: gb[:, n, :].unsqueeze(1).to_broadcast([P, Q, D])
        xpair = lambda n: X[:, bass.ds(n * (Q * D), Q * D)].rearrange("p (q w) -> p q w", w=D)
        with nc.Block() as block:

            @block.gpsimd
            def _(e):
                g = nc.gpsimd
                c = Count(e, s["pool_ch"])
                g.memset(half[:, :], -0.5).then_inc(c.sem, 1)
                e.wait_ge(s["pool_ch"], c.next())
                c.reset()
                for par in range(2):
                    e.sem_inc(S["qs_free"][par], 1)

                def queries(n, par):
                    e.wait_ge(S["qs_free"][par], 1)
                    e.sem_inc(S["qs_free"][par], -1)
                    g.tensor_copy(qs[:, par, :], qT[:, bass.ds(n * (Q * 2 * P), Q * 2 * P)]).then_inc(S["qs_ready"][par], 1)

                def deviation(n):
                    e.wait_ge(S["var_ready"][n], 1)
                    e.sem_inc(S["var_ready"][n], -1)
                    g.tensor_scalar(ms[:, n, :, 1], ms[:, n, :, 1], 1e-5, None, ALU.add).then_inc(s["pool_ch"], 1)
                    e.wait_ge(s["pool_ch"], 1)
                    e.sem_inc(s["pool_ch"], -1)
                    g.tensor_tensor(out=ms[:, n, :, 2], in0=ms[:, n, :, 1], in1=half[:, :], op=ALU.pow).then_inc(S["rstd_ready"][n], 1)

                def turn(n, par, attend=True, finish=True, ahead=True, middle=True):
                    if ahead:
                        queries(n + 2, par)
                    if middle:
                        e.wait_ge(s["x1_for_sum"], 1)
                        e.sem_inc(s["x1_for_sum"], -1)
                        g.tensor_tensor(out=x1b[:, par, :, :], in0=x1[:, par, :, :], in1=both(2), op=ALU.add).then_inc(s["x1b_ready"], 1)
                        g.tensor_tensor(out=xpair(n), in0=xpair(n), in1=both(4), op=ALU.add).then_inc(s["xb_ready"], 1)
                    if attend:
                        deviation(0)
                    if finish:
                        deviation(1)
                queries(0, 0)
                queries(1, 1)
                deviation(0)
                turn(0, 0, finish=False)
                with e.Fori(0, (NS - 3) // 2) as i:
                    turn(i * 2 + 1, 1)
                    turn(i * 2 + 2, 0)
                turn(NS - 2, 1, ahead=False)
                turn(NS - 1, 0, ahead=False, attend=False)
                turn(NS, 1, ahead=False, attend=False, middle=False)

            @block.tensor
            def _(e):
                t_ = nc.tensor
                e.sem_inc(s["pt_free"], 1)

                def attention(par):
                    e.wait_ge(S["qs_ready"][par], 1)
                    e.sem_inc(S["qs_ready"][par], -1)
                    e.wait_ge(s["pt_free"], 1)
                    e.sem_inc(s["pt_free"], -1)
                    for q in range(Q):
                        for b in range(2):
                            ins = t_.matmul(pt[:P, q, b * 132:(b + 1) * 132], qs[:, par, (q * 2 + b) * P:(q * 2 + b + 1) * P], kv[:, b * 132:(b + 1) * 132], start=True, stop=True)
                    ins.then_inc(s["pt_ready"], 1)

                def turn(par, attend=True, finish=True, middle=True):
                    if finish:
                        e.wait_ge(s["hT_ready"], 1)
                        e.sem_inc(s["hT_ready"], -1)
                        if middle:
                            e.wait_ge(s["x1_ready"], 1)
                            e.sem_inc(s["x1_ready"], -1)
                        for q in range(Q):
                            for b in range(2):
                                ins = t_.matmul(py[:P, q * D:(q + 1) * D], hT[:, 1 - par, b, q * P:(q + 1) * P], w2[:, b, :], start=b == 0, stop=b == 1)
                        ins.then_inc(s["py_ready"], 1)
                    else:
                        e.wait_ge(s["x1_ready"], 1)
                        e.sem_inc(s["x1_ready"], -1)
                    if attend:
                        attention(1 - par)
                    if middle:
                        for b in range(2):
                            for q in range(Q):
                                ins = t_.transpose(pT[:, (b * Q + q) * P:(b * Q + q + 1) * P], x1[:, par, q, b * 128:(b + 1) * 128], const.ident[:P, :P])
                        ins.then_inc(s["pT_ready"], 1)
                        e.wait_ge(s["xT_ready"], 1)
                        e.sem_inc(s["xT_ready"], -1)
                        for o in range(2):
                            for b in range(2):
                                ins = t_.matmul(ph[:, o * Q * P:(o + 1) * Q * P], w1[:, b, o * 128:(o + 1) * 128], xT[:, b, :], start=b == 0, stop=b == 1)
                        ins.then_inc(s["ph_ready"], 1)
                attention(0)
                turn(0, finish=False)
                with e.Fori(0, (NS - 3) // 2) as i:
                    turn(1)
                    turn(0)
                turn(1)
                turn(0, attend=False)
                e.wait_ge(s["x1_ready"], 1)
                e.sem_inc(s["x1_ready"], -1)
                turn(1, attend=False, middle=False)

            @block.scalar
            def _(e):
                A = nc.scalar
                c = Count(e, s["act_ch"])
                for par in range(2):
                    e.sem_inc(S["xn_free"][par], 1)

                def normed(n, par):
                    e.wait_ge(S["xn_free"][par], 1)
                    e.sem_inc(S["xn_free"][par], -1)
                    for q in range(Q):
                        ins = A.activation(xc[:, par, q, :], X[:, bass.ds((n * Q + q) * D, D)], ACT.Identity, bias=nmean[:, bass.ds(n * Q + q, 1)])
                    ins.then_inc(s["act_ch"], 1)
                    e.wait_ge(s["act_ch"], c.next())
                    for q in range(Q):
                        ins = A.activation(xn[:, par, q, :], xc[:, par, q, :], ACT.Copy, scale=rstd[:, bass.ds(n * Q + q, 1)])
                    ins.then_inc(S["xn_ready"][par], 1)
                    c.reset()

                def turn(n, par, ahead=True):
                    if ahead:
                        normed(n + 2, par)
                    e.wait_ge(s["pT_ready"], 1)
                    e.sem_inc(s["pT_ready"], -1)
                    A.activation(xT[:, :, :], pT[:, 0:2 * Q * P].rearrange("p (b n) -> p b n", b=2), ACT.Copy).then_inc(s["xT_ready"], 1)
                    e.wait_ge(s["ph_ready"], 1)
                    e.sem_inc(s["ph_ready"], -1)
                    for o in range(2):
                        ins = A.activation(hT[:, par, o, :], ph[:, o * Q * P:(o + 1) * Q * P], ACT.Gelu, bias=b1[:, o:o + 1])
                    ins.then_inc(s["hT_ready"], 1)
                e.wait_ge(s["nm_ready"], 1)
                e.sem_inc(s["nm_ready"], -1)
                normed(0, 0)
                normed(1, 1)
                with e.Fori(0, (NS - 3) // 2) as i:
                    turn(i * 2, 0)
                    turn(i * 2 + 1, 1)
                turn(NS - 3, 0)
                turn(NS - 2, 1, ahead=False)
                turn(NS - 1, 0, ahead=False)

            @block.vector
            def _(e):
                v = nc.vector
                c = Count(e, s["ch"])
                v.tensor_scalar(nmean[:, :], mean[:, :], -1.0, None, ALU.mult).then_inc(s["nm_ready"], 1)

                def stats(n, x):
                    for q in range(Q):
                        ins = v.bn_stats(out=stat[:, n, q, :], in_=x[:, q, :])
                    ins.then_inc(s["ch"], 1)
                    e.wait_ge(s["ch"], c.next())
                    for q in range(Q):
                        ins = v.bn_aggr(out=ms[:, n, q, 0:2], in_=stat[:, n, q, :])
                    ins.then_inc(S["var_ready"][n], 1)

                def norm(n, x, gamma):
                    e.wait_ge(S["rstd_ready"][n], 1)
                    e.sem_inc(S["rstd_ready"][n], -1)
                    for q in range(Q):
                        ins = v.scalar_tensor_tensor(x[:, q, :], x[:, q, :], ms[:, n, q, 0:1], gamma, ALU.subtract, ALU.mult)
                    ins.then_inc(s["ch"], 1)
                    e.wait_ge(s["ch"], c.next())

                def attend(par):
                    e.wait_ge(s["pt_ready"], 1)
                    e.sem_inc(s["pt_ready"], -1)
                    e.sem_inc(S["qs_free"][par], 1)
                    p4 = pt[:P, :, 0:264].rearrange("p q (b w) -> p q b w", w=132)
                    v.tensor_scalar(den[:, :, :].rearrange("p q (b g) -> p q b g", b=2), p4[:, :, :, 128:132], 1e-6, None, ALU.add).then_inc(s["ch"], 1)
                    e.wait_ge(s["ch"], c.next())
                    v.reciprocal(den[:, :, :], den[:, :, :]).then_inc(s["ch"], 1)
                    e.wait_ge(s["ch"], c.next())
                    for q in range(Q):
                        ins = v.tensor_tensor(out=at[:, q, :].rearrange("p (b g d) -> p b g d", b=2, g=4), in0=p4[:, q, :, 0:128].rearrange("p b (g d) -> p b g d", g=4),
                                              in1=den[:, q, :].rearrange("p (b g) -> p b g", b=2).unsqueeze(3).to_broadcast([P, 2, 4, 32]), op=ALU.mult)
                    ins.then_inc(s["ch"], 1)
                    e.wait_ge(s["ch"], c.next())
                    e.sem_inc(s["pt_free"], 1)
                    e.wait_ge(S["xn_ready"][par], 1)
                    e.sem_inc(S["xn_ready"][par], -1)
                    v.tensor_tensor(out=u[:, :, :], in0=xn[:, par, :, :], in1=at[:, :, :], op=ALU.add).then_inc(s["ch"], 1)
                    e.wait_ge(s["ch"], c.next())
                    e.sem_inc(S["xn_free"][par], 1)
                    stats(0, u)

                def attended(par):
                    norm(0, u, gb[:, 0, :])
                    for q in range(Q):
                        ins = v.scalar_tensor_tensor(x1[:, par, q, :], u[:, q, :], ms[:, 0, q, 2:3], gb[:, 1, :], ALU.mult, ALU.add)
                    ins.then_inc(s["ch"], 1)
                    e.wait_ge(s["ch"], c.next())
                    e.sem_inc(s["x1_ready"], 1)
                    e.sem_inc(s["x1_for_sum"], 1)

                def turn(n, par, att=True, finish=True):
                    if att:
                        attend(1 - par)
                    if finish:
                        e.wait_ge(s["py_ready"], 1)
                        e.sem_inc(s["py_ready"], -1)
                        e.wait_ge(s["x1b_ready"], 1)
                        e.sem_inc(s["x1b_ready"], -1)
                        v.tensor_tensor(out=u2[:, :, :], in0=py[:P, 0:Q * D].rearrange("p (q w) -> p q w", w=D), in1=x1b[:, 1 - par, :, :], op=ALU.add).then_inc(s["ch"], 1)
                        e.wait_ge(s["ch"], c.next())
                        stats(1, u2)
                    if att:
                        attended(1 - par)
                    elif finish and n is not None:
                        e.sem_inc(s["x1_ready"], 1)
                    if finish:
                        norm(1, u2, gb[:, 3, :])
                        e.wait_ge(s["xb_ready"], 1)
                        e.sem_inc(s["xb_ready"], -1)
                        k = n - 1 if n is not None else NS - 1
                        for q in range(Q):
                            xt = X[:, bass.ds((k * Q + q) * D, D)]
                            ins = v.scalar_tensor_tensor(xt, u2[:, q, :], ms[:, 1, q, 2:3], xt, ALU.mult, ALU.add)
                        ins.then_inc(s["ch"], 1)
                        e.wait_ge(s["ch"], c.next())
                    c.reset()
                attend(0)
                attended(0)
                turn(0, 0, finish=False)
                with e.Fori(0, (NS - 3) // 2) as i:
                    turn(i * 2 + 1, 1)
                    turn(i * 2 + 2, 0)
                turn(NS - 2, 1)
                turn(NS - 1, 0, att=False)
                turn(None, 1, att=False)


NE = 8
CAP0 = 977
ER = 1000
F0, F1 = 1024, 512
FLT_MAX = 3.4028235e38


def moe_gate(nc, const, X, mean, rstd, XN, gw, gb, bufx, slot_idx, back_idx, wgt):
    with Mem(nc, "mg") as m:
        xs = m.sb("xs", [P, 2, D])
        xT = m.sb("xT", [128, 2, 2 * P])
        lg = m.sb("lg", [P, T * NE])
        pr = m.sb("pr", [P, T * NE])
        oh = m.sb("oh", [P, T * NE])
        ohT = m.sb("ohT", [P, NE * T])
        cum = m.sb("cum", [P, NE * T])
        rm = m.sb("rm", [P, NE * T])
        tk = m.sb("tk", [P, 6, T])
        tot = m.sb("tot", [P, NE])
        pT = [m.ps("pT0"), m.ps("pT1")]
        pl = [m.ps("pl0"), m.ps("pl1")]
        poff = m.ps("poff")
        names = ("ch", "lg_sub", "ex_done", "tot_ready", "off_ready", "slots")
        s = {n: m.sem(n) for n in names}
        s["sc"] = m.counter("sc")
        S = {n: [m.sem(n + "0"), m.sem(n + "1")] for n in ("xn_ready", "pT_ready", "xT_ready", "pl_ready", "pl_free", "xs_free")}
        with nc.Block() as block:

            @block.vector
            def _(e):
                v = nc.vector
                c = Count(e, s["ch"])

                for par in range(2):
                    e.sem_inc(S["xs_free"][par], 1)

                def norm(t, par):
                    e.wait_ge(S["xs_free"][par], 1)
                    e.sem_inc(S["xs_free"][par], -1)
                    v.tensor_scalar(xs[:, par, :], X[:, bass.ds(t * D, D)], mean[:, bass.ds(t, 1)], rstd[:, bass.ds(t, 1)],
                                    ALU.subtract, ALU.mult).then_inc(S["xn_ready"][par], 1)

                def logits(t, par):
                    e.wait_ge(S["pl_ready"][par], 1)
                    e.sem_inc(S["pl_ready"][par], -1)
                    v.tensor_tensor(out=lg[:, bass.ds(t * NE, NE)], in0=pl[par][:P, 0:NE], in1=gb[:, :], op=ALU.add).then_inc(S["pl_free"][par], 1)
                norm(0, 0)
                with e.Fori(0, T // 2 - 1) as i:
                    norm(i * 2 + 1, 1)
                    logits(i * 2, 0)
                    norm(i * 2 + 2, 0)
                    logits(i * 2 + 1, 1)
                norm(T - 1, 1)
                logits(T - 2, 0)
                logits(T - 1, 1)
                te = lambda x: x[:, :].rearrange("p (t e) -> p t e", e=NE)
                et = lambda x: x[:, :].rearrange("p (e t) -> p t e", e=NE)
                bc = lambda x: x.unsqueeze(2).to_broadcast([P, T, NE])
                v.memset(rm[:, :], 1.0).then_inc(s["ch"], 1)
                e.wait_ge(s["ch"], c.next())
                v.memset(rm[:, :].rearrange("p (e t) -> p e t", e=NE)[:, :, 0:1], 0.0).then_inc(s["ch"], 1)
                e.wait_ge(s["ch"], c.next())
                v.tensor_reduce(out=tk[:, 0, :], in_=te(lg), axis=AX.X, op=ALU.max).then_inc(s["ch"], 1)
                e.wait_ge(s["ch"], c.next())
                v.tensor_tensor(out=te(lg), in0=te(lg), in1=bc(tk[:, 0, :]), op=ALU.subtract).then_inc(s["ch"], 1)
                e.wait_ge(s["ch"], c.next())
                e.sem_inc(s["lg_sub"], 1)
                e.wait_ge(s["ex_done"], 1)
                e.sem_inc(s["ex_done"], -1)
                v.tensor_reduce(out=tk[:, 0, :], in_=te(pr), axis=AX.X, op=ALU.add).then_inc(s["ch"], 1)
                e.wait_ge(s["ch"], c.next())
                v.reciprocal(tk[:, 0, :], tk[:, 0, :]).then_inc(s["ch"], 1)
                e.wait_ge(s["ch"], c.next())
                v.tensor_tensor(out=te(pr), in0=te(pr), in1=bc(tk[:, 0, :]), op=ALU.mult).then_inc(s["ch"], 1)
                e.wait_ge(s["ch"], c.next())
                v.tensor_reduce(out=tk[:, 0, :], in_=te(pr), axis=AX.X, op=ALU.max).then_inc(s["ch"], 1)
                e.wait_ge(s["ch"], c.next())
                v.tensor_tensor(out=te(oh), in0=te(pr), in1=bc(tk[:, 0, :]), op=ALU.is_equal).then_inc(s["ch"], 1)
                e.wait_ge(s["ch"], c.next())
                v.tensor_scalar(oh[:, :], oh[:, :], -float(NE), float(NE), ALU.mult, ALU.add).then_inc(s["ch"], 1)
                e.wait_ge(s["ch"], c.next())
                ib = const.iota[:P, 0:NE].unsqueeze(1).to_broadcast([P, T, NE])
                v.tensor_tensor(out=te(oh), in0=te(oh), in1=ib, op=ALU.add).then_inc(s["ch"], 1)
                e.wait_ge(s["ch"], c.next())
                v.tensor_reduce(out=tk[:, 1, :], in_=te(oh), axis=AX.X, op=ALU.min).then_inc(s["ch"], 1)
                e.wait_ge(s["ch"], c.next())
                v.tensor_tensor(out=et(ohT), in0=ib, in1=bc(tk[:, 1, :]), op=ALU.is_equal).then_inc(s["ch"], 1)
                e.wait_ge(s["ch"], c.next())
                v.tensor_tensor_scan(out=cum[:, :], data0=rm[:, :], data1=ohT[:, :], initial=0.0, op0=ALU.mult, op1=ALU.add).then_inc(s["ch"], 1)
                e.wait_ge(s["ch"], c.next())
                v.tensor_copy(tot[:, :], cum[:, :].rearrange("p (e t) -> p e t", e=NE)[:, :, T - 1]).then_inc(s["ch"], 1)
                e.wait_ge(s["ch"], c.next())
                e.sem_inc(s["tot_ready"], 1)
                e.wait_ge(s["off_ready"], 1)
                e.sem_inc(s["off_ready"], -1)
                c3 = cum[:, :].rearrange("p (e t) -> p e t", e=NE)
                v.tensor_tensor(out=c3, in0=c3, in1=poff[:P, 0:NE].unsqueeze(2).to_broadcast([P, NE, T]), op=ALU.add).then_inc(s["ch"], 1)
                e.wait_ge(s["ch"], c.next())
                v.tensor_tensor(out=cum[:, :], in0=cum[:, :], in1=ohT[:, :], op=ALU.mult).then_inc(s["ch"], 1)
                e.wait_ge(s["ch"], c.next())
                v.tensor_reduce(out=tk[:, 2, :], in_=et(cum), axis=AX.X, op=ALU.add).then_inc(s["ch"], 1)
                e.wait_ge(s["ch"], c.next())
                v.tensor_scalar(tk[:, 3, :], tk[:, 2, :], float(CAP0), None, ALU.is_le).then_inc(s["ch"], 1)
                e.wait_ge(s["ch"], c.next())
                v.tensor_tensor(out=wgt[:, :], in0=tk[:, 0, :], in1=tk[:, 3, :], op=ALU.mult).then_inc(s["ch"], 1)
                e.wait_ge(s["ch"], c.next())
                v.tensor_scalar(tk[:, 4, :], tk[:, 2, :], float(CAP0), -1.0, ALU.min, ALU.add).then_inc(s["ch"], 1)
                e.wait_ge(s["ch"], c.next())
                v.scalar_tensor_tensor(tk[:, 4, :], tk[:, 1, :], float(ER), tk[:, 4, :], ALU.mult, ALU.add).then_inc(s["ch"], 1)
                e.wait_ge(s["ch"], c.next())
                v.tensor_copy(back_idx[:, :], tk[:, 4, :]).then_inc(s["ch"], 1)
                e.wait_ge(s["ch"], c.next())
                v.tensor_scalar(tk[:, 5, :], tk[:, 3, :], -OOB, OOB, ALU.mult, ALU.add).then_inc(s["ch"], 1)
                e.wait_ge(s["ch"], c.next())
                v.tensor_tensor(out=tk[:, 5, :], in0=tk[:, 5, :], in1=tk[:, 4, :], op=ALU.add).then_inc(s["ch"], 1)
                e.wait_ge(s["ch"], c.next())
                v.tensor_copy(slot_idx[:, :], tk[:, 5, :]).then_inc(s["ch"], 1)
                e.wait_ge(s["ch"], c.next())
                e.wait_ge(S["xs_free"][0], 1)
                e.sem_inc(S["xs_free"][0], -1)
                e.wait_ge(S["xs_free"][1], 1)
                e.sem_inc(S["xs_free"][1], -1)
                e.sem_inc(s["slots"], 1)
                c.reset()

            @block.scalar
            def _(e):
                def body(t, par):
                    e.wait_ge(S["pT_ready"][par], 1)
                    e.sem_inc(S["pT_ready"][par], -1)
                    nc.scalar.activation(xT[:, par, :], pT[par][:, 0:2 * P], ACT.Copy).then_inc(S["xT_ready"][par], 1)
                    nc.scalar.activation(XN[:, bass.ds(t * D, D)], xs[:, par, :], ACT.Copy).then_inc(S["xs_free"][par], 1)
                steps(e, T, body)
                e.wait_ge(s["lg_sub"], 1)
                e.sem_inc(s["lg_sub"], -1)
                nc.scalar.activation(pr[:, :], lg[:, :], ACT.Exp).then_inc(s["ex_done"], 1)

            @block.tensor
            def _(e):
                t_ = nc.tensor
                e.sem_inc(S["pl_free"][0], 1)
                e.sem_inc(S["pl_free"][1], 1)

                def body(t, par):
                    e.wait_ge(S["xn_ready"][par], 1)
                    e.sem_inc(S["xn_ready"][par], -1)
                    for b in range(2):
                        ins = t_.transpose(pT[par][:, b * P:(b + 1) * P], xs[:, par, b * 128:(b + 1) * 128], const.ident[:P, :P])
                    ins.then_inc(S["pT_ready"][par], 1)
                    e.wait_ge(S["xT_ready"][par], 1)
                    e.sem_inc(S["xT_ready"][par], -1)
                    e.wait_ge(S["pl_free"][par], 1)
                    e.sem_inc(S["pl_free"][par], -1)
                    for b in range(2):
                        ins = t_.matmul(pl[par][:P, 0:NE], xT[:, par, b * P:(b + 1) * P], gw[:, b, :], start=b == 0, stop=b == 1)
                    ins.then_inc(S["pl_ready"][par], 1)
                steps(e, T, body)
                e.wait_ge(s["tot_ready"], 1)
                e.sem_inc(s["tot_ready"], -1)
                t_.matmul(poff[:P, 0:NE], const.tri[:P, :P], tot[:, :], start=True, stop=True).then_inc(s["off_ready"], 1)

            @block.gpsimd
            def _(e):
                e.wait_ge(s["slots"], 1)
                e.sem_inc(s["slots"], -1)
                for t in range(T):
                    e.indirect_dma_start(out=bufx[:, :], out_offset=bass.IndirectOffsetOnAxis(ap=slot_idx[:, t:t + 1], axis=0),
                                         in_=XN[:, t * D:(t + 1) * D], in_offset=None, bounds_check=NE * ER - 1, oob_is_err=False).then_inc(s["sc"], 16)
                e.wait_ge(s["sc"], 16 * T)


def moe_experts(nc, const, bufx, bufy, w1, w2, b1, b2):
    NF = F0 // 128
    R = 4 * P
    with Mem(nc, "me") as m:
        w1s = m.sb("w1", [128, 2, 2 * F0])
        w2s = m.sb("w2", [128, 2, NF * D])
        b1s = m.sb("b1", [128, NE * NF])
        b2s = m.sb("b2", [P, NE * D])
        xr = m.sb("xr", [P, 2, 4 * D])
        xT = m.sb("xT", [128, 2, R])
        hT = m.sb("hT", [128, NF, R])
        yr = m.sb("yr", [P, 2, 4 * D])
        pT = [m.ps("pT0"), m.ps("pT1")]
        ph = [m.ps(f"ph{i}") for i in range(3)]
        py = [m.ps(f"py{i}") for i in range(2)]
        S = {n: [m.sem(n + "0"), m.sem(n + "1")] for n in ("w_ld", "w_free", "x_ld", "x_free", "y_ready", "y_free", "py_ready", "py_free", "pT_ready")}
        S["y_st"] = [m.counter("y_st0"), m.counter("y_st1")]
        ph_ready, ph_free = [m.sem(f"ph_ready{i}") for i in range(3)], [m.sem(f"ph_free{i}") for i in range(3)]
        xT_ready, bld = m.sem("xT_ready"), m.sem("bld")
        xv = bufx.rearrange("(s p q) d -> (s p) (q d)", s=2 * NE, q=4)
        yv = bufy.rearrange("(s p q) d -> (s p) (q d)", s=2 * NE, q=4)
        with nc.Block() as block:

            @block.sync
            def _(e):
                e.dma_start(b1s[:, :], b1).then_inc(bld, 16)
                e.dma_start(b2s[:, :], b2.rearrange("e d -> (e d)").partition_broadcast(P)).then_inc(bld, 16)
                e.wait_ge(bld, 32)
                e.sem_inc(bld, -32)
        with nc.Block() as block:

            @block.sync
            def _(e):
                for b in range(2):
                    e.sem_inc(S["w_free"][b], 1)
                    e.sem_inc(S["x_free"][b], 1)

                def weights(x, p):
                    e.wait_ge(S["w_free"][p], 1)
                    e.sem_inc(S["w_free"][p], -1)
                    e.dma_start(w1s[:, p, :].rearrange("p (b f) -> p b f", b=2), w1[bass.ds(x * D, D), :].rearrange("(b i) f -> i b f", b=2)).then_inc(S["w_ld"][p], 16)
                    e.dma_start(w2s[:, p, :].rearrange("p (g d) -> p g d", d=D), w2[bass.ds(x * F0, F0), :].rearrange("(g f) d -> f g d", f=128)).then_inc(S["w_ld"][p], 16)

                def body(x, p, last=False):
                    for h in range(2):
                        e.wait_ge(S["x_free"][h], 1)
                        e.sem_inc(S["x_free"][h], -1)
                        e.dma_start(xr[:, h, :], xv[bass.ds((x * 2 + h) * P, P), :]).then_inc(S["x_ld"][h], 16)
                    if not last:
                        weights(x + 1, 1 - p)
                weights(0, 0)
                with e.Fori(0, NE // 2 - 1) as i:
                    body(i * 2, 0)
                    body(i * 2 + 1, 1)
                body(NE - 2, 0)
                body(NE - 1, 1, last=True)

            @block.tensor
            def _(e):
                t = nc.tensor
                for q in S["py_free"] + ph_free:
                    e.sem_inc(q, 1)

                def transposes(h):
                    e.wait_ge(S["x_ld"][h], 16)
                    e.sem_inc(S["x_ld"][h], -(16))
                    for b in range(2):
                        for q in range(4):
                            ins = t.transpose(pT[b][:, q * P:(q + 1) * P], xr[:, h, q * D + b * 128:q * D + b * 128 + 128], const.ident[:P, :P])
                        ins.then_inc(S["pT_ready"][b], 1)

                def half(p, h, first=False, last=False):
                    e.wait_ge(xT_ready, 2)
                    e.sem_inc(xT_ready, -(2))
                    for f in range(NF):
                        if f >= 3 or first:
                            e.wait_ge(ph_free[f % 3], 1)
                            e.sem_inc(ph_free[f % 3], -1)
                        for b in range(2):
                            ins = t.matmul(ph[f % 3][:, 0:R], w1s[:, p, b * F0 + f * 128:b * F0 + f * 128 + 128], xT[:, b, :], start=b == 0, stop=b == 1)
                        ins.then_inc(ph_ready[f % 3], 1)
                    if not last:
                        transposes(1 - h)
                    for q in range(4):
                        e.wait_ge(S["py_free"][q % 2], 1)
                        e.sem_inc(S["py_free"][q % 2], -1)
                        for f in range(NF):
                            if q == 0 and f >= NF - 3:
                                e.wait_ge(ph_free[f % 3], 1)
                                e.sem_inc(ph_free[f % 3], -1)
                            ins = t.matmul(py[q % 2][:P, 0:D], hT[:, f, q * P:(q + 1) * P], w2s[:, p, f * D:(f + 1) * D], start=f == 0, stop=f == NF - 1)
                        ins.then_inc(S["py_ready"][q % 2], 1)

                def expert(p, first=False, last=False):
                    e.wait_ge(S["w_ld"][p], 32)
                    e.sem_inc(S["w_ld"][p], -(32))
                    half(p, 0, first=first)
                    half(p, 1, last=last)
                transposes(0)
                expert(0, first=True)
                expert(1)
                with e.Fori(0, NE // 2 - 2) as i:
                    expert(0)
                    expert(1)
                expert(0)
                expert(1, last=True)

            @block.scalar
            def _(e):
                a = nc.scalar

                def transposed(h):
                    for b in range(2):
                        e.wait_ge(S["pT_ready"][b], 1)
                        e.sem_inc(S["pT_ready"][b], -1)
                        if b == 1:
                            e.sem_inc(S["x_free"][h], 1)
                        a.activation(xT[:, b, :], pT[b][:, 0:R], ACT.Copy).then_inc(xT_ready, 1)

                def half(x, h, last=False):
                    for f in range(NF):
                        e.wait_ge(ph_ready[f % 3], 1)
                        e.sem_inc(ph_ready[f % 3], -1)
                        a.activation(hT[:, f, :], ph[f % 3][:, 0:R], ACT.Relu, bias=b1s[:, bass.ds(x * NF + f, 1)]).then_inc(ph_free[f % 3], 1)
                    if not last:
                        transposed(1 - h)
                transposed(0)
                with e.Fori(0, NE - 1) as x:
                    half(x, 0)
                    half(x, 1)
                half(NE - 1, 0)
                half(NE - 1, 1, last=True)

            @block.vector
            def _(e):
                v = nc.vector
                for b in range(2):
                    e.sem_inc(S["y_free"][b], 1)

                def body(x, p):
                    for h in range(2):
                        e.wait_ge(S["y_free"][h], 1)
                        e.sem_inc(S["y_free"][h], -1)
                        for q in range(4):
                            e.wait_ge(S["py_ready"][q % 2], 1)
                            e.sem_inc(S["py_ready"][q % 2], -1)
                            if q == 3 and h == 1:
                                e.sem_inc(S["w_free"][p], 1)
                            ins = v.tensor_tensor(out=yr[:, h, q * D:(q + 1) * D], in0=py[q % 2][:P, 0:D], in1=b2s[:, bass.ds(x * D, D)], op=ALU.add)
                            ins.then_inc(S["py_free"][q % 2], 1)
                        e.drain().then_inc(S["y_ready"][h], 1)
                steps(e, NE, body)

            @block.gpsimd
            def _(e):
                def body(x, p):
                    for h in range(2):
                        e.wait_ge(S["y_ready"][h], 1)
                        e.sem_inc(S["y_ready"][h], -1)
                        e.dma_start(yv[bass.ds((x * 2 + h) * P, P), :], yr[:, h, :]).then_inc(S["y_st"][h], 16)
                        e.wait_ge(S["y_st"][h], x * 16 + 16)
                        e.sem_inc(S["y_free"][h], 1)
                steps(e, NE, body)


def moe_return(nc, X, bufy, back_idx, wgt):
    G = 5
    with Mem(nc, "mr") as m:
        y = m.sb("y", [P, 2, G * D])
        mk = m.sb("mk", [P, G * D])
        cst = m.sb("cst", [P, 3])
        idx = m.sb("idx", [P, 2, G], I32)
        ch = m.sem("ch")
        ready = [m.sem("ready0"), m.sem("ready1")]
        ga = [m.counter("ga0"), m.counter("ga1")]
        n_steps = T // G
        with nc.Block() as block:

            @block.gpsimd
            def _(e):
                with e.Fori(0, n_steps // 2) as i:
                    for b in range(2):
                        e.wait_ge(ready[b], 1)
                        e.sem_inc(ready[b], -1)
                        for k in range(G):
                            e.indirect_dma_start(out=y[:, b, k * D:(k + 1) * D], out_offset=None, in_=bufy[:, :],
                                                 in_offset=bass.IndirectOffsetOnAxis(ap=idx[:, b, k:k + 1], axis=0)).then_inc(ga[b], 16)

            @block.vector
            def _(e):
                v = nc.vector
                c = Count(e, ch)
                for n, x in enumerate((0.0, 10000.0, -10000.0)):
                    v.memset(cst[:, n:n + 1], x).then_inc(ch, 1)
                    e.wait_ge(ch, c.next())

                def stage(s, b):
                    v.tensor_copy(idx[:, b, :], back_idx[:, bass.ds(s * G, G)]).then_inc(ready[b], 1)

                def body(i, b, last):
                    s = i * 2 + b
                    if not last:
                        stage(s + 1, 1 - b)
                    e.wait_ge(ga[b], i * (16 * G) + 16 * G)
                    yb = y[:, b, :]
                    y3 = yb.rearrange("p (k w) -> p k w", w=D)
                    v.tensor_tensor(out=y3, in0=y3, in1=wgt[:, bass.ds(s * G, G)].unsqueeze(2).to_broadcast([P, G, D]), op=ALU.mult).then_inc(ch, 1)
                    e.wait_ge(ch, c.next())
                    v.tensor_scalar(mk[:, :], yb, FLT_MAX, None, ALU.is_gt).then_inc(ch, 1)
                    e.wait_ge(ch, c.next())
                    v.copy_predicated(yb, mk[:, :].bitcast(I32), cst[:, 1:2].to_broadcast([P, G * D])).then_inc(ch, 1)
                    e.wait_ge(ch, c.next())
                    v.tensor_scalar(mk[:, :], yb, -FLT_MAX, None, ALU.is_lt).then_inc(ch, 1)
                    e.wait_ge(ch, c.next())
                    v.copy_predicated(yb, mk[:, :].bitcast(I32), cst[:, 2:3].to_broadcast([P, G * D])).then_inc(ch, 1)
                    e.wait_ge(ch, c.next())
                    v.tensor_tensor(out=mk[:, :], in0=yb, in1=yb, op=ALU.not_equal).then_inc(ch, 1)
                    e.wait_ge(ch, c.next())
                    v.copy_predicated(yb, mk[:, :].bitcast(I32), cst[:, 0:1].to_broadcast([P, G * D])).then_inc(ch, 1)
                    e.wait_ge(ch, c.next())
                    xs = X[:, bass.ds(s * (G * D), G * D)]
                    v.tensor_tensor(out=xs, in0=xs, in1=yb, op=ALU.add).then_inc(ch, 1)
                    e.wait_ge(ch, c.next())
                    c.reset()
                c.reset()
                stage(0, 0)
                with e.Fori(0, n_steps // 2 - 1) as i:
                    body(i, 0, False)
                    body(i, 1, False)
                body(n_steps // 2 - 1, 0, False)
                body(n_steps // 2 - 1, 1, True)


VW = D + 1


def dense1(nc, const, ed, X, mean, rstd, wz, wqk, wv, bkv, bq, zt, edt, edn, edge_ed, KS, VS, kmax, q_dram):
    with Mem(nc, "d1") as m:
        xn = m.sb("xn", [P, 2, D])
        xT = m.sb("xT", [128, 2, 2 * P])
        zr = m.sb("zr", [P, 2, ZW + HEADS])
        qs = m.sb("qs", [128, 2, 2 * P])
        pT = m.ps("pT")
        pz, pkv, pq = m.ps("pz"), [m.ps("pkv0"), m.ps("pkv1")], [m.ps("pq0"), m.ps("pq1")]
        S = {n: [m.sem(n + "0"), m.sem(n + "1")] for n in
             ("xn_ready", "xn_free", "zr_ready", "zr_free", "zr_stored", "pkv_ready", "pkv_free", "pq_ready", "pq_free", "q_ready", "q_stored", "q_free")}
        pT_ready, xT_ready, ch, pz_ready, pz_free, ed_done, edst, row_ready = (
            m.sem(x) for x in ("pT_ready", "xT_ready", "ch", "pz_ready", "pz_free", "ed_done", "edst", "row_ready"))
        scattered = m.counter("scattered")
        zt_v = zt.rearrange("(p t) w -> p (t w)", t=T)
        with nc.Block() as block:

            @block.vector
            def _(e):
                v = nc.vector
                c = Count(e, ch)
                v.memset(VS[:, :].rearrange("p (t w) -> p t w", w=VW)[:, :, D:VW], 1.0).then_inc(ch, 1)
                e.wait_ge(ch, c.next())
                v.memset(kmax[:, :], -FLT_MAX).then_inc(ch, 1)
                e.wait_ge(ch, c.next())
                for par in range(2):
                    e.sem_inc(S["xn_free"][par], 1)
                c.reset()

                def norm(t, par):
                    e.wait_ge(S["xn_free"][par], 1)
                    e.sem_inc(S["xn_free"][par], -1)
                    v.tensor_scalar(xn[:, par, :], X[:, bass.ds(t * D, D)], mean[:, bass.ds(t, 1)], rstd[:, bass.ds(t, 1)],
                                    ALU.subtract, ALU.mult).then_inc(S["xn_ready"][par], 1)

                def keep(t, par):
                    e.wait_ge(S["pkv_ready"][par], 1)
                    e.sem_inc(S["pkv_ready"][par], -1)
                    k = KS[:, bass.ds(t * D, D)]
                    v.tensor_tensor(out=k, in0=pkv[par][:P, 0:D], in1=bkv[:, 0:D], op=ALU.add).then_inc(ch, 1)
                    e.wait_ge(ch, c.next())
                    v.tensor_tensor(out=VS[:, bass.ds(t * VW, D)], in0=pkv[par][:P, D:2 * D], in1=bkv[:, D:2 * D], op=ALU.add).then_inc(S["pkv_free"][par], 1)
                    v.tensor_tensor(out=kmax[:, :], in0=kmax[:, :], in1=k, op=ALU.max).then_inc(ch, 1)
                    e.wait_ge(ch, c.next())
                    c.reset()
                norm(0, 0)
                norm(1, 1)
                with e.Fori(0, T // 2 - 1) as i:
                    for par in range(2):
                        norm(i * 2 + par + 2, par)
                        keep(i * 2 + par, par)
                keep(T - 2, 0)
                keep(T - 1, 1)

            @block.scalar
            def _(e):
                a = nc.scalar

                def transposed(par):
                    e.wait_ge(pT_ready, 1)
                    e.sem_inc(pT_ready, -1)
                    e.sem_inc(S["xn_free"][par], 1)
                    a.activation(xT[:, par, :], pT[:, 0:2 * P], ACT.Copy).then_inc(xT_ready, 1)

                def body(t, par, last=False):
                    if not last:
                        transposed(1 - par)
                    e.wait_ge(pz_ready, 1)
                    e.sem_inc(pz_ready, -1)
                    e.wait_ge(S["zr_free"][par], 1)
                    e.sem_inc(S["zr_free"][par], -1)
                    a.activation(zr[:, par, :], pz[:P, 0:ZW + HEADS], ACT.Copy).then_inc(S["zr_ready"][par], 1)
                    a.activation(edn[:, bass.ds(t * HEADS, HEADS)], pz[:P, ZW:ZW + HEADS], ACT.Copy).then_inc(pz_free, 1)
                    e.drain().then_inc(row_ready, 1)
                    e.wait_ge(S["pq_ready"][par], 1)
                    e.sem_inc(S["pq_ready"][par], -1)
                    e.wait_ge(S["q_free"][par], 1)
                    e.sem_inc(S["q_free"][par], -1)
                    a.activation(qs[:, par, 0:P], pq[par][:, 0:P], ACT.Identity, bias=bq[:, 0:1])
                    a.activation(qs[:, par, P:2 * P], pq[par][:, P:2 * P], ACT.Identity, bias=bq[:, 1:2]).then_inc(S["pq_free"][par], 1)
                    e.drain().then_inc(S["q_ready"][par], 1)
                for par in range(2):
                    e.sem_inc(S["zr_free"][par], 1)
                    e.sem_inc(S["q_free"][par], 1)
                transposed(0)
                with e.Fori(0, T // 2 - 1) as i:
                    body(i * 2, 0)
                    body(i * 2 + 1, 1)
                body(T - 2, 0)
                body(T - 1, 1, last=True)
                e.drain().then_inc(ed_done, 1)

            @block.gpsimd
            def _(e):
                scatter_edge_inputs(e, ed, edn, edge_ed, row_ready, scattered)

            @block.sync
            def _(e):
                def store(t, par):
                    e.wait_ge(S["zr_ready"][par], 1)
                    e.sem_inc(S["zr_ready"][par], -1)
                    e.dma_start(zt_v[:, bass.ds(t * ZW, ZW)], zr[:, par, 0:ZW]).then_inc(S["zr_stored"][par], 16)
                    e.wait_ge(S["q_ready"][par], 1)
                    e.sem_inc(S["q_ready"][par], -1)
                    e.dma_start(q_dram[bass.ds(t * 128, 128), :], qs[:, par, :]).then_inc(S["q_stored"][par], 16)

                def stored(par):
                    e.wait_ge(S["zr_stored"][par], 16)
                    e.sem_inc(S["zr_stored"][par], -16)
                    e.sem_inc(S["zr_free"][par], 1)
                    e.wait_ge(S["q_stored"][par], 16)
                    e.sem_inc(S["q_stored"][par], -16)
                    e.sem_inc(S["q_free"][par], 1)
                store(0, 0)
                store(1, 1)
                stored(0)
                with e.Fori(0, T // 2 - 1) as i:
                    store(i * 2 + 2, 0)
                    stored(1)
                    store(i * 2 + 3, 1)
                    stored(0)
                stored(1)
                e.wait_ge(ed_done, 1)
                e.sem_inc(ed_done, -1)
                e.dma_start(edt.rearrange("(p t) w -> p (t w)", t=T), edn[:, :]).then_inc(edst, 16)
                e.wait_ge(edst, 16)
                e.sem_inc(edst, -16)

            @block.tensor
            def _(e):
                t_ = nc.tensor
                e.sem_inc(pz_free, 1)
                for par in range(2):
                    e.sem_inc(S["pkv_free"][par], 1)
                    e.sem_inc(S["pq_free"][par], 1)

                def transposes(par):
                    e.wait_ge(S["xn_ready"][par], 1)
                    e.sem_inc(S["xn_ready"][par], -1)
                    for b in range(2):
                        ins = t_.transpose(pT[:, b * P:(b + 1) * P], xn[:, par, b * 128:(b + 1) * 128], const.ident[:P, :P])
                    ins.then_inc(pT_ready, 1)

                def body(par, last=False):
                    e.wait_ge(xT_ready, 1)
                    e.sem_inc(xT_ready, -1)
                    if not last:
                        transposes(1 - par)
                    e.wait_ge(pz_free, 1)
                    e.sem_inc(pz_free, -1)
                    for b in range(2):
                        ins = t_.matmul(pz[:P, 0:ZW + HEADS], xT[:, par, b * P:(b + 1) * P], wz[:, b, :], start=b == 0, stop=b == 1)
                    ins.then_inc(pz_ready, 1)
                    e.wait_ge(S["pkv_free"][par], 1)
                    e.sem_inc(S["pkv_free"][par], -1)
                    for n, w in enumerate((wqk[:, :, D:2 * D], wv[:, :, :])):
                        for b in range(2):
                            ins = t_.matmul(pkv[par][:P, n * D:(n + 1) * D], xT[:, par, b * P:(b + 1) * P], w[:, b, :], start=b == 0, stop=b == 1)
                    ins.then_inc(S["pkv_ready"][par], 1)
                    e.wait_ge(S["pq_free"][par], 1)
                    e.sem_inc(S["pq_free"][par], -1)
                    for o in range(2):
                        for b in range(2):
                            ins = t_.matmul(pq[par][:, o * P:(o + 1) * P], wqk[:, b, o * 128:(o + 1) * 128], xT[:, par, b * P:(b + 1) * P], start=b == 0, stop=b == 1)
                    ins.then_inc(S["pq_ready"][par], 1)
                transposes(0)
                with e.Fori(0, T // 2 - 1) as i:
                    body(0)
                    body(1)
                body(0)
                body(1, last=True)


def attend1(nc, const, KS, VS, kmax, gbeta, bn):
    with Mem(nc, "a1") as m:
        mT = m.sb("mT", [128, 2])
        dg = m.sb("dg", [128, 2, 128])
        mb = m.sb("mb", [P, D])
        kd = m.sb("kd", [P, 2, D])
        ke = m.sb("ke", [P, 2, D])
        lam = m.sb("lam", [128, 2, D])
        st = m.sb("st", [128, 2, 6])
        ag = m.sb("ag", [128, 2, 2])
        rs = m.sb("rs", [128, 2, 3])
        pm = m.ps("pm")
        pb = m.ps("pb")
        pl = [m.ps("pl0"), m.ps("pl1")]
        ch, mt_ready, dg_ready, mb_ready, lam_ready, var_ready, sd_ready = (m.sem(x) for x in ("ch", "mt_ready", "dg_ready", "mb_ready", "lam_ready", "var_ready", "sd_ready"))
        S = {n: [m.sem(n + "0"), m.sem(n + "1")] for n in ("kd_ready", "kd_free", "ke_ready", "ke_free")}
        with nc.Block() as block:

            @block.tensor
            def _(e):
                t = nc.tensor
                for b in range(2):
                    ins = t.transpose(pm[:, b * P:(b + 1) * P], kmax[:, b * 128:(b + 1) * 128], const.ident[:P, :P])
                ins.then_inc(mt_ready, 1)
                e.wait_ge(dg_ready, 1)
                e.sem_inc(dg_ready, -1)
                for b in range(2):
                    ins = t.matmul(pb[:P, b * 128:(b + 1) * 128], const.ones[:, 0:P], dg[:, b, :], start=True, stop=True)
                ins.then_inc(mb_ready, 1)

                def body(t_, par, first=False, last=False):
                    e.wait_ge(S["ke_ready"][par], 1)
                    e.sem_inc(S["ke_ready"][par], -1)
                    for b in range(2):
                        ins = t.matmul(pl[b][:, 0:VW], ke[:, par, b * 128:(b + 1) * 128], VS[:, bass.ds(t_ * VW, VW)], start=first, stop=last)
                    ins.then_inc(lam_ready if last else S["ke_free"][par], 1)
                body(0, 0, first=True)
                with e.Fori(0, T // 2 - 1) as i:
                    body(i * 2 + 1, 1)
                    body(i * 2 + 2, 0)
                body(T - 1, 1, last=True)

            @block.scalar
            def _(e):
                e.sem_inc(S["ke_free"][0], 1)
                e.sem_inc(S["ke_free"][1], 1)

                def body(t, par):
                    e.wait_ge(S["kd_ready"][par], 1)
                    e.sem_inc(S["kd_ready"][par], -1)
                    e.wait_ge(S["ke_free"][par], 1)
                    e.sem_inc(S["ke_free"][par], -1)
                    nc.scalar.activation(ke[:, par, :], kd[:, par, :], ACT.Exp).then_inc(S["ke_ready"][par], 1)
                    e.drain().then_inc(S["kd_free"][par], 1)
                steps(e, T, body)
                e.wait_ge(var_ready, 1)
                e.sem_inc(var_ready, -1)
                nc.scalar.activation(rs[:, :, 1], rs[:, :, 0], ACT.Sqrt).then_inc(sd_ready, 1)

            @block.vector
            def _(e):
                v = nc.vector
                c = Count(e, ch)
                e.wait_ge(mt_ready, 1)
                e.sem_inc(mt_ready, -1)
                v.tensor_reduce(out=mT[:, :], in_=pm[:, 0:2 * P].rearrange("p (b n) -> p b n", b=2), axis=AX.X, op=ALU.max).then_inc(ch, 1)
                e.wait_ge(ch, c.next())
                for b in range(2):
                    v.tensor_scalar(dg[:, b, :], const.ident[:, :], mT[:, b:b + 1], None, ALU.mult).then_inc(ch, 1)
                    e.wait_ge(ch, c.next())
                e.sem_inc(dg_ready, 1)
                e.wait_ge(mb_ready, 1)
                e.sem_inc(mb_ready, -1)
                v.tensor_copy(mb[:, :], pb[:P, 0:D]).then_inc(ch, 1)
                e.wait_ge(ch, c.next())
                for par in range(2):
                    e.sem_inc(S["kd_free"][par], 1)

                def body(t, par):
                    e.wait_ge(S["kd_free"][par], 1)
                    e.sem_inc(S["kd_free"][par], -1)
                    v.tensor_tensor(out=kd[:, par, :], in0=KS[:, bass.ds(t * D, D)], in1=mb[:, :], op=ALU.subtract).then_inc(S["kd_ready"][par], 1)
                steps(e, T, body)
                e.wait_ge(lam_ready, 1)
                e.sem_inc(lam_ready, -1)
                for b in range(2):
                    v.reciprocal(rs[:, b, 2:3], pl[b][:, D:VW]).then_inc(ch, 1)
                    e.wait_ge(ch, c.next())
                    v.tensor_scalar(lam[:, b, :], pl[b][:, 0:D], rs[:, b, 2:3], None, ALU.mult).then_inc(ch, 1)
                    e.wait_ge(ch, c.next())
                    v.bn_stats(out=st[:, b, :], in_=lam[:, b, :]).then_inc(ch, 1)
                    e.wait_ge(ch, c.next())
                    v.bn_aggr(out=ag[:, b, :], in_=st[:, b, :]).then_inc(ch, 1)
                    e.wait_ge(ch, c.next())
                    v.tensor_scalar(rs[:, b, 0:1], ag[:, b, 1:2], 1e-5, None, ALU.add).then_inc(ch, 1)
                    e.wait_ge(ch, c.next())
                e.sem_inc(var_ready, 1)
                e.wait_ge(sd_ready, 1)
                e.sem_inc(sd_ready, -1)
                for b in range(2):
                    v.reciprocal(rs[:, b, 2:3], rs[:, b, 1:2]).then_inc(ch, 1)
                    e.wait_ge(ch, c.next())
                    v.tensor_scalar(lam[:, b, :], lam[:, b, :], ag[:, b, 0:1], rs[:, b, 2:3], ALU.subtract, ALU.mult).then_inc(ch, 1)
                    e.wait_ge(ch, c.next())
                    v.tensor_scalar(bn[:, b, :], lam[:, b, :], gbeta[:, b:b + 1], gbeta[:, 2 + b:3 + b], ALU.mult, ALU.add).then_inc(ch, 1)
                    e.wait_ge(ch, c.next())
                c.reset()


def query1(nc, X, bn, q_dram):
    with Mem(nc, "q1") as m:
        qs = m.sb("qs", [128, 2, 2 * P])
        po = [m.ps("po0"), m.ps("po1")]
        S = {n: [m.sem(n + "0"), m.sem(n + "1")] for n in ("q_ld", "q_free", "po_ready", "po_free")}
        with nc.Block() as block:

            @block.sync
            def _(e):
                for b in range(2):
                    e.sem_inc(S["q_free"][b], 1)

                def body(t, par):
                    e.wait_ge(S["q_free"][par], 1)
                    e.sem_inc(S["q_free"][par], -1)
                    e.dma_start(qs[:, par, :], q_dram[bass.ds(t * 128, 128), :]).then_inc(S["q_ld"][par], 16)
                steps(e, T, body)

            @block.tensor
            def _(e):
                for b in range(2):
                    e.sem_inc(S["po_free"][b], 1)

                def body(t, par):
                    e.wait_ge(S["q_ld"][par], 16)
                    e.sem_inc(S["q_ld"][par], -16)
                    e.wait_ge(S["po_free"][par], 1)
                    e.sem_inc(S["po_free"][par], -1)
                    for b in range(2):
                        ins = nc.tensor.matmul(po[par][:P, 0:D], qs[:, par, b * P:(b + 1) * P], bn[:, b, :], start=b == 0, stop=b == 1)
                    ins.then_inc(S["po_ready"][par], 1)
                steps(e, T, body)

            @block.vector
            def _(e):
                def body(t, par):
                    e.wait_ge(S["po_ready"][par], 1)
                    e.sem_inc(S["po_ready"][par], -1)
                    e.sem_inc(S["q_free"][par], 1)
                    xt = X[:, bass.ds(t * D, D)]
                    nc.vector.tensor_tensor(out=xt, in0=xt, in1=po[par][:P, 0:D], op=ALU.add).then_inc(S["po_free"][par], 1)
                steps(e, T, body)


def route1(nc, const, X, mean, rstd, XN, a, w1, w2, b1, b2):
    NF = F1 // 128
    with Mem(nc, "r1") as m:
        wr = m.sb("wr", [128, 2, NE])
        br = m.sb("br", [1, NE])
        mrow = m.sb("mrow", [1, D])
        mT = m.sb("mT", [128, 2])
        r = m.sb("r", [1, 8, NE])
        sc = m.sb("sc", [1, 16])
        ids = m.sb("ids", [1, 2], I32)
        wb = m.sb("wb", [128, 2])
        b2s = m.sb("b2s", [P, 2, D])
        pmn = m.ps("pmn")
        pt = m.ps("pt")
        pl = m.ps("pl")
        names = ("ch", "ld", "xn_ready", "sum_ready", "row_ready", "mt_ready", "mts_ready", "lg_ready", "x1", "e1", "x2", "e2", "x3", "e3", "ids_ready", "w_ready", "wb_ready", "wld")
        s = {n: m.sem(n) for n in names}
        with nc.Block() as block:

            @block.sync
            def _(e):
                e.dma_start(wr[:, :, :], a["L1_ffn_Wr"].rearrange("(b i) x -> i b x", b=2)).then_inc(s["ld"], 16)
                e.dma_start(br[:, :], a["L1_ffn_br"].rearrange("(o x) -> o x", o=1)).then_inc(s["ld"], 16)
                e.wait_ge(s["ids_ready"], 1)
                e.sem_inc(s["ids_ready"], -1)
                for n in range(2):
                    i = nc.sync.value_load(ids[0:1, n:n + 1], min_val=0, max_val=NE - 1)
                    e.dma_start(w1[:, n, :, :], a["L1_ffn_W1"].rearrange("x d f -> (x d) f")[bass.ds(i * D, D), :].rearrange("(b i) f -> i b f", b=2)).then_inc(s["wld"], 16)
                    e.dma_start(w2[:, n, :, :], a["L1_ffn_W2"].rearrange("x f d -> (x f) d")[bass.ds(i * F1, F1), :].rearrange("(g f) d -> f g d", f=128)).then_inc(s["wld"], 16)
                    e.dma_start(b1[:, n, :], a["ffn1_b1"][bass.ds(i * 128, 128), :]).then_inc(s["wld"], 16)
                    e.dma_start(b2s[:, n, :], a["ffn1_b2"][bass.ds(i, 1), :].to_broadcast([P, D])).then_inc(s["wld"], 16)

            @block.tensor
            def _(e):
                t = nc.tensor
                e.wait_ge(s["xn_ready"], 1)
                e.sem_inc(s["xn_ready"], -1)
                t.matmul(pmn[0:1, 0:D], const.ones[:P, 0:1], XN[:, 0:D], start=True, stop=False)
                with e.Fori(0, (T - 2) // 8) as i:
                    for k in range(8):
                        t.matmul(pmn[0:1, 0:D], const.ones[:P, 0:1], XN[:, bass.ds(i * (8 * D) + (k + 1) * D, D)], start=False, stop=False)
                t.matmul(pmn[0:1, 0:D], const.ones[:P, 0:1], XN[:, (T - 1) * D:T * D], start=False, stop=True).then_inc(s["sum_ready"], 1)
                e.wait_ge(s["row_ready"], 1)
                e.sem_inc(s["row_ready"], -1)
                for b in range(2):
                    ins = t.matmul(pt[:, b:b + 1], mrow[0:1, b * 128:(b + 1) * 128], const.ones[0:1, 0:1], start=True, stop=True)
                ins.then_inc(s["mt_ready"], 1)
                e.wait_ge(s["mts_ready"], 1)
                e.sem_inc(s["mts_ready"], -1)
                for b in range(2):
                    ins = t.matmul(pl[0:1, 0:NE], mT[:, b:b + 1], wr[:, b, :], start=b == 0, stop=b == 1)
                ins.then_inc(s["lg_ready"], 1)
                e.wait_ge(s["w_ready"], 1)
                e.sem_inc(s["w_ready"], -1)
                t.matmul(pt[:, 2:4], const.ones[0:1, 0:128], sc[0:1, 8:10], start=True, stop=True).then_inc(s["wb_ready"], 1)

            @block.scalar
            def _(e):
                A = nc.scalar
                e.wait_ge(s["x1"], 1)
                e.sem_inc(s["x1"], -1)
                A.activation(r[:, 1, :], r[:, 0, :], ACT.Exp).then_inc(s["e1"], 1)
                e.wait_ge(s["x2"], 1)
                e.sem_inc(s["x2"], -1)
                A.activation(r[:, 1, :], r[:, 0, :], ACT.Exp).then_inc(s["e2"], 1)
                e.wait_ge(s["x3"], 1)
                e.sem_inc(s["x3"], -1)
                A.activation(sc[:, 5:6], sc[:, 4:5], ACT.Exp).then_inc(s["e3"], 1)

            @block.vector
            def _(e):
                v = nc.vector
                c = Count(e, s["ch"])
                with e.Fori(0, T // 10) as i:
                    for k in range(10):
                        t = i * 10 + k
                        v.tensor_scalar(XN[:, bass.ds(t * D, D)], X[:, bass.ds(t * D, D)], mean[:, bass.ds(t, 1)], rstd[:, bass.ds(t, 1)], ALU.subtract, ALU.mult)
                v.memset(sc[:, :], 0.0).then_inc(s["ch"], 1)
                e.wait_ge(s["ch"], c.next())
                e.sem_inc(s["xn_ready"], 1)
                e.wait_ge(s["sum_ready"], 1)
                e.sem_inc(s["sum_ready"], -1)
                v.tensor_scalar(mrow[:, :], pmn[0:1, 0:D], 1.0 / N, None, ALU.mult).then_inc(s["ch"], 1)
                e.wait_ge(s["ch"], c.next())
                e.sem_inc(s["row_ready"], 1)
                e.wait_ge(s["mt_ready"], 1)
                e.sem_inc(s["mt_ready"], -1)
                v.tensor_copy(mT[:, :], pt[:, 0:2]).then_inc(s["ch"], 1)
                e.wait_ge(s["ch"], c.next())
                e.wait_ge(s["ld"], 32)
                e.sem_inc(s["ld"], -32)
                e.sem_inc(s["mts_ready"], 1)
                e.wait_ge(s["lg_ready"], 1)
                e.sem_inc(s["lg_ready"], -1)
                v.tensor_tensor(out=r[:, 0, :], in0=pl[0:1, 0:NE], in1=br[:, :], op=ALU.add).then_inc(s["ch"], 1)
                e.wait_ge(s["ch"], c.next())

                def softmax(x, done):
                    v.tensor_reduce(out=sc[:, 0:1], in_=r[:, 0, :], axis=AX.X, op=ALU.max).then_inc(s["ch"], 1)
                    e.wait_ge(s["ch"], c.next())
                    v.tensor_scalar(r[:, 0, :], r[:, 0, :], sc[:, 0:1], None, ALU.subtract).then_inc(s["ch"], 1)
                    e.wait_ge(s["ch"], c.next())
                    e.sem_inc(x, 1)
                    e.wait_ge(done, 1)
                    e.sem_inc(done, -1)
                    v.tensor_reduce(out=sc[:, 1:2], in_=r[:, 1, :], axis=AX.X, op=ALU.add).then_inc(s["ch"], 1)
                    e.wait_ge(s["ch"], c.next())
                    v.reciprocal(sc[:, 1:2], sc[:, 1:2]).then_inc(s["ch"], 1)
                    e.wait_ge(s["ch"], c.next())
                    v.tensor_scalar(r[:, 2, :], r[:, 1, :], sc[:, 1:2], None, ALU.mult).then_inc(s["ch"], 1)
                    e.wait_ge(s["ch"], c.next())
                softmax(s["x1"], s["e1"])
                v.tensor_scalar(r[:, 3, :], r[:, 2, :], float(N), None, ALU.mult).then_inc(s["ch"], 1)
                e.wait_ge(s["ch"], c.next())
                v.tensor_scalar(r[:, 5, :], r[:, 3, :], float(CAP0), None, ALU.is_gt).then_inc(s["ch"], 1)
                e.wait_ge(s["ch"], c.next())
                v.tensor_scalar(r[:, 3, :], r[:, 3, :], float(CAP0), None, ALU.max).then_inc(s["ch"], 1)
                e.wait_ge(s["ch"], c.next())
                v.reciprocal(r[:, 4, :], r[:, 3, :]).then_inc(s["ch"], 1)
                e.wait_ge(s["ch"], c.next())
                v.tensor_scalar(r[:, 4, :], r[:, 4, :], float(CAP0), -1.0, ALU.mult, ALU.add).then_inc(s["ch"], 1)
                e.wait_ge(s["ch"], c.next())
                v.tensor_tensor(out=r[:, 4, :], in0=r[:, 4, :], in1=r[:, 5, :], op=ALU.mult).then_inc(s["ch"], 1)
                e.wait_ge(s["ch"], c.next())
                v.tensor_scalar(r[:, 4, :], r[:, 4, :], 1.0, None, ALU.add).then_inc(s["ch"], 1)
                e.wait_ge(s["ch"], c.next())
                v.tensor_tensor(out=r[:, 0, :], in0=r[:, 2, :], in1=r[:, 4, :], op=ALU.mult).then_inc(s["ch"], 1)
                e.wait_ge(s["ch"], c.next())
                softmax(s["x2"], s["e2"])
                for n in range(2):
                    v.tensor_reduce(out=sc[:, 2 + n:3 + n], in_=r[:, 2, :], axis=AX.X, op=ALU.max).then_inc(s["ch"], 1)
                    e.wait_ge(s["ch"], c.next())
                    v.tensor_scalar(r[:, 3, :], r[:, 2, :], sc[:, 2 + n:3 + n], None, ALU.is_equal).then_inc(s["ch"], 1)
                    e.wait_ge(s["ch"], c.next())
                    v.tensor_scalar(r[:, 3, :], r[:, 3, :], -float(NE), float(NE), ALU.mult, ALU.add).then_inc(s["ch"], 1)
                    e.wait_ge(s["ch"], c.next())
                    v.tensor_tensor(out=r[:, 3, :], in0=r[:, 3, :], in1=const.iota[0:1, 0:NE], op=ALU.add).then_inc(s["ch"], 1)
                    e.wait_ge(s["ch"], c.next())
                    v.tensor_reduce(out=sc[:, 6 + n:7 + n], in_=r[:, 3, :], axis=AX.X, op=ALU.min).then_inc(s["ch"], 1)
                    e.wait_ge(s["ch"], c.next())
                    if n == 0:
                        v.tensor_scalar(r[:, 3, :], const.iota[0:1, 0:NE], sc[:, 6:7], None, ALU.is_equal).then_inc(s["ch"], 1)
                        e.wait_ge(s["ch"], c.next())
                        v.scalar_tensor_tensor(r[:, 2, :], r[:, 3, :], -2.0, r[:, 2, :], ALU.mult, ALU.add).then_inc(s["ch"], 1)
                        e.wait_ge(s["ch"], c.next())
                v.tensor_copy(ids[:, :], sc[:, 6:8]).then_inc(s["ch"], 1)
                e.wait_ge(s["ch"], c.next())
                e.sem_inc(s["ids_ready"], 1)
                v.tensor_tensor(out=sc[:, 4:5], in0=sc[:, 3:4], in1=sc[:, 2:3], op=ALU.subtract).then_inc(s["ch"], 1)
                e.wait_ge(s["ch"], c.next())
                e.sem_inc(s["x3"], 1)
                e.wait_ge(s["e3"], 1)
                e.sem_inc(s["e3"], -1)
                v.tensor_scalar(sc[:, 10:11], sc[:, 5:6], 1.0, None, ALU.add).then_inc(s["ch"], 1)
                e.wait_ge(s["ch"], c.next())
                v.reciprocal(sc[:, 8:9], sc[:, 10:11]).then_inc(s["ch"], 1)
                e.wait_ge(s["ch"], c.next())
                v.tensor_tensor(out=sc[:, 9:10], in0=sc[:, 5:6], in1=sc[:, 8:9], op=ALU.mult).then_inc(s["ch"], 1)
                e.wait_ge(s["ch"], c.next())
                e.sem_inc(s["w_ready"], 1)
                e.wait_ge(s["wb_ready"], 1)
                e.sem_inc(s["wb_ready"], -1)
                v.tensor_copy(wb[:, :], pt[:, 2:4]).then_inc(s["ch"], 1)
                e.wait_ge(s["ch"], c.next())
                e.wait_ge(s["wld"], 128)
                e.sem_inc(s["wld"], -128)
                for n in range(2):
                    v.tensor_scalar(w2[:, n, :, :], w2[:, n, :, :], wb[:, n:n + 1], None, ALU.mult).then_inc(s["ch"], 1)
                    e.wait_ge(s["ch"], c.next())
                    v.tensor_scalar(b2s[:, n, :], b2s[:, n, :], wb[:P, n:n + 1], None, ALU.mult).then_inc(s["ch"], 1)
                    e.wait_ge(s["ch"], c.next())
                v.tensor_tensor(out=b2[:, :], in0=b2s[:, 0, :], in1=b2s[:, 1, :], op=ALU.add).then_inc(s["ch"], 1)
                e.wait_ge(s["ch"], c.next())
                c.reset()


def ffn1(nc, const, X, XN, w1, w2, b1, b2, a, out):
    NF = F1 // 128
    with Mem(nc, "x1") as m:
        gb = m.sb("gb", [P, 2, D])
        xs = m.sb("xs", [P, 4 * D])
        xT = m.sb("xT", [128, 2, 4 * P])
        hT = m.sb("hT", [128, 2 * NF, 4 * P])
        u = m.sb("u", [P, 4, D])
        o = m.sb("o", [P, 2, 4 * D])
        half = m.sb("half", [P, 4])
        stat = m.sb("stat", [P, 4, 6])
        ms = m.sb("ms", [P, 4, 3])
        pT = [m.ps("pT0"), m.ps("pT1")]
        ph = [m.ps(f"ph{i}") for i in range(3)]
        py = [m.ps("py0"), m.ps("py1")]
        names = ("ch", "ld", "xs_ready", "xs_free", "xT_ready", "norm_ready", "norm_done", "g")
        s = {n: m.sem(n) for n in names}
        S = {n: [m.sem(n + "0"), m.sem(n + "1")] for n in ("pT_ready", "py_ready", "py_free", "o_ready", "o_free", "o_st")}
        ph_ready, ph_free = [m.sem(f"ph_ready{i}") for i in range(3)], [m.sem(f"ph_free{i}") for i in range(3)]
        out_v = out.rearrange("(p t) d -> p (t d)", t=T)
        full, rest = T // 4, T % 4

        def tile_steps(e, body):
            steps(e, full, lambda i, par: body(i * 4, par, 4))
            body(full * 4, full % 2, rest)
        with nc.Block() as block:

            @block.sync
            def _(e):
                for n, name in enumerate(("L1_ffn_gamma", "L1_ffn_beta")):
                    e.dma_start(gb[:, n, :], a[name].partition_broadcast(P)).then_inc(s["ld"], 16)
                e.wait_ge(s["ld"], 32)
                e.sem_inc(s["ld"], -32)
        with nc.Block() as block:

            @block.gpsimd
            def _(e):
                g = nc.gpsimd
                g.memset(half[:, :], -0.5).then_inc(s["g"], 1)
                e.wait_ge(s["g"], 1)
                e.sem_inc(s["g"], -1)

                def rows(t, n):
                    e.wait_ge(s["xs_free"], 1)
                    e.sem_inc(s["xs_free"], -1)
                    g.tensor_copy(xs[:, 0:n * D], XN[:, bass.ds(t * D, n * D)]).then_inc(s["xs_ready"], 1)

                def deviation():
                    e.wait_ge(s["norm_ready"], 1)
                    e.sem_inc(s["norm_ready"], -1)
                    g.tensor_scalar(ms[:, :, 1], ms[:, :, 1], 1e-5, None, ALU.add).then_inc(s["g"], 1)
                    e.wait_ge(s["g"], 1)
                    e.sem_inc(s["g"], -1)
                    g.tensor_tensor(out=ms[:, :, 2], in0=ms[:, :, 1], in1=half[:, :], op=ALU.pow).then_inc(s["norm_done"], 1)
                rows(0, 4)
                with e.Fori(0, full - 1) as i:
                    rows(i * 4 + 4, 4)
                    deviation()
                rows(full * 4, rest)
                deviation()
                deviation()

            @block.tensor
            def _(e):
                t_ = nc.tensor
                for q in S["py_free"] + ph_free:
                    e.sem_inc(q, 1)
                e.sem_inc(s["xs_free"], 1)

                def transposes(n):
                    e.wait_ge(s["xs_ready"], 1)
                    e.sem_inc(s["xs_ready"], -1)
                    for b in range(2):
                        for q in range(n):
                            ins = t_.transpose(pT[b][:, q * P:(q + 1) * P], xs[:, q * D + b * 128:q * D + b * 128 + 128], const.ident[:P, :P])
                        ins.then_inc(S["pT_ready"][b], 1)

                def body(n, after, first=False):
                    e.wait_ge(s["xT_ready"], 2)
                    e.sem_inc(s["xT_ready"], -(2))
                    e.sem_inc(s["xs_free"], 1)
                    for f in range(2 * NF):
                        if f >= 3 or first:
                            e.wait_ge(ph_free[f % 3], 1)
                            e.sem_inc(ph_free[f % 3], -1)
                        x, g = f // NF, f % NF
                        for b in range(2):
                            ins = t_.matmul(ph[f % 3][:, 0:n * P], w1[:, x, b, g * 128:(g + 1) * 128], xT[:, b, 0:n * P], start=b == 0, stop=b == 1)
                        ins.then_inc(ph_ready[f % 3], 1)
                    if after:
                        transposes(after)
                    for q in range(n):
                        e.wait_ge(S["py_free"][q % 2], 1)
                        e.sem_inc(S["py_free"][q % 2], -1)
                        for f in range(2 * NF):
                            if q == 0 and f >= 2 * NF - 3:
                                e.wait_ge(ph_free[f % 3], 1)
                                e.sem_inc(ph_free[f % 3], -1)
                            ins = t_.matmul(py[q % 2][:P, 0:D], hT[:, f, q * P:(q + 1) * P], w2[:, f // NF, f % NF, :], start=f == 0, stop=f == 2 * NF - 1)
                        ins.then_inc(S["py_ready"][q % 2], 1)
                transposes(4)
                body(4, 4, first=True)
                with e.Fori(0, full - 2) as i:
                    body(4, 4)
                body(4, rest)
                body(rest, 0)

            @block.scalar
            def _(e):
                A = nc.scalar

                def transposed(n):
                    for b in range(2):
                        e.wait_ge(S["pT_ready"][b], 1)
                        e.sem_inc(S["pT_ready"][b], -1)
                        A.activation(xT[:, b, 0:n * P], pT[b][:, 0:n * P], ACT.Copy).then_inc(s["xT_ready"], 1)

                def body(n, after):
                    for f in range(2 * NF):
                        e.wait_ge(ph_ready[f % 3], 1)
                        e.sem_inc(ph_ready[f % 3], -1)
                        A.activation(hT[:, f, 0:n * P], ph[f % 3][:, 0:n * P], ACT.Gelu, bias=b1[:, f // NF, f % NF:f % NF + 1]).then_inc(ph_free[f % 3], 1)
                    if after:
                        transposed(after)
                transposed(4)
                with e.Fori(0, full - 1) as i:
                    body(4, 4)
                body(4, rest)
                body(rest, 0)

            @block.vector
            def _(e):
                v = nc.vector
                c = Count(e, s["ch"])
                for b in range(2):
                    e.sem_inc(S["o_free"][b], 1)
                v.memset(ms[:, :, :], 1.0).then_inc(s["ch"], 1)
                e.wait_ge(s["ch"], c.next())

                def body(t, par, n):
                    v.tensor_tensor(out=u[:, 0:n, :], in0=XN[:, bass.ds(t * D, n * D)].rearrange("p (k w) -> p k w", w=D),
                                    in1=b2[:, :].unsqueeze(1).to_broadcast([P, n, D]), op=ALU.add).then_inc(s["ch"], 1)
                    e.wait_ge(s["ch"], c.next())
                    for q in range(n):
                        e.wait_ge(S["py_ready"][q % 2], 1)
                        e.sem_inc(S["py_ready"][q % 2], -1)
                        v.tensor_tensor(out=u[:, q, :], in0=py[q % 2][:P, 0:D], in1=u[:, q, :], op=ALU.add).then_inc(s["ch"], 1)
                        e.wait_ge(s["ch"], c.next())
                        e.sem_inc(S["py_free"][q % 2], 1)
                        v.bn_stats(out=stat[:, q, :], in_=u[:, q, :]).then_inc(s["ch"], 1)
                        e.wait_ge(s["ch"], c.next())
                        v.bn_aggr(out=ms[:, q, 0:2], in_=stat[:, q, :]).then_inc(s["ch"], 1)
                        e.wait_ge(s["ch"], c.next())
                    e.sem_inc(s["norm_ready"], 1)
                    e.wait_ge(s["norm_done"], 1)
                    e.sem_inc(s["norm_done"], -1)
                    for q in range(n):
                        v.tensor_scalar(u[:, q, :], u[:, q, :], ms[:, q, 0:1], ms[:, q, 2:3], ALU.subtract, ALU.mult)
                    v.memset(stat[:, :, :], 0.0).then_inc(s["ch"], 1)
                    e.wait_ge(s["ch"], c.next())
                    v.tensor_tensor(out=u[:, 0:n, :], in0=u[:, 0:n, :], in1=gb[:, 0, :].unsqueeze(1).to_broadcast([P, n, D]), op=ALU.mult).then_inc(s["ch"], 1)
                    e.wait_ge(s["ch"], c.next())
                    v.tensor_tensor(out=u[:, 0:n, :], in0=u[:, 0:n, :], in1=gb[:, 1, :].unsqueeze(1).to_broadcast([P, n, D]), op=ALU.add).then_inc(s["ch"], 1)
                    e.wait_ge(s["ch"], c.next())
                    e.wait_ge(S["o_free"][par], 1)
                    e.sem_inc(S["o_free"][par], -1)
                    v.tensor_tensor(out=o[:, par, 0:n * D].rearrange("p (k w) -> p k w", w=D), in0=u[:, 0:n, :],
                                    in1=X[:, bass.ds(t * D, n * D)].rearrange("p (k w) -> p k w", w=D), op=ALU.add).then_inc(s["ch"], 1)
                    e.wait_ge(s["ch"], c.next())
                    e.sem_inc(S["o_ready"][par], 1)
                    c.reset()
                c.reset()
                tile_steps(e, body)

            @block.sync
            def _(e):
                def body(t, par, n):
                    e.wait_ge(S["o_ready"][par], 1)
                    e.sem_inc(S["o_ready"][par], -1)
                    e.dma_start(out_v[:, bass.ds(t * D, n * D)], o[:, par, 0:n * D]).then_inc(S["o_st"][par], 16)
                    e.wait_ge(S["o_st"][par], 16)
                    e.sem_inc(S["o_st"][par], -16)
                    e.sem_inc(S["o_free"][par], 1)
                tile_steps(e, body)


class Const:

    def __init__(self, m):
        self.all = m.sb("const", [128, 4 * 128 + CK])
        self.ident = self.all[:, 0:128]
        self.tri = self.all[:, 128:256]
        self.iota = self.all[:, 256:384]
        self.ones = self.all[:, 384:512]
        self.rowbase = self.all[:, 512:512 + CK]


def const_table():
    import numpy as np
    out = np.zeros((128, 4 * 128 + CK), np.float32)
    out[:, 0:128] = np.eye(128)
    out[:, 128:256] = np.triu(np.ones((128, 128)), 1)
    out[:, 256:384] = np.arange(128)[None, :]
    out[:, 384:512] = 1.0
    c = np.arange(CP)[:, None] * CK + np.arange(CK)[None, :]
    out[:CP, 512:] = (c // BC) * (P * BC) + c % BC
    return out


def network(nc, a, out):
    dram = lambda n, shape, dt=F32: nc.dram_tensor(n, list(shape), dt).ap()
    start_dram = dram("start_dram", [C, J])
    zt = dram("zt", [N, ZW])
    edt = dram("edt", [N, HEADS])
    edge_ed = dram("edge_ed", [E + BC * J, HEADS])
    sums = dram("sums", [NB * P * BC, GW])
    extras = dram("extras", [C, GW])
    bufx = dram("bufx", [NE * ER, D])
    bufy = dram("bufy", [NE * ER, D])
    q_dram = dram("q_dram", [T * 128, 2 * P])
    with Mem(nc, "g") as m:
        const = Const(m)
        ed = Edges(m)
        X = m.sb("X", [P, T * D])
        mean = m.sb("mean", [P, T])
        rstd = m.sb("rstd", [P, T])
        loaded = m.sem("loaded")
        with nc.Block() as block:
            @block.sync
            def _(e):
                e.dma_start(const.all[:, :], a["consts"][:, :]).then_inc(loaded, 16)
                e.dma_start(X[:, :], a["x"].rearrange("(p t) d -> p (t d)", t=T)).then_inc(loaded, 16)
                e.wait_ge(loaded, 32)
                e.sem_inc(loaded, -32)
        fill(nc, "fz", [bufx.rearrange("(p r w) d -> p r (w d)", p=125, r=16), edge_ed.rearrange("(p r w) h -> p r (w h)", p=120, r=5)])
        edge_tables(nc, ed, const, a["src"], a["dst"], start_dram)
        norm_stats(nc, "n0", X, mean, rstd, 1e-5)
        with Mem(nc, "l0") as l:
            edn = l.sb("edn", [P, T * HEADS])
            kv = l.sb("kv", [128, 2 * 132])
            with Mem(nc, "q") as mq:
                qT = mq.sb("qT", [128, T * 2 * P])
                wz = mq.sb("wz", [128, 2, ZW + HEADS])
                wkv = mq.sb("wkv", [128, 2, 2 * D])
                wq = mq.sb("wq", [128, 2, D])
                with nc.Block() as block:
                    @block.sync
                    def _(e):
                        w = a["mix_wqkv"].rearrange("(b i) o -> i b o", b=2)
                        e.dma_start(wq[:, :, :], w[:, :, 0:D]).then_inc(loaded, 16)
                        e.dma_start(wkv[:, :, :], w[:, :, D:3 * D]).then_inc(loaded, 16)
                        e.wait_ge(loaded, 32)
                        e.sem_inc(loaded, -32)
                gat_weights(nc, "gw0", a["gnn0_w_in"], a["gnn0_w_out"], a["gnn0_att"], wz)
                dense0(nc, const, ed, X, mean, rstd, wz, wkv, wq, zt, edt, edn, edge_ed, qT, kv)
                mix0(nc, const, X, mean, rstd, qT, kv, a)
            chunk_edge_inputs(nc, "gi0", ed, edt, edge_ed)
            gat_edges(nc, "ge0", const, ed, zt, edge_ed, sums, 0.01)
            gat_extras(nc, "gx0", const, ed, sums, extras)
            gat_merge(nc, "gm0", ed, X, sums, extras)
        with Mem(nc, "f0") as l:
            back_idx = l.sb("back_idx", [P, T], I32)
            wgt = l.sb("wgt", [P, T])
            norm_stats(nc, "n1", X, mean, rstd, 1e-5)
            with Mem(nc, "f0g") as g:
                XN = g.sb("XN", [P, T * D])
                slot_idx = g.sb("slot_idx", [P, T], I32)
                gw = g.sb("gw", [128, 2, NE])
                gb = g.sb("gb", [P, NE])
                with nc.Block() as block:
                    @block.sync
                    def _(e):
                        e.dma_start(gw[:, :, :], a["L0_ffn_gate_w"].rearrange("(b i) x -> i b x", b=2)).then_inc(loaded, 16)
                        e.dma_start(gb[:, :], a["L0_ffn_gate_b"].partition_broadcast(P)).then_inc(loaded, 16)
                        e.wait_ge(loaded, 32)
                        e.sem_inc(loaded, -32)
                moe_gate(nc, const, X, mean, rstd, XN, gw, gb, bufx, slot_idx, back_idx, wgt)
            moe_experts(nc, const, bufx, bufy, a["L0_ffn_w1"].rearrange("x d f -> (x d) f"), a["L0_ffn_w2"].rearrange("x f d -> (x f) d"),
                        a["ffn0_b1"], a["L0_ffn_b2"])
            moe_return(nc, X, bufy, back_idx, wgt)
        norm_stats(nc, "n2", X, mean, rstd, 1e-5)
        with Mem(nc, "l1") as l:
            edn = l.sb("edn", [P, T * HEADS])
            with Mem(nc, "l1m") as g:
                VS = g.sb("VS", [P, T * VW])
                KS = g.sb("KS", [P, T * D])
                wz = g.sb("wz", [128, 2, ZW + HEADS])
                wqk = g.sb("wqk", [128, 2, 2 * D])
                wv = g.sb("wv", [128, 2, D])
                bkv = g.sb("bkv", [P, 2 * D])
                bq = g.sb("bq", [128, 2])
                gbeta = g.sb("gbeta", [128, 4])
                kmax = g.sb("kmax", [P, D])
                bn = g.sb("bn", [128, 2, D])
                with nc.Block() as block:
                    @block.sync
                    def _(e):
                        w = a["L1_mix_W_qk"]
                        for n in range(2):
                            e.dma_start(wqk[:, :, n * D:(n + 1) * D], w[n, :, :].rearrange("(b i) o -> i b o", b=2)).then_inc(loaded, 16)
                        e.dma_start(wv[:, :, :], a["L1_mix_W_v"].rearrange("(b i) o -> i b o", b=2)).then_inc(loaded, 16)
                        e.dma_start(bkv[:, 0:D], a["L1_mix_b_qk"][1, :].partition_broadcast(P)).then_inc(loaded, 16)
                        e.dma_start(bkv[:, D:2 * D], a["L1_mix_b_v"].partition_broadcast(P)).then_inc(loaded, 16)
                        e.dma_start(bq[:, :], a["mix1_bq"]).then_inc(loaded, 16)
                        e.dma_start(gbeta[:, :], a["mix1_gbeta"]).then_inc(loaded, 16)
                        e.wait_ge(loaded, 112)
                        e.sem_inc(loaded, -112)
                gat_weights(nc, "gw1", a["L1_gnn_W"], a["gnn1_w_out"], a["gnn1_att"], wz)
                dense1(nc, const, ed, X, mean, rstd, wz, wqk, wv, bkv, bq, zt, edt, edn, edge_ed, KS, VS, kmax, q_dram)
                attend1(nc, const, KS, VS, kmax, gbeta, bn)
                query1(nc, X, bn, q_dram)
            chunk_edge_inputs(nc, "gi1", ed, edt, edge_ed)
            gat_edges(nc, "ge1", const, ed, zt, edge_ed, sums, 0.2)
            gat_extras(nc, "gx1", const, ed, sums, extras)
            gat_merge(nc, "gm1", ed, X, sums, extras, zt=zt, edn=edn, bias=a["L1_gnn_bias"], slope=0.2)
        norm_stats(nc, "n3", X, mean, rstd, 1e-5)
        with Mem(nc, "f1") as l:
            XN = l.sb("XN", [P, T * D])
            w1 = l.sb("w1", [128, 2, 2, F1])
            w2 = l.sb("w2", [128, 2, F1 // 128, D])
            b1 = l.sb("b1", [128, 2, F1 // 128])
            b2 = l.sb("b2", [P, D])
            route1(nc, const, X, mean, rstd, XN, a, w1, w2, b1, b2)
            ffn1(nc, const, X, XN, w1, w2, b1, b2, a, out)


def kernel(**inputs):
    import numpy as _np
    import concourse.bacc as _bacc
    from concourse.bass_utils import run_bass_kernel_spmd as _run

    nc = _bacc.Bacc("TRN2", target_bir_lowering=False, num_devices=1)
    data = {k: _np.asarray(v) for k, v in inputs.items()}
    data["consts"] = const_table()
    data["mix_wqkv"] = _np.transpose(data.pop("L0_mix_Wqkv"))
    data["mix_w1"] = _np.transpose(data.pop("L0_mix_W1"))
    data["mix_w2"] = _np.transpose(data.pop("L0_mix_W2"))
    data["mix_b1"] = _np.transpose(data.pop("L0_mix_b1").reshape(2, 128))
    data["ffn0_b1"] = _np.transpose(data.pop("L0_ffn_b1").reshape(NE * F0 // 128, 128))
    data["ffn1_b1"] = _np.transpose(data.pop("L1_ffn_b1").reshape(NE, F1 // 128, 128), (0, 2, 1)).reshape(NE * 128, F1 // 128)
    data["ffn1_b2"] = data.pop("L1_ffn_b2")
    data["mix1_bq"] = _np.transpose(data["L1_mix_b_qk"][0].reshape(2, 128))
    data["mix1_gbeta"] = _np.concatenate([_np.transpose(data.pop(n).reshape(2, 128)) for n in ("L1_mix_gamma", "L1_mix_beta")], 1)
    data["gnn1_w_out"] = _np.transpose(data["L1_gnn_W"].reshape(D, HEADS, DO), (2, 1, 0))
    att = [data.pop(n).reshape(HEADS, DO) for n in ("L1_gnn_att_src", "L1_gnn_att_dst")]
    data["gnn1_att"] = _np.transpose(_np.concatenate(att, 0))
    w = data.pop("L0_gnn_W")
    data["gnn0_w_in"] = _np.transpose(w, (2, 0, 1)).reshape(D, D)
    data["gnn0_w_out"] = _np.transpose(w, (1, 0, 2))
    att = data.pop("L0_gnn_att").reshape(HEADS, 2, DO)
    data["gnn0_att"] = _np.transpose(att, (2, 1, 0)).reshape(DO, 2 * HEADS)
    arrays, args = {}, {}
    for name, x in data.items():
        x = _np.ascontiguousarray(x)
        arrays[f"in_{name}"] = x
        args[name] = nc.dram_tensor(f"in_{name}", x.shape, mybir.dt.from_np(x.dtype), kind="ExternalInput").ap()
    out = nc.dram_tensor("out", (N, D), F32, kind="ExternalOutput").ap()
    network(nc, args, out)
    r = _run(nc, [arrays], core_ids=[0])
    return r.results[0]["out"]
```

```python
import concourse.bass as bass
from concourse import mybir
from contextlib import ExitStack

F32 = mybir.dt.float32
BF16 = mybir.dt.bfloat16
I32 = mybir.dt.int32
ALU = mybir.AluOpType
ACT = mybir.ActivationFunctionType
AX = mybir.AxisListType

N, E, D = 6250, 100000, 256
P, T = 125, 50
J = 125
C = E // J
CP, CK = 100, 8
BC = 40
NB = C // BC
GC = 10
NG = BC // GC
HEADS, DO = 4, 64
ZW = D + HEADS
GW = D + 2 * HEADS
BIG = 1e38
OOB = 200000.0
ROUND = 12582912.0


class Count:

    def __init__(self, e, sem):
        self.e, self.sem, self.n = e, sem, 0

    def next(self):
        self.n += 1
        return self.n

    def reset(self):
        if self.n:
            self.e.sem_inc(self.sem, -self.n)
            self.n = 0


def steps(e, n, body):
    with e.Fori(0, n // 2) as i:
        body(i * 2, 0)
        body(i * 2 + 1, 1)
    if n % 2:
        body(n - 1, 0)


class Mem:

    def __init__(self, nc, stage):
        self.nc, self.stage, self.ctx, self.sems = nc, stage, ExitStack(), []

    def __enter__(self):
        return self

    def __exit__(self, *a):
        if self.sems:
            self.nc.clear_and_free_semaphores(self.sems)
            self.nc.all_engine_barrier()
        self.ctx.close()

    def sb(self, name, shape, dt=F32):
        return self.ctx.enter_context(self.nc.sbuf_tensor(f"{self.stage}_{name}", shape, dt))

    def ps(self, name, shape=(128, 512), dt=F32):
        return self.ctx.enter_context(self.nc.psum_tensor(f"{self.stage}_{name}", list(shape), dt))

    def sem(self, name):
        self.sems.append(self.nc.alloc_semaphore(f"{self.stage}_{name}"))
        return self.sems[-1]

    def counter(self, name):
        return self.nc.alloc_semaphore(f"{self.stage}_{name}")


class Edges:

    def __init__(self, m):
        self.gT = m.sb("gT", [P, C])
        self.srcT = m.sb("srcT", [P, C + 2 * BC], I32)
        self.start = m.sb("start", [BC, (NB + 1) * J])
        self.main_row = m.sb("main_row", [P, T], I32)
        self.extra_row = m.sb("extra_row", [P, T], I32)
        self.edge_row = m.sb("edge_row", [P, T], I32)
        self.first_node = m.sb("first_node", [CP, CK], I32)
        self.first_nodef = m.sb("first_nodef", [CP, CK])
        self.first_row = m.sb("first_row", [CP, CK], I32)
        self.cont = m.sb("cont", [CP, CK])
        self.first_all = m.sb("first_all", [CP, C])
        self.group_mask = m.sb("group_mask", [HEADS, C + 1])


def edge_tables(nc, ed, const, src, dst, start_dram, X, x, zeros):
    ident, tri, iota, rowbase = const.ident, const.tri, const.iota, const.rowbase
    W = CK * J
    with Mem(nc, "et") as m:
        srcn = m.sb("srcn", [CP, W], I32)
        dstx = m.sb("dstx", [CP, W + 1], I32)
        dstf = m.sb("dstf", [CP, W + 1])
        start = m.sb("start", [CP, W])
        ones = m.sb("ones", [CP, W])
        seg = m.sb("seg", [CP, W])
        t1 = m.sb("t1", [CP, W])
        t2 = m.sb("t2", [CP, W])
        hi = m.sb("hi", [CP, W])
        lo = m.sb("lo", [CP, W])
        srcf = m.sb("srcf", [CP, W])
        hiT = m.sb("hiT", [P, C], BF16)
        loT = m.sb("loT", [P, C], BF16)
        iota16 = m.sb("iota16", [P, P, GC], BF16)
        ohi = m.sb("ohi", [P, 2, P, GC], BF16)
        olo = m.sb("olo", [P, 2, T, GC], BF16)
        cnt = m.sb("cnt", [P, T])
        ncum = m.sb("ncum", [P, 2, T])
        nb = m.sb("nb", [P, 8, T])
        tot = m.sb("tot", [P, 2])
        frow = m.sb("frow", [1, C], I32)
        frowf = m.sb("frowf", [1, C])
        pst = m.ps("pst", [128, 2, 4, 128])
        pcnt = m.ps("pcnt")
        poff = m.ps("poff")
        pfa = m.ps("pfa", [128, 2, 512])
        loaded = m.sem("loaded")
        loaded2 = m.sem("loaded2")
        floaded = m.sem("floaded")
        ch = m.sem("ch")
        ready = m.sem("ready")
        tr_done = m.sem("tr_done")
        tr_free = m.sem("tr_free")
        totals = m.sem("totals")
        offs = m.sem("offs")
        oh_ready = [m.sem("oh_ready0"), m.sem("oh_ready1")]
        oh_free = [m.sem("oh_free0"), m.sem("oh_free1")]
        counted = m.sem("counted")
        ntot = m.sem("ntot")
        noff = m.sem("noff")
        fready = m.sem("fready")
        fall = m.sem("fall")
        stored = m.sem("stored")
        st_ready = m.sem("st_ready")
        st_loaded = m.sem("st_loaded")
        z = m.sb("z", [128, 1024])
        z_ready, x_loaded, filled = m.sem("z_ready"), m.sem("x_loaded"), m.sem("filled")
        with nc.Block() as block:

            @block.sync
            def _(e):
                e.dma_start(srcn[:, :], src.rearrange("(p w) -> p w", p=CP)).then_inc(loaded, 16)
                e.dma_start(dstx[:, 1:W + 1], dst.rearrange("(p w) -> p w", p=CP)).then_inc(loaded, 16)
                with nc.allow_non_contiguous_dma(reason="99 single elements"):
                    e.dma_start(dstx[1:CP, 0:1], dst.rearrange("(p w) -> p w", p=CP)[0:CP - 1, W - 1:W]).then_inc(loaded, 16)
                    e.wait_ge(loaded, 48)
                    e.sem_inc(loaded, -48)
                    e.dma_start(frow[:, :], dst.rearrange("(a c j) -> a c j", a=1, j=J)[:, :, 0]).then_inc(floaded, 16)
                e.sem_inc(loaded2, 1)
                e.wait_ge(st_ready, 1)
                e.sem_inc(st_ready, -1)
                e.dma_start(start_dram.rearrange("(p k) j -> p (k j)", p=CP), start[:, :]).then_inc(stored, 16)
                e.wait_ge(stored, 16)
                e.sem_inc(stored, -16)
                e.dma_start(ed.start[:, 0:NB * J].rearrange("k (b j) -> k b j", j=J), start_dram.rearrange("(b k) j -> k b j", k=BC)).then_inc(st_loaded, 16)

            @block.gpsimd
            def _(e):
                nc.gpsimd.memset(z[:, :], 0.0).then_inc(z_ready, 1)

            @block.scalar
            def _(e):
                e.dma_start(X[:, :], x.rearrange("(p t) d -> p (t d)", t=T)).then_inc(x_loaded, 16)
                e.wait_ge(z_ready, 1)
                e.sem_inc(z_ready, -1)
                for view in zeros:
                    p, r, w = view.shape
                    for i in range(r):
                        e.dma_start(view[:, i, :], z[:p, 0:w]).then_inc(filled, 16)
                    e.wait_ge(filled, 16 * r)
                    e.sem_inc(filled, -16 * r)
                e.wait_ge(x_loaded, 16)
                e.sem_inc(x_loaded, -16)

            @block.vector
            def _(e):
                v = nc.vector
                c = Count(e, ch)
                v.memset(dstx[0:1, 0:1], -1).then_inc(ch, 1)
                e.wait_ge(ch, c.next())
                v.memset(ed.start[:, NB * J:], 0.0)
                v.tensor_copy(iota16[:, :, :], iota[:P, 0:P].unsqueeze(2).to_broadcast([P, P, GC]))
                v.memset(ones[:, :], 1.0).then_inc(ch, 1)
                e.wait_ge(ch, c.next())
                v.memset(ed.srcT[:, C:C + 2 * BC], 0).then_inc(ch, 1)
                e.wait_ge(ch, c.next())
                e.wait_ge(loaded2, 1)
                e.sem_inc(loaded2, -1)
                v.tensor_copy(srcf[:, :], srcn[:, :])
                v.tensor_copy(dstf[:, :], dstx[:, :]).then_inc(ch, 1)
                e.wait_ge(ch, c.next())
                v.tensor_tensor(out=start[:, :], in0=dstf[:, 1:W + 1], in1=dstf[:, 0:W], op=ALU.not_equal).then_inc(ch, 1)
                e.wait_ge(ch, c.next())
                e.sem_inc(st_ready, 1)
                v.tensor_tensor_scan(out=seg[:, :], data0=ones[:, :], data1=start[:, :], initial=0.0,
                                     op0=ALU.mult, op1=ALU.add).then_inc(ch, 1)
                e.wait_ge(ch, c.next())
                v.tensor_copy(tot[:CP, 0:1], seg[:, W - 1:W]).then_inc(totals, 1)
                v.tensor_scalar(t1[:, :], dstf[:, 1:W + 1], 0.5, 1.0 / T, ALU.add, ALU.mult).then_inc(ch, 1)
                e.wait_ge(ch, c.next())
                v.tensor_scalar(t1[:, :], t1[:, :], -0.5, ROUND, ALU.add, ALU.add).then_inc(ch, 1)
                e.wait_ge(ch, c.next())
                v.tensor_scalar(hi[:, :], t1[:, :], -ROUND, None, ALU.add).then_inc(ch, 1)
                e.wait_ge(ch, c.next())
                v.scalar_tensor_tensor(lo[:, :], hi[:, :], -float(T), dstf[:, 1:W + 1], ALU.mult, ALU.add).then_inc(ch, 1)
                e.wait_ge(ch, c.next())
                e.wait_ge(offs, 1)
                e.sem_inc(offs, -1)
                v.tensor_scalar(seg[:, :], seg[:, :], poff[:CP, 0:1], -1.0, ALU.add, ALU.add).then_inc(ch, 1)
                e.wait_ge(ch, c.next())
                v.tensor_scalar(t1[:, :], seg[:, :], 0.5, 1.0 / J, ALU.add, ALU.mult).then_inc(ch, 1)
                e.wait_ge(ch, c.next())
                v.tensor_scalar(t1[:, :], t1[:, :], -0.5, ROUND, ALU.add, ALU.add).then_inc(ch, 1)
                e.wait_ge(ch, c.next())
                v.tensor_scalar(t1[:, :], t1[:, :], -ROUND, None, ALU.add).then_inc(ch, 1)
                e.wait_ge(ch, c.next())
                v.scalar_tensor_tensor(t2[:, :], t1[:, :], -float(J), seg[:, :], ALU.mult, ALU.add).then_inc(ch, 1)
                e.wait_ge(ch, c.next())
                e.sem_inc(ready, 1)
                for k in range(CK):
                    e.wait_ge(tr_done, 1)
                    e.sem_inc(tr_done, -1)
                    for n, tab in enumerate((ed.gT, ed.srcT, hiT, loT)):
                        ins = v.tensor_copy(tab[:, 0:C].rearrange("j (p k) -> j p k", k=CK)[:, :, k], pst[:J, k % 2, n, :CP])
                    ins.then_inc(tr_free, 1)
                sv = start[:, :].rearrange("p (k j) -> p k j", j=J)[:, :, 0]
                v.tensor_scalar(ed.cont[:, :], sv, -1.0, 1.0, ALU.mult, ALU.add).then_inc(ch, 1)
                e.wait_ge(ch, c.next())
                v.tensor_copy(ed.first_nodef[:, :], dstf[:, 1:W + 1].rearrange("p (k j) -> p k j", j=J)[:, :, 0]).then_inc(ch, 1)
                e.wait_ge(ch, c.next())
                v.tensor_copy(ed.first_node[:, :], ed.first_nodef[:, :]).then_inc(ch, 1)
                e.wait_ge(ch, c.next())
                v.scalar_tensor_tensor(t1[:, 0:CK], t2[:, :].rearrange("p (k j) -> p k j", j=J)[:, :, 0], float(BC),
                                       rowbase[:CP, :], ALU.mult, ALU.add).then_inc(ch, 1)
                e.wait_ge(ch, c.next())
                v.tensor_copy(ed.first_row[:, :], t1[:, 0:CK]).then_inc(ch, 1)
                e.wait_ge(ch, c.next())
                e.sem_inc(oh_free[0], 1)
                e.sem_inc(oh_free[1], 1)
                c.reset()

                def body(g, par):
                    e.wait_ge(oh_free[par], 1)
                    e.sem_inc(oh_free[par], -1)
                    v.tensor_tensor(out=ohi[:, par], in0=iota16[:, :, :],
                                    in1=hiT[:, bass.ds(g * GC, GC)].unsqueeze(1).to_broadcast([P, P, GC]),
                                    op=ALU.is_equal)
                    v.tensor_tensor(out=olo[:, par], in0=iota16[:, 0:T, :],
                                    in1=loT[:, bass.ds(g * GC, GC)].unsqueeze(1).to_broadcast([P, T, GC]),
                                    op=ALU.is_equal).then_inc(oh_ready[par], 1)
                steps(e, C // GC, body)
                e.wait_ge(counted, 1)
                e.sem_inc(counted, -1)
                v.tensor_copy(cnt[:, :], pcnt[:P, 0:T]).then_inc(ch, 1)
                e.wait_ge(ch, c.next())
                v.tensor_scalar(nb[:, 0, :], cnt[:, :], 0.0, None, ALU.is_gt).then_inc(ch, 1)
                e.wait_ge(ch, c.next())
                v.tensor_tensor_scan(out=ncum[:, 0, :], data0=iota[:P, 1:2].to_broadcast([P, T]), data1=cnt[:, :], initial=0.0,
                                     op0=ALU.mult, op1=ALU.add).then_inc(ch, 1)
                e.wait_ge(ch, c.next())
                v.tensor_tensor_scan(out=ncum[:, 1, :], data0=iota[:P, 1:2].to_broadcast([P, T]), data1=nb[:, 0, :], initial=0.0,
                                     op0=ALU.mult, op1=ALU.add).then_inc(ch, 1)
                e.wait_ge(ch, c.next())
                v.tensor_copy(tot[:, 0:2], ncum[:, :, T - 1]).then_inc(ntot, 1)
                e.wait_ge(noff, 1)
                e.sem_inc(noff, -1)
                v.tensor_scalar(ncum[:, 0, :], ncum[:, 0, :], poff[:P, 4:5], None, ALU.add).then_inc(ch, 1)
                e.wait_ge(ch, c.next())
                v.tensor_scalar(ncum[:, 1, :], ncum[:, 1, :], poff[:P, 5:6], None, ALU.add).then_inc(ch, 1)
                e.wait_ge(ch, c.next())
                v.tensor_tensor(out=nb[:, 1, :], in0=ncum[:, 0, :], in1=cnt[:, :], op=ALU.subtract).then_inc(ch, 1)
                e.wait_ge(ch, c.next())
                v.tensor_tensor(out=nb[:, 2, :], in0=ncum[:, 1, :], in1=nb[:, 0, :], op=ALU.subtract).then_inc(ch, 1)
                e.wait_ge(ch, c.next())

                def floordiv(dst_, src_, d):
                    v.tensor_scalar(dst_, src_, 0.5, 1.0 / d, ALU.add, ALU.mult).then_inc(ch, 1)
                    e.wait_ge(ch, c.next())
                    v.tensor_scalar(dst_, dst_, -0.5, ROUND, ALU.add, ALU.add).then_inc(ch, 1)
                    e.wait_ge(ch, c.next())
                    v.tensor_scalar(dst_, dst_, -ROUND, None, ALU.add).then_inc(ch, 1)
                    e.wait_ge(ch, c.next())

                floordiv(nb[:, 3, :], nb[:, 1, :], J)
                floordiv(nb[:, 4, :], nb[:, 2, :], J)
                v.scalar_tensor_tensor(nb[:, 2, :], nb[:, 4, :], -float(J), nb[:, 2, :], ALU.mult, ALU.add).then_inc(ch, 1)
                e.wait_ge(ch, c.next())
                floordiv(nb[:, 4, :], nb[:, 3, :], BC)
                v.scalar_tensor_tensor(nb[:, 5, :], nb[:, 4, :], float(P * BC - BC), nb[:, 3, :], ALU.mult, ALU.add).then_inc(ch, 1)
                e.wait_ge(ch, c.next())
                v.scalar_tensor_tensor(nb[:, 5, :], nb[:, 2, :], float(BC), nb[:, 5, :], ALU.mult, ALU.add).then_inc(ch, 1)
                e.wait_ge(ch, c.next())
                v.tensor_scalar(nb[:, 6, :], nb[:, 0, :], -OOB, OOB, ALU.mult, ALU.add).then_inc(ch, 1)
                e.wait_ge(ch, c.next())
                v.tensor_tensor(out=nb[:, 5, :], in0=nb[:, 5, :], in1=nb[:, 6, :], op=ALU.add).then_inc(ch, 1)
                e.wait_ge(ch, c.next())
                v.tensor_copy(ed.main_row[:, :], nb[:, 5, :]).then_inc(ch, 1)
                e.wait_ge(ch, c.next())
                v.tensor_tensor(out=nb[:, 5, :], in0=nb[:, 1, :], in1=nb[:, 6, :], op=ALU.add).then_inc(ch, 1)
                e.wait_ge(ch, c.next())
                v.tensor_copy(ed.edge_row[:, :], nb[:, 5, :]).then_inc(ch, 1)
                e.wait_ge(ch, c.next())
                v.tensor_scalar(nb[:, 3, :], nb[:, 3, :], 1.0, None, ALU.add).then_inc(ch, 1)
                e.wait_ge(ch, c.next())
                v.tensor_scalar(nb[:, 4, :], nb[:, 3, :], float(J), None, ALU.mult).then_inc(ch, 1)
                e.wait_ge(ch, c.next())
                v.tensor_tensor(out=nb[:, 4, :], in0=ncum[:, 0, :], in1=nb[:, 4, :], op=ALU.is_le).then_inc(ch, 1)
                e.wait_ge(ch, c.next())
                v.scalar_tensor_tensor(nb[:, 5, :], nb[:, 4, :], OOB, nb[:, 3, :], ALU.mult, ALU.add).then_inc(ch, 1)
                e.wait_ge(ch, c.next())
                v.tensor_tensor(out=nb[:, 5, :], in0=nb[:, 5, :], in1=nb[:, 6, :], op=ALU.add).then_inc(ch, 1)
                e.wait_ge(ch, c.next())
                v.tensor_copy(ed.extra_row[:, :], nb[:, 5, :]).then_inc(ch, 1)
                e.wait_ge(ch, c.next())
                e.wait_ge(floaded, 16)
                e.sem_inc(floaded, -16)
                v.tensor_copy(frowf[:, :], frow[:, :]).then_inc(ch, 1)
                e.wait_ge(ch, c.next())
                e.sem_inc(fready, 1)
                e.wait_ge(fall, 1)
                e.sem_inc(fall, -1)
                v.tensor_copy(ed.first_all[:, :].rearrange("p (a c) -> p a c", a=2), pfa[:CP, :, 0:C // 2]).then_inc(ch, 1)
                e.wait_ge(ch, c.next())
                v.memset(ed.group_mask[:, :], -BIG).then_inc(ch, 1)
                e.wait_ge(ch, c.next())
                v.tensor_tensor(out=ed.group_mask[:, 1:C], in0=ed.first_all[0:HEADS, 1:C], in1=ed.first_all[0:HEADS, 0:C - 1],
                                op=ALU.is_equal).then_inc(ch, 1)
                e.wait_ge(ch, c.next())
                v.tensor_scalar(ed.group_mask[:, 1:C], ed.group_mask[:, 1:C], 2 * BIG, -BIG, ALU.mult, ALU.add).then_inc(ch, 1)
                e.wait_ge(ch, c.next())
                e.wait_ge(st_loaded, 16)
                e.sem_inc(st_loaded, -16)
                v.memset(ed.start[:, 0:NB * J].rearrange("k (b j) -> k b j", j=J)[:, :, 0:1], 1.0).then_inc(ch, 1)
                e.wait_ge(ch, c.next())
                c.reset()

            @block.tensor
            def _(e):
                t = nc.tensor
                e.wait_ge(totals, 1)
                e.sem_inc(totals, -1)
                t.matmul(poff[:CP, 0:1], tri[:CP, :CP], tot[:CP, 0:1], start=True, stop=True).then_inc(offs, 1)
                e.wait_ge(ready, 1)
                e.sem_inc(ready, -1)
                e.sem_inc(tr_free, 2)
                for k in range(CK):
                    e.wait_ge(tr_free, 1)
                    e.sem_inc(tr_free, -1)
                    for n, tab in enumerate((t2, srcf, hi, lo)):
                        ins = t.transpose(pst[:J, k % 2, n, :CP], tab[:, k * J:(k + 1) * J], ident[:CP, :CP])
                    ins.then_inc(tr_done, 1)

                def group(par, first=False, last=False):
                    e.wait_ge(oh_ready[par], 1)
                    e.sem_inc(oh_ready[par], -1)
                    for k in range(GC):
                        ins = t.matmul(pcnt[:P, 0:T], ohi[:, par, :, k], olo[:, par, :, k], start=first and k == 0,
                                       stop=last and k == GC - 1)
                    if last:
                        ins.then_inc(counted, 1)
                    else:
                        ins.then_inc(oh_free[par], 1)
                group(0, first=True)
                with e.Fori(0, C // GC // 2 - 1) as i:
                    group(1)
                    group(0)
                group(1, last=True)
                e.wait_ge(ntot, 1)
                e.sem_inc(ntot, -1)
                t.matmul(poff[:P, 4:6], tri[:P, :P], tot[:, 0:2], start=True, stop=True).then_inc(noff, 1)
                e.wait_ge(fready, 1)
                e.sem_inc(fready, -1)
                for a in range(2):
                    ins = t.matmul(pfa[:CP, a, 0:C // 2], const.ones[0:1, :CP], frowf[0:1, a * (C // 2):(a + 1) * (C // 2)],
                                   start=True, stop=True)
                ins.then_inc(fall, 1)



def norm_stats(nc, stage, X, mean, rstd, eps, row_stats=None):
    with Mem(nc, stage) as m:
        st = m.sb("st", [P, T * 6]) if row_stats is None else row_stats
        dd = m.sb("dd", [P, 2, T])
        ch, var_ready, sd_ready = m.sem("ch"), m.sem("var_ready"), m.sem("sd_ready")
        with nc.Block() as block:

            @block.vector
            def _(e):
                v = nc.vector
                c = Count(e, ch)
                if row_stats is None:
                    with e.Fori(0, T // 10) as i:
                        for k in range(10):
                            v.bn_stats(out=st[:, bass.ds(i * 60 + k * 6, 6)], in_=X[:, bass.ds(i * (10 * D) + k * D, D)])
                v.memset(dd[:, :, :], 0.0).then_inc(ch, 1)
                e.wait_ge(ch, c.next())
                s = st[:, :].rearrange("p (t s) -> p s t", s=6)
                v.tensor_tensor(out=mean[:, :], in0=s[:, 1, :], in1=s[:, 4, :], op=ALU.add).then_inc(ch, 1)
                e.wait_ge(ch, c.next())
                v.tensor_scalar(mean[:, :], mean[:, :], 0.5, None, ALU.mult).then_inc(ch, 1)
                e.wait_ge(ch, c.next())
                v.tensor_tensor(out=dd[:, 0, :], in0=s[:, 1, :], in1=s[:, 4, :], op=ALU.subtract).then_inc(ch, 1)
                e.wait_ge(ch, c.next())
                v.tensor_tensor(out=dd[:, 0, :], in0=dd[:, 0, :], in1=dd[:, 0, :], op=ALU.mult).then_inc(ch, 1)
                e.wait_ge(ch, c.next())
                v.tensor_tensor(out=dd[:, 1, :], in0=s[:, 2, :], in1=s[:, 5, :], op=ALU.add).then_inc(ch, 1)
                e.wait_ge(ch, c.next())
                v.tensor_scalar(dd[:, 1, :], dd[:, 1, :], 1.0 / D, eps, ALU.mult, ALU.add).then_inc(ch, 1)
                e.wait_ge(ch, c.next())
                v.scalar_tensor_tensor(dd[:, 1, :], dd[:, 0, :], 0.25, dd[:, 1, :], ALU.mult, ALU.add).then_inc(ch, 1)
                e.wait_ge(ch, c.next())
                e.sem_inc(var_ready, 1)
                e.wait_ge(sd_ready, 1)
                e.sem_inc(sd_ready, -1)
                v.reciprocal(rstd[:, :], dd[:, 0, :]).then_inc(ch, 1)
                e.wait_ge(ch, c.next())
                c.reset()

            @block.scalar
            def _(e):
                e.wait_ge(var_ready, 1)
                e.sem_inc(var_ready, -1)
                nc.scalar.activation(dd[:, 0, :], dd[:, 1, :], ACT.Sqrt).then_inc(sd_ready, 1)


def gat_weights(nc, stage, w_in, w_out, att, wz):
    with Mem(nc, stage) as m:
        wo = m.sb("wo", [DO, HEADS, D])
        at = m.sb("at", [DO, 2 * HEADS])
        pw = m.ps("pw")
        ld, done = m.sem("ld"), m.sem("done")
        with nc.Block() as block:

            @block.sync
            def _(e):
                e.dma_start(wo[:, :, :], w_out).then_inc(ld, 16)
                e.dma_start(at[:, :], att).then_inc(ld, 16)
                e.dma_start(wz[:, :, 0:D], w_in.rearrange("(b i) o -> i b o", b=2)).then_inc(ld, 16)

            @block.tensor
            def _(e):
                e.wait_ge(ld, 48)
                e.sem_inc(ld, -48)
                for b in range(2):
                    for h in range(HEADS):
                        for s in range(2):
                            ins = nc.tensor.matmul(pw[:, (b * 8 + s * 4 + h):(b * 8 + s * 4 + h) + 1], wo[:, h, b * 128:(b + 1) * 128],
                                                   at[:, s * 4 + h:s * 4 + h + 1], start=True, stop=True)
                ins.then_inc(done, 1)

            @block.vector
            def _(e):
                e.wait_ge(done, 1)
                e.sem_inc(done, -1)
                nc.vector.tensor_copy(wz[:, :, D:D + 8], pw[:, 0:16].rearrange("p (b s) -> p b s", b=2))


def dense0(nc, const, ed, X, mean, rstd, wz, wkv, wq, zt, edt, edn, edge_ed, qT, kv):
    with Mem(nc, "d0") as m:
        xn = m.sb("xn", [P, 2, D])
        xT = m.sb("xT", [128, 2, 2, P])
        zr = m.sb("zr", [P, 2, ZW + HEADS])
        ke, kr = m.sb("ke", [P, 2, D]), m.sb("kr", [P, 2, D])
        qe, qr = m.sb("qe", [128, 2, 2 * P]), m.sb("qr", [128, 2, 2 * P])
        kk = m.sb("kk", [P, 2, D])
        vv = m.sb("vv", [P, 2, 2, 129])
        pT = m.ps("pT")
        pz = m.ps("pz")
        pkv = [m.ps("pkv0"), m.ps("pkv1")]
        pq = [m.ps("pq0"), m.ps("pq1")]
        pacc = [m.ps("pacc0"), m.ps("pacc1")]
        ch = m.sem("ch")
        S = {n: [m.sem(n + "0"), m.sem(n + "1")] for n in
             ("xn_ready", "xn_free", "zr_ready", "zr_free", "zr_stored", "exps_ready", "exps_free", "k_ready", "k_free",
              "pkv_ready", "pkv_free", "pq_ready", "pq_free")}
        pT_ready, xT_ready = m.sem("pT_ready"), m.sem("xT_ready")
        pz_ready, pz_free = m.sem("pz_ready"), m.sem("pz_free")
        acc_ready = m.sem("acc_ready")
        edst = m.sem("edst")
        ed_done = m.sem("ed_done")
        row_ready, scattered = m.sem("row_ready"), m.counter("scattered")
        zt_v = zt.rearrange("(p t) w -> p (t w)", t=T)
        with nc.Block() as block:

            @block.vector
            def _(e):
                v = nc.vector
                c = Count(e, ch)
                v.memset(vv[:, :, :, :], 1.0).then_inc(ch, 1)
                e.wait_ge(ch, c.next())
                c.reset()
                for par in range(2):
                    e.sem_inc(S["xn_free"][par], 1)
                    e.sem_inc(S["k_free"][par], 1)
                    e.sem_inc(S["exps_free"][par], 1)

                def norm(t, par):
                    e.wait_ge(S["xn_free"][par], 1)
                    e.sem_inc(S["xn_free"][par], -1)
                    v.tensor_scalar(xn[:, par, :], X[:, bass.ds(t * D, D)], mean[:, bass.ds(t, 1)], rstd[:, bass.ds(t, 1)],
                                    ALU.subtract, ALU.mult).then_inc(S["xn_ready"][par], 1)

                def body(t, par):
                    e.wait_ge(S["exps_ready"][par], 1)
                    e.sem_inc(S["exps_ready"][par], -1)
                    v.scalar_tensor_tensor(kk[:, par, :], ke[:, par, :], 1.0, kr[:, par, :], ALU.min, ALU.add).then_inc(S["k_ready"][par], 1)
                    v.scalar_tensor_tensor(qT[:, bass.ds(t * 2 * P, 2 * P)], qe[:, par, :], 1.0, qr[:, par, :], ALU.min, ALU.add).then_inc(S["exps_free"][par], 1)
                norm(0, 0)
                norm(1, 1)
                with e.Fori(0, T // 2 - 1) as i:
                    for par in range(2):
                        norm(i * 2 + par + 2, par)
                        body(i * 2 + par, par)
                body(T - 2, 0)
                body(T - 1, 1)
                v.memset(kv[:, :], 0.0).then_inc(ch, 1)
                e.wait_ge(ch, c.next())
                e.wait_ge(acc_ready, 1)
                e.sem_inc(acc_ready, -1)
                for b in range(2):
                    for g in range(4):
                        r = slice(32 * g, 32 * g + 32)
                        o = b * 132
                        v.tensor_copy(kv[r, o + 32 * g:o + 32 * g + 32], pacc[b][r, 32 * g:32 * g + 32])
                        v.tensor_copy(kv[r, o + 128 + g:o + 129 + g], pacc[b][r, 128:129])
                c.reset()

            @block.scalar
            def _(e):
                a = nc.scalar

                def transposed(par):
                    e.wait_ge(pT_ready, 1)
                    e.sem_inc(pT_ready, -1)
                    e.sem_inc(S["xn_free"][par], 1)
                    a.activation(xT[:, par, :, :], pT[:, 0:2 * P].rearrange("p (b n) -> p b n", b=2), ACT.Copy).then_inc(xT_ready, 1)

                def body(t, par, last=False):
                    if not last:
                        transposed(1 - par)
                    e.wait_ge(pz_ready, 1)
                    e.sem_inc(pz_ready, -1)
                    e.wait_ge(S["zr_free"][par], 1)
                    e.sem_inc(S["zr_free"][par], -1)
                    a.activation(zr[:, par, :], pz[:P, 0:ZW + HEADS], ACT.Copy).then_inc(S["zr_ready"][par], 1)
                    a.activation(edn[:, bass.ds(t * HEADS, HEADS)], pz[:P, ZW:ZW + HEADS], ACT.Copy).then_inc(pz_free, 1)
                    e.drain().then_inc(row_ready, 1)
                    e.wait_ge(S["pkv_ready"][par], 1)
                    e.sem_inc(S["pkv_ready"][par], -1)
                    e.wait_ge(S["k_free"][par], 1)
                    e.sem_inc(S["k_free"][par], -1)
                    e.wait_ge(S["exps_free"][par], 1)
                    e.sem_inc(S["exps_free"][par], -1)
                    a.activation(ke[:, par, :], pkv[par][:P, 0:D], ACT.Exp)
                    a.activation(kr[:, par, :], pkv[par][:P, 0:D], ACT.Relu)
                    a.activation(vv[:, par, :, 0:128], pkv[par][:P, D:2 * D].rearrange("p (a b) -> p a b", a=2), ACT.Copy).then_inc(S["pkv_free"][par], 1)
                    e.wait_ge(S["pq_ready"][par], 1)
                    e.sem_inc(S["pq_ready"][par], -1)
                    a.activation(qe[:, par, :], pq[par][:, 0:2 * P], ACT.Exp)
                    a.activation(qr[:, par, :], pq[par][:, 0:2 * P], ACT.Relu).then_inc(S["pq_free"][par], 1)
                    e.drain().then_inc(S["exps_ready"][par], 1)
                for par in range(2):
                    e.sem_inc(S["zr_free"][par], 1)
                transposed(0)
                with e.Fori(0, T // 2 - 1) as i:
                    body(i * 2, 0)
                    body(i * 2 + 1, 1)
                body(T - 2, 0)
                body(T - 1, 1, last=True)
                e.drain().then_inc(ed_done, 1)

            @block.gpsimd
            def _(e):
                scatter_edge_inputs(e, ed, edn, edge_ed, row_ready, scattered)

            @block.sync
            def _(e):
                def body(t, par):
                    e.wait_ge(S["zr_ready"][par], 1)
                    e.sem_inc(S["zr_ready"][par], -1)
                    e.dma_start(zt_v[:, bass.ds(t * ZW, ZW)], zr[:, par, 0:ZW]).then_inc(S["zr_stored"][par], 16)
                    e.wait_ge(S["zr_stored"][par], 16)
                    e.sem_inc(S["zr_stored"][par], -16)
                    e.sem_inc(S["zr_free"][par], 1)
                steps(e, T, body)
                e.wait_ge(ed_done, 1)
                e.sem_inc(ed_done, -1)
                e.dma_start(edt.rearrange("(p t) w -> p (t w)", t=T), edn[:, :]).then_inc(edst, 16)
                e.wait_ge(edst, 16)
                e.sem_inc(edst, -16)

            @block.tensor
            def _(e):
                t_ = nc.tensor
                e.sem_inc(pz_free, 1)
                for par in range(2):
                    e.sem_inc(S["pkv_free"][par], 1)
                    e.sem_inc(S["pq_free"][par], 1)

                def transposes(par):
                    e.wait_ge(S["xn_ready"][par], 1)
                    e.sem_inc(S["xn_ready"][par], -1)
                    for b in range(2):
                        ins = t_.transpose(pT[:, b * P:(b + 1) * P], xn[:, par, b * 128:(b + 1) * 128], const.ident[:P, :P])
                    ins.then_inc(pT_ready, 1)

                def accumulate(par, first=False, last=False):
                    e.wait_ge(S["k_ready"][par], 1)
                    e.sem_inc(S["k_ready"][par], -1)
                    for b in range(2):
                        ins = t_.matmul(pacc[b][:, 0:129], kk[:, par, b * 128:(b + 1) * 128], vv[:, par, b, :], start=first, stop=last)
                    ins.then_inc(acc_ready if last else S["k_free"][par], 1)

                def body(par, last=False):
                    e.wait_ge(xT_ready, 1)
                    e.sem_inc(xT_ready, -1)
                    if not last:
                        transposes(1 - par)
                    e.wait_ge(pz_free, 1)
                    e.sem_inc(pz_free, -1)
                    for b in range(2):
                        ins = t_.matmul(pz[:P, 0:ZW + HEADS], xT[:, par, b, :], wz[:, b, :], start=b == 0, stop=b == 1)
                    ins.then_inc(pz_ready, 1)
                    e.wait_ge(S["pkv_free"][par], 1)
                    e.sem_inc(S["pkv_free"][par], -1)
                    for b in range(2):
                        ins = t_.matmul(pkv[par][:P, 0:2 * D], xT[:, par, b, :], wkv[:, b, :], start=b == 0, stop=b == 1)
                    ins.then_inc(S["pkv_ready"][par], 1)
                    e.wait_ge(S["pq_free"][par], 1)
                    e.sem_inc(S["pq_free"][par], -1)
                    for o in range(2):
                        for b in range(2):
                            ins = t_.matmul(pq[par][:, o * P:(o + 1) * P], wq[:, b, o * 128:(o + 1) * 128], xT[:, par, b, :], start=b == 0, stop=b == 1)
                    ins.then_inc(S["pq_ready"][par], 1)
                transposes(0)
                body(0)
                body(1)
                accumulate(0, first=True)
                with e.Fori(0, T // 2 - 2) as i:
                    body(0)
                    accumulate(1)
                    body(1)
                    accumulate(0)
                body(0)
                accumulate(1)
                body(1, last=True)
                accumulate(0)
                accumulate(1, last=True)


def scatter_edge_inputs(e, ed, edn, edge_ed, row_ready, scattered):
    for t in range(T):
        e.wait_ge(row_ready, 1)
        e.sem_inc(row_ready, -1)
        e.indirect_dma_start(out=edge_ed[:, :], out_offset=bass.IndirectOffsetOnAxis(ap=ed.edge_row[:, t:t + 1], axis=0),
                             in_=edn[:, t * HEADS:(t + 1) * HEADS], in_offset=None,
                             bounds_check=E - 1, oob_is_err=False).then_inc(scattered, 16)
    e.wait_ge(scattered, 16 * T)


def chunk_edge_inputs(nc, stage, ed, edt, edge_ed):
    with Mem(nc, stage) as m:
        fe = m.sb("fe", [CP, CK, HEADS])
        gathered, stored = m.counter("gathered"), m.sem("stored")
        with nc.Block() as block:

            @block.gpsimd
            def _(e):
                for k in range(CK):
                    e.indirect_dma_start(out=fe[:, k, :], out_offset=None, in_=edt[:, :],
                                         in_offset=bass.IndirectOffsetOnAxis(ap=ed.first_node[:, k:k + 1], axis=0)).then_inc(gathered, 16)

            @block.sync
            def _(e):
                e.wait_ge(gathered, 16 * CK)
                e.dma_start(edge_ed[0:E, :].rearrange("(p k j) h -> p k (j h)", k=CK, j=J)[:, :, 0:HEADS], fe[:, :, :]).then_inc(stored, 16)
                e.wait_ge(stored, 16)
                e.sem_inc(stored, -16)


def gat_edges(nc, stage, const, ed, zt, edge_ed, sums, slope):
    HW = J + 1
    W4 = HEADS * HW
    with Mem(nc, stage) as m:
        Z = m.sb("Z", [P, 2 * BC * GW])
        onehot = m.sb("onehot", [P, 2, GC * J])
        sumrow = m.sb("sumrow", [P, 2, GC * GW])
        idx = m.sb("idx", [P, 2, BC], I32)
        edv = m.sb("edv", [BC, 2, J * HEADS])
        vs = m.sb("vs", [BC, W4])
        cm = m.sb("cm", [BC, W4])
        mk = m.sb("mk", [BC, W4 + 1])
        edf = m.sb("edf", [BC, W4])
        ev = m.sb("ev", [BC, W4])
        fw = m.sb("fw", [BC, W4])
        bw, ex, ms = edf, cm, vs
        pes = m.ps("pes")
        pex = m.ps("pex")
        NPO = 5
        po = [m.ps(f"po{i}") for i in range(NPO)]
        ch = m.sem("ch")
        S = {n: [m.sem(n + "0"), m.sem(n + "1")] for n in
             ("slot_free", "staged", "edv_ld", "edv_ready", "edv_free", "grp_ready", "oh_free", "out_ready", "out_free", "stored")}
        S["gathered"] = [m.counter("gathered0"), m.counter("gathered1")]
        es_ready, es_free = m.sem("es_ready"), m.sem("es_free")
        d_ready, ex_ready, ms_ready = m.sem("d_ready"), m.sem("ex_ready"), m.sem("ms_ready")
        pex_ready, pex_free = m.sem("pex_ready"), m.sem("pex_free")
        po_ready = [m.sem(f"po_ready{i}") for i in range(NPO)]
        po_free = [m.sem(f"po_free{i}") for i in range(NPO)]
        zv = [Z[:, b * BC * GW:(b + 1) * BC * GW].rearrange("p (k w) -> p k w", w=GW) for b in range(2)]
        h4 = lambda x: x[:, 0:W4].rearrange("k (h j) -> k h j", h=HEADS)[:, :, 0:J]
        sums_v = sums.rearrange("(x k) w -> x (k w)", k=BC)
        ed_v = edge_ed.rearrange("(c j) h -> c (j h)", j=J)
        with nc.Block() as block:

            @block.gpsimd
            def _(e):
                e.sem_inc(S["slot_free"][0], NG)
                e.sem_inc(S["slot_free"][1], NG)
                with e.Fori(0, NB // 2) as i:
                    for b in range(2):
                        e.wait_ge(S["staged"][b], 1)
                        e.sem_inc(S["staged"][b], -1)
                        for k in range(BC):
                            if k % GC == 0:
                                e.wait_ge(S["slot_free"][b], 1)
                                e.sem_inc(S["slot_free"][b], -1)
                            e.indirect_dma_start(out=zv[b][:, k, 0:ZW], out_offset=None, in_=zt[:, :],
                                                 in_offset=bass.IndirectOffsetOnAxis(ap=idx[:, b, k:k + 1], axis=0)).then_inc(S["gathered"][b], 16)

            @block.sync
            def _(e):
                def load(B, b):
                    e.wait_ge(S["edv_free"][b], 1)
                    e.sem_inc(S["edv_free"][b], -1)
                    e.dma_start(edv[:, b, :], ed_v[bass.ds(B * BC, BC), :]).then_inc(S["edv_ld"][b], 16)
                    e.wait_ge(S["edv_ld"][b], 16)
                    e.sem_inc(S["edv_ld"][b], -16)
                    e.sem_inc(S["edv_ready"][b], 1)
                e.sem_inc(S["edv_free"][0], 1)
                e.sem_inc(S["edv_free"][1], 1)
                load(0, 0)
                with e.Fori(0, NB // 2) as i:
                    for b in range(2):
                        load(i * 2 + b + 1, 1 - b)
                        for q in range(NG):
                            e.wait_ge(S["out_ready"][q % 2], 1)
                            e.sem_inc(S["out_ready"][q % 2], -1)
                            e.dma_start(sums_v[bass.ds((i * 2 + b) * P, P), q * GC * GW:(q + 1) * GC * GW], sumrow[:, q % 2, :]).then_inc(S["stored"][q % 2], 16)
                            e.wait_ge(S["stored"][q % 2], 16)
                            e.sem_inc(S["stored"][q % 2], -16)
                            e.sem_inc(S["out_free"][q % 2], 1)

            @block.vector
            def _(e):
                v = nc.vector
                c = Count(e, ch)
                for x in (vs, cm, edf, ev):
                    v.memset(x[:, :], 0.0)
                v.memset(mk[:, :], -BIG).then_inc(ch, 1)
                e.wait_ge(ch, c.next())
                for b in range(2):
                    v.tensor_copy(idx[:, b, :], ed.srcT[:, b * BC:(b + 1) * BC]).then_inc(S["staged"][b], 1)
                c.reset()

                def e_dst(B, b):
                    st = ed.start[:, bass.ds(B * J, J)].unsqueeze(1).to_broadcast([BC, HEADS, J])
                    v.tensor_scalar(h4(cm), st, -1.0, 1.0, ALU.mult, ALU.add)
                    v.tensor_scalar(h4(mk), st, -2 * BIG, BIG, ALU.mult, ALU.add)
                    e.wait_ge(S["edv_ready"][b], 1)
                    e.sem_inc(S["edv_ready"][b], -1)
                    v.tensor_tensor(out=h4(vs), in0=edv[:, b, :].rearrange("k (j h) -> k h j", h=HEADS), in1=st, op=ALU.mult).then_inc(ch, 1)
                    e.wait_ge(ch, c.next())
                    e.sem_inc(S["edv_free"][b], 1)
                    v.tensor_tensor_scan(out=edf[:, :], data0=cm[:, :], data1=vs[:, :], initial=0.0, op0=ALU.mult, op1=ALU.add).then_inc(ch, 1)
                    e.wait_ge(ch, c.next())

                def onehots(i, b, q):
                    e.wait_ge(S["oh_free"][q % 2], 1)
                    e.sem_inc(S["oh_free"][q % 2], -1)
                    v.tensor_tensor(out=onehot[:, q % 2, :].rearrange("p (k j) -> p k j", k=GC),
                                    in0=const.iota[:P, 0:J].unsqueeze(1).to_broadcast([P, GC, J]),
                                    in1=ed.gT[:, bass.ds(i * (2 * BC) + (b * BC + q * GC), GC)].unsqueeze(2).to_broadcast([P, GC, J]),
                                    op=ALU.is_equal)

                def weigh(b, q):
                    for k in (0, GC // 2):
                        zg = zv[b][:, q * GC + k:q * GC + k + GC // 2, :]
                        v.tensor_tensor(out=zg[:, :, 0:D].rearrange("p k (h o) -> p k h o", h=HEADS),
                                        in0=zg[:, :, 0:D].rearrange("p k (h o) -> p k h o", h=HEADS),
                                        in1=zg[:, :, D:D + HEADS].unsqueeze(3).to_broadcast([P, GC // 2, HEADS, DO]), op=ALU.mult).then_inc(S["grp_ready"][q % 2], 1)
                e_dst(0, 0)
                c.reset()
                with e.Fori(0, NB // 2) as i:
                    for b in range(2):
                        B = i * 2 + b
                        st = ed.start[:, bass.ds(B * J, J)].unsqueeze(1).to_broadcast([BC, HEADS, J])
                        e.wait_ge(S["gathered"][b], i * (16 * BC) + 16 * BC)
                        v.tensor_copy(idx[:, b, :], ed.srcT[:, bass.ds(B * BC + 2 * BC, BC)]).then_inc(S["staged"][b], 1)
                        e.wait_ge(es_ready, 1)
                        e.sem_inc(es_ready, -1)
                        v.tensor_tensor(out=h4(ev), in0=pes[:BC, :].rearrange("k (h j) -> k h j", h=HEADS)[:, :, 0:J], in1=h4(edf), op=ALU.add).then_inc(ch, 1)
                        e.wait_ge(ch, c.next())
                        e.sem_inc(es_free, 1)
                        v.scalar_tensor_tensor(ev[:, :], ev[:, :], slope, ev[:, :], ALU.mult, ALU.max).then_inc(ch, 1)
                        e.wait_ge(ch, c.next())
                        v.tensor_tensor_scan(out=fw[:, :], data0=mk[:, 0:W4], data1=ev[:, :], initial=-BIG, op0=ALU.min, op1=ALU.max)
                        v.tensor_tensor_scan(out=bw[:, ::-1], data0=mk[:, W4:0:-1], data1=ev[:, ::-1], initial=-BIG, op0=ALU.min, op1=ALU.max).then_inc(ch, 1)
                        e.wait_ge(ch, c.next())
                        v.tensor_tensor(out=fw[:, :], in0=fw[:, :], in1=bw[:, :], op=ALU.max).then_inc(ch, 1)
                        e.wait_ge(ch, c.next())
                        v.tensor_tensor(out=ev[:, :], in0=ev[:, :], in1=fw[:, :], op=ALU.subtract).then_inc(d_ready, 1)
                        v.tensor_tensor(out=h4(ms), in0=h4(fw), in1=st, op=ALU.mult).then_inc(ms_ready, 1)
                        onehots(i, b, 0)
                        e.wait_ge(pex_ready, 1)
                        e.sem_inc(pex_ready, -1)
                        v.tensor_copy(zv[b].rearrange("p k w -> p w k")[:, D:GW, :], pex[:P, 0:8 * BC].rearrange("p (w k) -> p w k", w=8)).then_inc(ch, 1)
                        e.wait_ge(ch, c.next())
                        e.sem_inc(pex_free, 1)
                        c.reset()
                        for q in range(NG):
                            if q:
                                onehots(i, b, q)
                            weigh(b, q)
                            if q == NG // 2 - 1:
                                e_dst(B + 1, 1 - b)
                                c.reset()

            @block.scalar
            def _(e):
                a = nc.scalar
                e.sem_inc(S["out_free"][0], 1)
                e.sem_inc(S["out_free"][1], 1)
                with e.Fori(0, NB // 2) as i:
                    for b in range(2):
                        e.wait_ge(d_ready, 1)
                        e.sem_inc(d_ready, -1)
                        a.activation(ex[:, :], ev[:, :], ACT.Exp).then_inc(ex_ready, 1)
                        with e.Fori(0, NG // 2) as g:
                            for par in range(2):
                                e.wait_ge(S["out_free"][par], 1)
                                e.sem_inc(S["out_free"][par], -1)
                                for k in range(GC):
                                    e.wait_ge(po_ready[k % NPO], 1)
                                    e.sem_inc(po_ready[k % NPO], -1)
                                    if k == GC - 1:
                                        e.sem_inc(S["oh_free"][par], 1)
                                        e.sem_inc(S["slot_free"][b], 1)
                                    a.activation(sumrow[:, par, k * GW:(k + 1) * GW], po[k % NPO][:P, 0:GW], ACT.Copy).then_inc(po_free[k % NPO], 1)
                                e.drain().then_inc(S["out_ready"][par], 1)

            @block.tensor
            def _(e):
                t = nc.tensor
                for s in [es_free, pex_free, S["oh_free"][0], S["oh_free"][1]] + po_free:
                    e.sem_inc(s, 1)
                with e.Fori(0, NB // 2) as i:
                    for b in range(2):
                        e.wait_ge(S["gathered"][b], i * (16 * BC) + 16 * BC)
                        e.wait_ge(es_free, 1)
                        e.sem_inc(es_free, -1)
                        for h in range(HEADS):
                            ins = t.transpose(pes[:BC, h * 128:h * 128 + J], zv[b][:, :, D + h], const.ident[:P, :P])
                        ins.then_inc(es_ready, 1)
                        e.wait_ge(ex_ready, 1)
                        e.sem_inc(ex_ready, -1)
                        e.wait_ge(ms_ready, 1)
                        e.sem_inc(ms_ready, -1)
                        e.wait_ge(pex_free, 1)
                        e.sem_inc(pex_free, -1)
                        for n in range(2 * HEADS):
                            x, h = (ex, ms)[n // HEADS], n % HEADS
                            ins = t.transpose(pex[:P, n * BC:(n + 1) * BC], x[:, h * HW:h * HW + J], const.ident[:BC, :BC])
                        ins.then_inc(pex_ready, 1)
                        with e.Fori(0, NG // 2) as g:
                            for par in range(2):
                                for k in range(GC):
                                    if k % (GC // 2) == 0:
                                        e.wait_ge(S["grp_ready"][par], 1)
                                        e.sem_inc(S["grp_ready"][par], -1)
                                    e.wait_ge(po_free[k % NPO], 1)
                                    e.sem_inc(po_free[k % NPO], -1)
                                    ins = t.matmul(po[k % NPO][:P, 0:GW], onehot[:, par, k * J:(k + 1) * J],
                                                   Z[:, bass.ds(g * (2 * GC * GW) + (b * BC + par * GC + k) * GW, GW)], start=True, stop=True)
                                    ins.then_inc(po_ready[k % NPO], 1)


def gat_extras(nc, m, block, const, ed, sums, extras, extras_stored):
    R = m.sb("R", [CP, CK * GW])
    same = m.sb("same", [CP, 2, C])
    mt = m.sb("mt", [HEADS, C])
    fw = m.sb("fw", [HEADS, C])
    bw = m.sb("bw", [HEADS, C])
    mc = m.sb("mc", [CP, CK])
    df = m.sb("df", [CP, CK * HEADS])
    fac = m.sb("fac", [CP, CK * HEADS])
    mg = m.sb("mg", [CP, CK * HEADS])
    tot = m.sb("tot", [CP, CK * GW])
    pm = [m.ps("pm0"), m.ps("pm1")]
    pb = m.ps("pb")
    po = [m.ps(f"po{k}") for k in range(4)]
    ga = m.counter("ga")
    ch, m_ready, mt_ready, mg_ready, back = (m.sem(x) for x in ("ch", "m_ready", "mt_ready", "mg_ready", "back"))
    df_ready, fac_ready, po_ready, po_free, tot_ready, st = (m.sem(x) for x in ("df_ready", "fac_ready", "po_ready", "po_free", "tot_ready", "st"))
    eq_ready = [m.sem("eq_ready0"), m.sem("eq_ready1")]
    eq_free = [m.sem("eq_free0"), m.sem("eq_free1")]
    r3 = R[:, :].rearrange("p (k w) -> p k w", w=GW)
    t3 = tot[:, :].rearrange("p (k w) -> p k w", w=GW)
    kh = lambda x: x[:, :].rearrange("p (k h) -> p k h", h=HEADS)

    @block.gpsimd
    def _(e):
        for k in range(CK):
            e.indirect_dma_start(out=R[:, k * GW:(k + 1) * GW], out_offset=None, in_=sums[:, :],
                                 in_offset=bass.IndirectOffsetOnAxis(ap=ed.first_row[:, k:k + 1], axis=0)).then_inc(ga, 16)

    @block.vector
    def _(e):
        v = nc.vector
        c = Count(e, ch)
        v.tensor_scalar(mc[:, :], ed.cont[:, :], BIG, -BIG, ALU.mult, ALU.add).then_inc(ch, 1)
        e.wait_ge(ch, c.next())
        e.wait_ge(ga, 16 * CK)
        v.tensor_tensor(out=r3[:, :, :], in0=r3[:, :, :], in1=ed.cont[:, :].unsqueeze(2).to_broadcast([CP, CK, GW]), op=ALU.mult).then_inc(ch, 1)
        e.wait_ge(ch, c.next())
        v.tensor_tensor(out=r3[:, :, ZW:GW], in0=r3[:, :, ZW:GW], in1=mc[:, :].unsqueeze(2).to_broadcast([CP, CK, HEADS]), op=ALU.add).then_inc(ch, 1)
        e.wait_ge(ch, c.next())
        e.sem_inc(m_ready, 1)
        e.wait_ge(mt_ready, 1)
        e.sem_inc(mt_ready, -1)
        mv = mt[:, :].rearrange("h (p k) -> h k p", k=CK)
        for a in range(2):
            v.tensor_copy(mv[:, 4 * a:4 * a + 4, :], pm[a][:HEADS, :].rearrange("h (k p) -> h k p", k=4)[:, :, 0:CP]).then_inc(ch, 1)
            e.wait_ge(ch, c.next())
        v.tensor_tensor_scan(out=fw[:, :], data0=ed.group_mask[:, 0:C], data1=mt[:, :], initial=-BIG, op0=ALU.min, op1=ALU.max).then_inc(ch, 1)
        e.wait_ge(ch, c.next())
        v.tensor_tensor_scan(out=bw[:, ::-1], data0=ed.group_mask[:, C:0:-1], data1=mt[:, ::-1], initial=-BIG, op0=ALU.min, op1=ALU.max).then_inc(ch, 1)
        e.wait_ge(ch, c.next())
        v.tensor_tensor(out=fw[:, :], in0=fw[:, :], in1=bw[:, :], op=ALU.max).then_inc(ch, 1)
        e.wait_ge(ch, c.next())
        e.sem_inc(mg_ready, 1)
        e.wait_ge(back, 1)
        e.sem_inc(back, -1)
        v.tensor_copy(mg[:, :], pb[:CP, 0:CK * HEADS]).then_inc(ch, 1)
        e.wait_ge(ch, c.next())
        v.tensor_tensor(out=kh(df), in0=r3[:, :, ZW:GW], in1=kh(mg), op=ALU.subtract).then_inc(ch, 1)
        e.wait_ge(ch, c.next())
        e.sem_inc(df_ready, 1)
        e.wait_ge(fac_ready, 1)
        e.sem_inc(fac_ready, -1)
        v.tensor_tensor(out=r3[:, :, D:ZW], in0=r3[:, :, D:ZW], in1=kh(fac), op=ALU.mult).then_inc(ch, 1)
        e.wait_ge(ch, c.next())
        v.tensor_tensor(out=r3[:, :, 0:D].rearrange("p k (h o) -> p k h o", h=HEADS),
                        in0=r3[:, :, 0:D].rearrange("p k (h o) -> p k h o", h=HEADS),
                        in1=kh(fac).unsqueeze(3).to_broadcast([CP, CK, HEADS, DO]), op=ALU.mult).then_inc(ch, 1)
        e.wait_ge(ch, c.next())
        v.tensor_copy(t3[:, :, ZW:GW], kh(mg)).then_inc(ch, 1)
        e.wait_ge(ch, c.next())
        for half in range(2):
            for k in range(CK):
                if half or k >= 2:
                    e.wait_ge(eq_free[k % 2], 1)
                    e.sem_inc(eq_free[k % 2], -1)
                v.tensor_scalar(same[:, k % 2, :], ed.first_all[:, :], ed.first_nodef[:, k:k + 1], None, ALU.is_equal).then_inc(eq_ready[k % 2], 1)
            e.wait_ge(po_ready, 1)
            e.sem_inc(po_ready, -1)
            for q in range(4):
                v.tensor_copy(t3[:, half * 4 + q, 0:ZW], po[q][:CP, 0:ZW]).then_inc(ch, 1)
                e.wait_ge(ch, c.next())
            e.sem_inc(po_free, 1)
        e.sem_inc(tot_ready, 1)
        c.reset()

    @block.scalar
    def _(e):
        e.wait_ge(df_ready, 1)
        e.sem_inc(df_ready, -1)
        nc.scalar.activation(fac[:, :], df[:, :], ACT.Exp).then_inc(fac_ready, 1)

    @block.tensor
    def _(e):
        t = nc.tensor
        e.wait_ge(m_ready, 1)
        e.sem_inc(m_ready, -1)
        for k in range(CK):
            ins = t.transpose(pm[k // 4][:HEADS, (k % 4) * 128:(k % 4) * 128 + CP], r3[:, k, ZW:GW], const.ident[:CP, :CP])
        ins.then_inc(mt_ready, 1)
        e.wait_ge(mg_ready, 1)
        e.sem_inc(mg_ready, -1)
        gv = fw[:, :].rearrange("h (p k) -> h k p", k=CK)
        for k in range(CK):
            ins = t.transpose(pb[:CP, k * HEADS:(k + 1) * HEADS], gv[:, k, :], const.ident[:HEADS, :HEADS])
        ins.then_inc(back, 1)
        for half in range(2):
            if half:
                e.wait_ge(po_free, 1)
                e.sem_inc(po_free, -1)
            for k in range(CK):
                e.wait_ge(eq_ready[k % 2], 1)
                e.sem_inc(eq_ready[k % 2], -1)
                sv = same[:, k % 2, :].rearrange("p (c k) -> p k c", k=CK)
                for q in range(4):
                    ins = t.matmul(po[q][:CP, 0:ZW], sv[:, half * 4 + q, :], r3[:, k, 0:ZW], start=k == 0, stop=k == CK - 1)
                if k == CK - 1:
                    ins.then_inc(po_ready, 1)
                elif not (half and k >= CK - 2):
                    ins.then_inc(eq_free[k % 2], 1)
            if not half:
                e.sem_inc(eq_free[1], 1)

    @block.sync
    def _(e):
        e.wait_ge(tot_ready, 1)
        e.sem_inc(tot_ready, -1)
        e.dma_start(extras.rearrange("(p k) w -> p (k w)", k=CK), tot[:, :]).then_inc(st, 16)
        e.wait_ge(st, 16)
        e.sem_inc(st, -16)
        e.sem_inc(extras_stored, 1)


def gat_merge(nc, stage, const, ed, X, sums, extras, row_stats, zt=None, edn=None, slope=None):
    G = 5
    SL = 5
    NP = 3 if zt is not None else 2
    with Mem(nc, stage) as m, Mem(nc, stage + "x") as mx_:
        part = [m.sb(f"part{i}", [P, SL, G * GW]) for i in range(NP)]
        mx = m.sb("mx", [P, SL, G * HEADS])
        df = m.sb("df", [P, SL, NP, G * HEADS])
        fac = m.sb("fac", [P, SL, NP, G * HEADS])
        den = m.sb("den", [P, SL, G * HEADS])
        idx = m.sb("idx", [P, SL, 2, G], I32)
        ch, df_ready, fac_ready, weighed, extras_stored = (m.sem(x) for x in ("ch", "df_ready", "fac_ready", "weighed", "extras_stored"))
        share_ready = m.sem("share_ready")
        S = {n: [m.sem(f"{n}{b}") for b in range(SL)] for n in ("ready", "self_ld", "self_free")}
        S["ga"] = [m.counter(f"ga{b}") for b in range(SL)]
        h4 = lambda x: x.rearrange("p (k w) -> p k w", w=GW)
        gh = lambda x: x.rearrange("p (k h) -> p k h", h=HEADS)
        n_steps = T // G

        def prefill(s, b):
            for n in range(2):
                nc.vector.memset(h4(part[n][:, b, :])[:, :, ZW:GW], -BIG)
            nc.vector.tensor_copy(idx[:, b, 0, :], ed.main_row[:, bass.ds(s * G, G)])
            nc.vector.tensor_copy(idx[:, b, 1, :], ed.extra_row[:, bass.ds(s * G, G)]).then_inc(S["ready"][b], 1)
        with nc.Block() as block:

            @block.vector
            def _(e):
                for b in range(SL):
                    for n in range(2):
                        nc.vector.memset(h4(part[n][:, b, :])[:, :, 0:ZW], 0.0)
                    prefill(b, b)

            gat_extras(nc, mx_, block, const, ed, sums, extras, extras_stored)

            @block.gpsimd
            def _(e):
                def gather(b, s, table, rows):
                    for k in range(G):
                        e.indirect_dma_start(out=part[s][:, b, k * GW:(k + 1) * GW], out_offset=None, in_=table[:, :],
                                             in_offset=bass.IndirectOffsetOnAxis(ap=idx[:, b, s, k:k + 1], axis=0),
                                             bounds_check=rows - 1, oob_is_err=False).then_inc(S["ga"][b], 16)
                for b in range(SL):
                    e.wait_ge(S["ready"][b], 1)
                    e.sem_inc(S["ready"][b], -1)
                    gather(b, 0, sums, NB * P * BC)
                e.wait_ge(extras_stored, 1)
                e.sem_inc(extras_stored, -1)
                for b in range(SL):
                    gather(b, 1, extras, C)
                with e.Fori(1, n_steps // SL) as i:
                    for b in range(SL):
                        e.wait_ge(S["ready"][b], 1)
                        e.sem_inc(S["ready"][b], -1)
                        gather(b, 0, sums, NB * P * BC)
                        gather(b, 1, extras, C)

            if zt is not None:
                @block.sync
                def _(e):
                    zt_v = zt.rearrange("(p t) w -> p t w", t=T)
                    for b in range(SL):
                        e.sem_inc(S["self_free"][b], 1)
                    with e.Fori(0, n_steps // SL) as i:
                        for b in range(SL):
                            e.wait_ge(S["self_free"][b], 1)
                            e.sem_inc(S["self_free"][b], -1)
                            e.dma_start(h4(part[2][:, b, :])[:, :, 0:ZW], zt_v[:, bass.ds(i * (SL * G) + b * G, G), :]).then_inc(S["self_ld"][b], 16)

            @block.scalar
            def _(e):
                def factors(b):
                    e.wait_ge(df_ready, 1)
                    e.sem_inc(df_ready, -1)
                    nc.scalar.activation(fac[:, b, :, :], df[:, b, :, :], ACT.Exp).then_inc(fac_ready, 1)

                def weigh(b):
                    e.wait_ge(share_ready, 1)
                    e.sem_inc(share_ready, -1)
                    for n in range(1, NP):
                        for k in range(G):
                            for h in range(HEADS):
                                rows = part[n][:, b, k * GW + h * DO:k * GW + (h + 1) * DO]
                                ins = nc.scalar.activation(rows, rows, ACT.Copy, scale=fac[:, b, n, k * HEADS + h:k * HEADS + h + 1])
                    ins.then_inc(weighed, 1)
                factors(0)
                with e.Fori(0, n_steps // SL - 1) as i:
                    for b in range(SL):
                        factors((b + 1) % SL)
                        weigh(b)
                for b in range(SL):
                    if b + 1 < SL:
                        factors(b + 1)
                    weigh(b)

            @block.vector
            def _(e):
                v = nc.vector
                c = Count(e, ch)

                def maxima(i, b):
                    i, b = i + b // SL, b % SL
                    e.wait_ge(S["ga"][b], i * (16 * 2 * G) + 16 * 2 * G)
                    p3 = [h4(part[n][:, b, :]) for n in range(NP)]
                    M = gh(mx[:, b, :])
                    v.scalar_tensor_tensor(M, p3[0][:, :, ZW:GW], -0.1 * BIG, p3[1][:, :, ZW:GW], ALU.max, ALU.max).then_inc(ch, 1)
                    e.wait_ge(ch, c.next())
                    if zt is not None:
                        e.wait_ge(S["self_ld"][b], 16)
                        e.sem_inc(S["self_ld"][b], -16)
                        s = i * SL + b
                        v.tensor_tensor(out=p3[2][:, :, ZW:GW], in0=p3[2][:, :, D:ZW], in1=gh(edn[:, bass.ds(s * (G * HEADS), G * HEADS)]), op=ALU.add).then_inc(ch, 1)
                        e.wait_ge(ch, c.next())
                        v.scalar_tensor_tensor(p3[2][:, :, ZW:GW], p3[2][:, :, ZW:GW], slope, p3[2][:, :, ZW:GW], ALU.mult, ALU.max).then_inc(ch, 1)
                        e.wait_ge(ch, c.next())
                        v.tensor_tensor(out=M, in0=M, in1=p3[2][:, :, ZW:GW], op=ALU.max).then_inc(ch, 1)
                        e.wait_ge(ch, c.next())
                    for n in range(NP):
                        ins = v.tensor_tensor(out=gh(df[:, b, n, :]), in0=p3[n][:, :, ZW:GW], in1=M, op=ALU.subtract)
                    ins.then_inc(df_ready, 1)

                def shares(b):
                    b = b % SL
                    p3 = [h4(part[n][:, b, :]) for n in range(NP)]
                    e.wait_ge(fac_ready, 1)
                    e.sem_inc(fac_ready, -1)
                    for n in range(2):
                        ins = v.tensor_tensor(out=p3[n][:, :, D:ZW], in0=p3[n][:, :, D:ZW], in1=gh(fac[:, b, n, :]), op=ALU.mult)
                    ins.then_inc(ch, 1)
                    e.wait_ge(ch, c.next())
                    v.tensor_tensor(out=gh(den[:, b, :]), in0=p3[0][:, :, D:ZW], in1=p3[1][:, :, D:ZW], op=ALU.add).then_inc(ch, 1)
                    e.wait_ge(ch, c.next())
                    if NP == 3:
                        v.tensor_tensor(out=den[:, b, :], in0=den[:, b, :], in1=fac[:, b, 2, :], op=ALU.add).then_inc(ch, 1)
                        e.wait_ge(ch, c.next())
                    v.tensor_scalar(den[:, b, :], den[:, b, :], 1e-16, None, ALU.max).then_inc(ch, 1)
                    e.wait_ge(ch, c.next())
                    v.reciprocal(den[:, b, :], den[:, b, :]).then_inc(ch, 1)
                    e.wait_ge(ch, c.next())
                    v.tensor_tensor(out=fac[:, b, :, :], in0=fac[:, b, :, :], in1=den[:, b, :].unsqueeze(1).to_broadcast([P, NP, G * HEADS]), op=ALU.mult).then_inc(ch, 1)
                    e.wait_ge(ch, c.next())
                    e.sem_inc(share_ready, 1)

                def body(i, b, last):
                    s = i * SL + b
                    if not last or b + 2 < SL:
                        maxima(i, b + 2)
                    if not last or b + 1 < SL:
                        shares(b + 1)
                    p3 = [h4(part[n][:, b, :]) for n in range(NP)]
                    first = p3[0][:, :, 0:D].rearrange("p k (h o) -> p k h o", h=HEADS)
                    v.tensor_tensor(out=first, in0=first, in1=gh(fac[:, b, 0, :]).unsqueeze(3).to_broadcast([P, G, HEADS, DO]), op=ALU.mult).then_inc(ch, 1)
                    e.wait_ge(ch, c.next())
                    e.wait_ge(weighed, 1)
                    e.sem_inc(weighed, -1)
                    for n in range(1, NP):
                        v.tensor_tensor(out=p3[0][:, :, 0:D], in0=p3[0][:, :, 0:D], in1=p3[n][:, :, 0:D], op=ALU.add).then_inc(ch, 1)
                        e.wait_ge(ch, c.next())
                    xs = X[:, bass.ds(s * (G * D), G * D)].rearrange("p (k w) -> p k w", w=D)
                    v.tensor_tensor(out=xs, in0=xs, in1=p3[0][:, :, 0:D], op=ALU.add).then_inc(ch, 1)
                    e.wait_ge(ch, c.next())
                    if zt is not None:
                        e.sem_inc(S["self_free"][b], 1)
                    if not last:
                        prefill(s + SL, b)
                    for k in range(G):
                        v.bn_stats(out=row_stats[:, bass.ds(s * (G * 6) + k * 6, 6)], in_=X[:, bass.ds(s * (G * D) + k * D, D)])
                    c.reset()
                maxima(0, 0)
                maxima(0, 1)
                shares(0)
                c.reset()
                with e.Fori(0, n_steps // SL - 1) as i:
                    for b in range(SL):
                        body(i, b, False)
                for b in range(SL):
                    body(n_steps // SL - 1, b, True)


def mix0(nc, const, X, mean, rstd, qT, kv, a):
    Q = 2
    NS = T // Q
    with Mem(nc, "m0") as m:
        w1 = m.sb("w1", [128, 2, D])
        w2 = m.sb("w2", [128, 2, D])
        b1 = m.sb("b1", [128, 2])
        gb = m.sb("gb", [P, 5, D])
        nmean = m.sb("nmean", [P, T])
        qs = m.sb("qs", [128, 2, Q * 2 * P])
        xc = m.sb("xc", [P, 2, Q, D])
        xn = m.sb("xn", [P, 2, Q, D])
        at = m.sb("at", [P, Q, D])
        u = m.sb("u", [P, Q, D])
        u2 = m.sb("u2", [P, Q, D])
        x1 = m.sb("x1", [P, 2, Q, D])
        x1b = m.sb("x1b", [P, 2, Q, D])
        xT = m.sb("xT", [128, 2, Q * P])
        hT = m.sb("hT", [128, 2, 2, Q * P])
        den = m.sb("den", [P, Q, 8])
        stat = m.sb("stat", [P, 2, Q, 6])
        ms = m.sb("ms", [P, 2, Q, 3])
        half = m.sb("half", [P, Q])
        pt = m.ps("pt", [128, Q, 512])
        pT = m.ps("pT")
        ph = m.ps("ph")
        py = m.ps("py")
        names = ("nm_ready", "pt_ready", "pt_free", "x1_ready", "x1_for_sum", "x1b_ready", "xb_ready", "pT_ready", "xT_ready", "ph_ready", "hT_ready",
                 "py_ready", "py_free", "ch", "act_ch", "pool_ch", "ld")
        s = {n: m.sem(n) for n in names}
        S = {n: [m.sem(n + "0"), m.sem(n + "1")] for n in ("qs_ready", "qs_free", "xn_ready", "xn_free", "var_ready", "rstd_ready")}
        both = lambda n: gb[:, n, :].unsqueeze(1).to_broadcast([P, Q, D])
        xpair = lambda n: X[:, bass.ds(n * (Q * D), Q * D)].rearrange("p (q w) -> p q w", w=D)
        with nc.Block() as block:

            @block.sync
            def _(e):
                e.dma_start(w1[:, :, :], a["mix_w1"].rearrange("(b i) o -> i b o", b=2)).then_inc(s["ld"], 16)
                e.dma_start(w2[:, :, :], a["mix_w2"].rearrange("(b i) o -> i b o", b=2)).then_inc(s["ld"], 16)
                e.dma_start(b1[:, :], a["mix_b1"]).then_inc(s["ld"], 16)
                for n, name in enumerate(("L0_mix_ln1_g", "L0_mix_ln1_b", "L0_mix_b2", "L0_mix_ln2_g", "L0_mix_ln2_b")):
                    e.dma_start(gb[:, n, :], a[name].partition_broadcast(P)).then_inc(s["ld"], 16)

            @block.gpsimd
            def _(e):
                g = nc.gpsimd
                c = Count(e, s["pool_ch"])
                g.memset(half[:, :], -0.5).then_inc(c.sem, 1)
                e.wait_ge(s["pool_ch"], c.next())
                c.reset()
                def deviation(n):
                    e.wait_ge(S["var_ready"][n], 1)
                    e.sem_inc(S["var_ready"][n], -1)
                    g.tensor_scalar(ms[:, n, :, 1], ms[:, n, :, 1], 1e-5, None, ALU.add).then_inc(s["pool_ch"], 1)
                    e.wait_ge(s["pool_ch"], 1)
                    e.sem_inc(s["pool_ch"], -1)
                    g.tensor_tensor(out=ms[:, n, :, 2], in0=ms[:, n, :, 1], in1=half[:, :], op=ALU.pow).then_inc(S["rstd_ready"][n], 1)

                def turn(n, par, attend=True, finish=True, middle=True):
                    if middle:
                        e.wait_ge(s["x1_for_sum"], 1)
                        e.sem_inc(s["x1_for_sum"], -1)
                        g.tensor_tensor(out=x1b[:, par, :, :], in0=x1[:, par, :, :], in1=both(2), op=ALU.add).then_inc(s["x1b_ready"], 1)
                    if finish:
                        deviation(1)
                    if attend:
                        deviation(0)
                    if middle:
                        g.tensor_tensor(out=xpair(n), in0=xpair(n), in1=both(4), op=ALU.add).then_inc(s["xb_ready"], 1)
                deviation(0)
                e.wait_ge(s["ld"], 128)
                turn(0, 0, finish=False)
                with e.Fori(0, (NS - 3) // 2) as i:
                    turn(i * 2 + 1, 1)
                    turn(i * 2 + 2, 0)
                turn(NS - 2, 1)
                turn(NS - 1, 0, attend=False)
                turn(NS, 1, attend=False, middle=False)

            @block.tensor
            def _(e):
                t_ = nc.tensor
                e.sem_inc(s["pt_free"], 1)
                e.sem_inc(s["py_free"], 1)

                def attention(par):
                    e.wait_ge(S["qs_ready"][par], 1)
                    e.sem_inc(S["qs_ready"][par], -1)
                    e.wait_ge(s["pt_free"], 1)
                    e.sem_inc(s["pt_free"], -1)
                    for q in range(Q):
                        for b in range(2):
                            ins = t_.matmul(pt[:P, q, b * 132:(b + 1) * 132], qs[:, par, (q * 2 + b) * P:(q * 2 + b + 1) * P], kv[:, b * 132:(b + 1) * 132], start=True, stop=True)
                    ins.then_inc(s["pt_ready"], 1)

                def turn(par, attend=True, finish=True, middle=True):
                    if attend:
                        attention(1 - par)
                    if finish:
                        e.wait_ge(s["hT_ready"], 1)
                        e.sem_inc(s["hT_ready"], -1)
                        e.wait_ge(s["py_free"], 1)
                        e.sem_inc(s["py_free"], -1)
                        for q in range(Q):
                            for b in range(2):
                                ins = t_.matmul(py[:P, q * D:(q + 1) * D], hT[:, 1 - par, b, q * P:(q + 1) * P], w2[:, b, :], start=b == 0, stop=b == 1)
                        ins.then_inc(s["py_ready"], 1)
                    if middle:
                        e.wait_ge(s["x1_ready"], 1)
                        e.sem_inc(s["x1_ready"], -1)
                        for b in range(2):
                            for q in range(Q):
                                ins = t_.transpose(pT[:, (b * Q + q) * P:(b * Q + q + 1) * P], x1[:, par, q, b * 128:(b + 1) * 128], const.ident[:P, :P])
                        ins.then_inc(s["pT_ready"], 1)
                        e.wait_ge(s["xT_ready"], 1)
                        e.sem_inc(s["xT_ready"], -1)
                        for o in range(2):
                            for b in range(2):
                                ins = t_.matmul(ph[:, o * Q * P:(o + 1) * Q * P], w1[:, b, o * 128:(o + 1) * 128], xT[:, b, :], start=b == 0, stop=b == 1)
                        ins.then_inc(s["ph_ready"], 1)
                attention(0)
                e.wait_ge(s["ld"], 128)
                turn(0, finish=False)
                with e.Fori(0, (NS - 3) // 2) as i:
                    turn(1)
                    turn(0)
                turn(1)
                turn(0, attend=False)
                turn(1, attend=False, middle=False)

            @block.scalar
            def _(e):
                A = nc.scalar
                c = Count(e, s["act_ch"])
                for par in range(2):
                    e.sem_inc(S["xn_free"][par], 1)

                for par in range(2):
                    e.sem_inc(S["qs_free"][par], 1)

                def queries(n, par):
                    e.wait_ge(S["qs_free"][par], 1)
                    e.sem_inc(S["qs_free"][par], -1)
                    A.activation(qs[:, par, :], qT[:, bass.ds(n * (Q * 2 * P), Q * 2 * P)], ACT.Copy).then_inc(S["qs_ready"][par], 1)

                def normed(n, par):
                    e.wait_ge(S["xn_free"][par], 1)
                    e.sem_inc(S["xn_free"][par], -1)
                    for q in range(Q):
                        ins = A.activation(xc[:, par, q, :], X[:, bass.ds((n * Q + q) * D, D)], ACT.Identity, bias=nmean[:, bass.ds(n * Q + q, 1)])
                    ins.then_inc(s["act_ch"], 1)
                    e.wait_ge(s["act_ch"], c.next())
                    for q in range(Q):
                        ins = A.activation(xn[:, par, q, :], xc[:, par, q, :], ACT.Copy, scale=rstd[:, bass.ds(n * Q + q, 1)])
                    ins.then_inc(S["xn_ready"][par], 1)
                    c.reset()

                def turn(n, par, ahead=True):
                    if ahead:
                        queries(n + 2, par)
                        normed(n + 2, par)
                    e.wait_ge(s["pT_ready"], 1)
                    e.sem_inc(s["pT_ready"], -1)
                    A.activation(xT[:, :, :], pT[:, 0:2 * Q * P].rearrange("p (b n) -> p b n", b=2), ACT.Copy).then_inc(s["xT_ready"], 1)
                    e.wait_ge(s["ph_ready"], 1)
                    e.sem_inc(s["ph_ready"], -1)
                    for o in range(2):
                        ins = A.activation(hT[:, par, o, :], ph[:, o * Q * P:(o + 1) * Q * P], ACT.Gelu, bias=b1[:, o:o + 1])
                    ins.then_inc(s["hT_ready"], 1)
                e.wait_ge(s["nm_ready"], 1)
                e.sem_inc(s["nm_ready"], -1)
                for n in range(2):
                    queries(n, n)
                    normed(n, n)
                e.wait_ge(s["ld"], 128)
                with e.Fori(0, (NS - 3) // 2) as i:
                    turn(i * 2, 0)
                    turn(i * 2 + 1, 1)
                turn(NS - 3, 0)
                turn(NS - 2, 1, ahead=False)
                turn(NS - 1, 0, ahead=False)

            @block.vector
            def _(e):
                v = nc.vector
                c = Count(e, s["ch"])
                v.tensor_scalar(nmean[:, :], mean[:, :], -1.0, None, ALU.mult).then_inc(s["nm_ready"], 1)

                def stats(n, x):
                    for q in range(Q):
                        ins = v.bn_stats(out=stat[:, n, q, :], in_=x[:, q, :])
                    ins.then_inc(s["ch"], 1)
                    e.wait_ge(s["ch"], c.next())
                    for q in range(Q):
                        ins = v.bn_aggr(out=ms[:, n, q, 0:2], in_=stat[:, n, q, :])
                    ins.then_inc(S["var_ready"][n], 1)

                def norm(n, x, gamma):
                    e.wait_ge(S["rstd_ready"][n], 1)
                    e.sem_inc(S["rstd_ready"][n], -1)
                    for q in range(Q):
                        ins = v.scalar_tensor_tensor(x[:, q, :], x[:, q, :], ms[:, n, q, 0:1], gamma, ALU.subtract, ALU.mult)
                    ins.then_inc(s["ch"], 1)
                    e.wait_ge(s["ch"], c.next())

                def attend(par):
                    e.wait_ge(s["pt_ready"], 1)
                    e.sem_inc(s["pt_ready"], -1)
                    e.sem_inc(S["qs_free"][par], 1)
                    p4 = pt[:P, :, 0:264].rearrange("p q (b w) -> p q b w", w=132)
                    v.tensor_scalar(den[:, :, :].rearrange("p q (b g) -> p q b g", b=2), p4[:, :, :, 128:132], 1e-6, None, ALU.add).then_inc(s["ch"], 1)
                    e.wait_ge(s["ch"], c.next())
                    v.reciprocal(den[:, :, :], den[:, :, :]).then_inc(s["ch"], 1)
                    e.wait_ge(s["ch"], c.next())
                    for q in range(Q):
                        ins = v.tensor_tensor(out=at[:, q, :].rearrange("p (b g d) -> p b g d", b=2, g=4), in0=p4[:, q, :, 0:128].rearrange("p b (g d) -> p b g d", g=4),
                                              in1=den[:, q, :].rearrange("p (b g) -> p b g", b=2).unsqueeze(3).to_broadcast([P, 2, 4, 32]), op=ALU.mult)
                    ins.then_inc(s["ch"], 1)
                    e.wait_ge(s["ch"], c.next())
                    e.sem_inc(s["pt_free"], 1)
                    e.wait_ge(S["xn_ready"][par], 1)
                    e.sem_inc(S["xn_ready"][par], -1)
                    v.tensor_tensor(out=u[:, :, :], in0=xn[:, par, :, :], in1=at[:, :, :], op=ALU.add).then_inc(s["ch"], 1)
                    e.wait_ge(s["ch"], c.next())
                    e.sem_inc(S["xn_free"][par], 1)
                    stats(0, u)

                def attended(par):
                    norm(0, u, gb[:, 0, :])
                    for q in range(Q):
                        ins = v.scalar_tensor_tensor(x1[:, par, q, :], u[:, q, :], ms[:, 0, q, 2:3], gb[:, 1, :], ALU.mult, ALU.add)
                    ins.then_inc(s["ch"], 1)
                    e.wait_ge(s["ch"], c.next())
                    e.sem_inc(s["x1_ready"], 1)
                    e.sem_inc(s["x1_for_sum"], 1)

                def turn(n, par, att=True, finish=True):
                    if att:
                        attend(1 - par)
                    if finish:
                        e.wait_ge(s["py_ready"], 1)
                        e.sem_inc(s["py_ready"], -1)
                        e.wait_ge(s["x1b_ready"], 1)
                        e.sem_inc(s["x1b_ready"], -1)
                        v.tensor_tensor(out=u2[:, :, :], in0=py[:P, 0:Q * D].rearrange("p (q w) -> p q w", w=D), in1=x1b[:, 1 - par, :, :], op=ALU.add).then_inc(s["ch"], 1)
                        e.wait_ge(s["ch"], c.next())
                        e.sem_inc(s["py_free"], 1)
                        stats(1, u2)
                    if att:
                        attended(1 - par)
                    if finish:
                        norm(1, u2, gb[:, 3, :])
                        e.wait_ge(s["xb_ready"], 1)
                        e.sem_inc(s["xb_ready"], -1)
                        k = n - 1 if n is not None else NS - 1
                        for q in range(Q):
                            xt = X[:, bass.ds((k * Q + q) * D, D)]
                            ins = v.scalar_tensor_tensor(xt, u2[:, q, :], ms[:, 1, q, 2:3], xt, ALU.mult, ALU.add)
                        ins.then_inc(s["ch"], 1)
                        e.wait_ge(s["ch"], c.next())
                    c.reset()
                def full_turn(n, par):
                    a = 1 - par
                    e.wait_ge(s["pt_ready"], 1)
                    e.sem_inc(s["pt_ready"], -1)
                    e.sem_inc(S["qs_free"][a], 1)
                    p4 = pt[:P, :, 0:264].rearrange("p q (b w) -> p q b w", w=132)
                    v.tensor_scalar(den[:, :, :].rearrange("p q (b g) -> p q b g", b=2), p4[:, :, :, 128:132], 1e-6, None, ALU.add).then_inc(s["ch"], 1)
                    den_done = c.next()
                    e.wait_ge(s["py_ready"], 1)
                    e.sem_inc(s["py_ready"], -1)
                    e.wait_ge(s["x1b_ready"], 1)
                    e.sem_inc(s["x1b_ready"], -1)
                    v.tensor_tensor(out=u2[:, :, :], in0=py[:P, 0:Q * D].rearrange("p (q w) -> p q w", w=D), in1=x1b[:, a, :, :], op=ALU.add).then_inc(s["ch"], 1)
                    u2_done = c.next()
                    e.wait_ge(s["ch"], den_done)
                    v.reciprocal(den[:, :, :], den[:, :, :]).then_inc(s["ch"], 1)
                    inverse_done = c.next()
                    e.wait_ge(s["ch"], u2_done)
                    e.sem_inc(s["py_free"], 1)
                    for q in range(Q):
                        ins = v.bn_stats(out=stat[:, 1, q, :], in_=u2[:, q, :])
                    ins.then_inc(s["ch"], 1)
                    stat_done = c.next()
                    e.wait_ge(s["ch"], inverse_done)
                    for q in range(Q):
                        ins = v.tensor_tensor(out=at[:, q, :].rearrange("p (b g d) -> p b g d", b=2, g=4), in0=p4[:, q, :, 0:128].rearrange("p b (g d) -> p b g d", g=4),
                                              in1=den[:, q, :].rearrange("p (b g) -> p b g", b=2).unsqueeze(3).to_broadcast([P, 2, 4, 32]), op=ALU.mult)
                    ins.then_inc(s["ch"], 1)
                    at_done = c.next()
                    e.wait_ge(s["ch"], stat_done)
                    for q in range(Q):
                        ins = v.bn_aggr(out=ms[:, 1, q, 0:2], in_=stat[:, 1, q, :])
                    ins.then_inc(S["var_ready"][1], 1)
                    e.wait_ge(s["ch"], at_done)
                    e.sem_inc(s["pt_free"], 1)
                    e.wait_ge(S["xn_ready"][a], 1)
                    e.sem_inc(S["xn_ready"][a], -1)
                    v.tensor_tensor(out=u[:, :, :], in0=xn[:, a, :, :], in1=at[:, :, :], op=ALU.add).then_inc(s["ch"], 1)
                    e.wait_ge(s["ch"], c.next())
                    e.sem_inc(S["xn_free"][a], 1)
                    stats(0, u)
                    norm(1, u2, gb[:, 3, :])
                    e.wait_ge(s["xb_ready"], 1)
                    e.sem_inc(s["xb_ready"], -1)
                    for q in range(Q):
                        xt = X[:, bass.ds(((n - 1) * Q + q) * D, D)]
                        ins = v.scalar_tensor_tensor(xt, u2[:, q, :], ms[:, 1, q, 2:3], xt, ALU.mult, ALU.add)
                    ins.then_inc(s["ch"], 1)
                    c.next()
                    attended(a)
                    c.reset()
                attend(0)
                e.wait_ge(s["ld"], 128)
                attended(0)
                turn(0, 0, finish=False)
                with e.Fori(0, (NS - 3) // 2) as i:
                    full_turn(i * 2 + 1, 1)
                    full_turn(i * 2 + 2, 0)
                full_turn(NS - 2, 1)
                turn(NS - 1, 0, att=False)
                turn(None, 1, att=False)


NE = 8
CAP0 = 977
ER = 1000
F0, F1 = 1024, 512
FLT_MAX = 3.4028235e38


def moe_gate(nc, const, X, mean, rstd, XN, gw, gb, bufx, slot_idx, back_idx, wgt):
    with Mem(nc, "mg") as m:
        xs = m.sb("xs", [P, 2, 2 * D])
        xT = m.sb("xT", [128, 2, 4 * P])
        lg = m.sb("lg", [P, T * NE])
        pr = m.sb("pr", [P, T * NE])
        oh = m.sb("oh", [P, T * NE])
        ohT = m.sb("ohT", [P, NE * T])
        cum = m.sb("cum", [P, NE * T])
        rm = m.sb("rm", [P, NE * T])
        tk = m.sb("tk", [P, 6, T])
        tot = m.sb("tot", [P, NE])
        pT = [m.ps("pT0"), m.ps("pT1")]
        pl = [m.ps("pl0"), m.ps("pl1")]
        poff = m.ps("poff")
        names = ("ch", "lg_sub", "ex_done", "tot_ready", "off_ready", "slots")
        s = {n: m.sem(n) for n in names}
        s["sc"] = m.counter("sc")
        S = {n: [m.sem(n + "0"), m.sem(n + "1")] for n in ("xn_ready", "pT_ready", "xT_ready", "pl_ready", "pl_free", "xs_free")}
        with nc.Block() as block:

            @block.vector
            def _(e):
                v = nc.vector
                c = Count(e, s["ch"])

                for par in range(2):
                    e.sem_inc(S["xs_free"][par], 1)

                def norm(n, par):
                    e.wait_ge(S["xs_free"][par], 1)
                    e.sem_inc(S["xs_free"][par], -1)
                    for q in range(2):
                        ins = v.tensor_scalar(xs[:, par, q * D:(q + 1) * D], X[:, bass.ds(n * (2 * D) + q * D, D)], mean[:, bass.ds(n * 2 + q, 1)], rstd[:, bass.ds(n * 2 + q, 1)],
                                              ALU.subtract, ALU.mult)
                    ins.then_inc(S["xn_ready"][par], 1)

                def logits(n, par):
                    e.wait_ge(S["pl_ready"][par], 1)
                    e.sem_inc(S["pl_ready"][par], -1)
                    v.tensor_tensor(out=lg[:, bass.ds(n * (2 * NE), 2 * NE)].rearrange("p (q x) -> p q x", x=NE), in0=pl[par][:P, 0:2 * NE].rearrange("p (q x) -> p q x", x=NE),
                                    in1=gb[:, :].unsqueeze(1).to_broadcast([P, 2, NE]), op=ALU.add).then_inc(S["pl_free"][par], 1)
                NP2 = T // 2
                norm(0, 0)
                norm(1, 1)
                with e.Fori(0, (NP2 - 3) // 2) as i:
                    for par in range(2):
                        norm(i * 2 + par + 2, par)
                        logits(i * 2 + par, par)
                norm(NP2 - 1, 0)
                logits(NP2 - 3, 0)
                logits(NP2 - 2, 1)
                logits(NP2 - 1, 0)
                te = lambda x: x[:, :].rearrange("p (t e) -> p t e", e=NE)
                et = lambda x: x[:, :].rearrange("p (e t) -> p t e", e=NE)
                bc = lambda x: x.unsqueeze(2).to_broadcast([P, T, NE])
                v.memset(rm[:, :], 1.0).then_inc(s["ch"], 1)
                e.wait_ge(s["ch"], c.next())
                v.memset(rm[:, :].rearrange("p (e t) -> p e t", e=NE)[:, :, 0:1], 0.0).then_inc(s["ch"], 1)
                e.wait_ge(s["ch"], c.next())
                v.tensor_reduce(out=tk[:, 0, :], in_=te(lg), axis=AX.X, op=ALU.max).then_inc(s["ch"], 1)
                e.wait_ge(s["ch"], c.next())
                v.tensor_tensor(out=te(lg), in0=te(lg), in1=bc(tk[:, 0, :]), op=ALU.subtract).then_inc(s["ch"], 1)
                e.wait_ge(s["ch"], c.next())
                e.sem_inc(s["lg_sub"], 1)
                e.wait_ge(s["ex_done"], 1)
                e.sem_inc(s["ex_done"], -1)
                v.tensor_reduce(out=tk[:, 0, :], in_=te(pr), axis=AX.X, op=ALU.add).then_inc(s["ch"], 1)
                e.wait_ge(s["ch"], c.next())
                v.reciprocal(tk[:, 0, :], tk[:, 0, :]).then_inc(s["ch"], 1)
                e.wait_ge(s["ch"], c.next())
                v.tensor_tensor(out=te(pr), in0=te(pr), in1=bc(tk[:, 0, :]), op=ALU.mult).then_inc(s["ch"], 1)
                e.wait_ge(s["ch"], c.next())
                v.tensor_reduce(out=tk[:, 0, :], in_=te(pr), axis=AX.X, op=ALU.max).then_inc(s["ch"], 1)
                e.wait_ge(s["ch"], c.next())
                v.tensor_tensor(out=te(oh), in0=te(pr), in1=bc(tk[:, 0, :]), op=ALU.is_equal).then_inc(s["ch"], 1)
                e.wait_ge(s["ch"], c.next())
                v.tensor_scalar(oh[:, :], oh[:, :], -float(NE), float(NE), ALU.mult, ALU.add).then_inc(s["ch"], 1)
                e.wait_ge(s["ch"], c.next())
                ib = const.iota[:P, 0:NE].unsqueeze(1).to_broadcast([P, T, NE])
                v.tensor_tensor(out=te(oh), in0=te(oh), in1=ib, op=ALU.add).then_inc(s["ch"], 1)
                e.wait_ge(s["ch"], c.next())
                v.tensor_reduce(out=tk[:, 1, :], in_=te(oh), axis=AX.X, op=ALU.min).then_inc(s["ch"], 1)
                e.wait_ge(s["ch"], c.next())
                v.tensor_tensor(out=et(ohT), in0=ib, in1=bc(tk[:, 1, :]), op=ALU.is_equal).then_inc(s["ch"], 1)
                e.wait_ge(s["ch"], c.next())
                v.tensor_tensor_scan(out=cum[:, :], data0=rm[:, :], data1=ohT[:, :], initial=0.0, op0=ALU.mult, op1=ALU.add).then_inc(s["ch"], 1)
                e.wait_ge(s["ch"], c.next())
                v.tensor_copy(tot[:, :], cum[:, :].rearrange("p (e t) -> p e t", e=NE)[:, :, T - 1]).then_inc(s["ch"], 1)
                e.wait_ge(s["ch"], c.next())
                e.sem_inc(s["tot_ready"], 1)
                e.wait_ge(s["off_ready"], 1)
                e.sem_inc(s["off_ready"], -1)
                c3 = cum[:, :].rearrange("p (e t) -> p e t", e=NE)
                v.tensor_tensor(out=c3, in0=c3, in1=poff[:P, 0:NE].unsqueeze(2).to_broadcast([P, NE, T]), op=ALU.add).then_inc(s["ch"], 1)
                e.wait_ge(s["ch"], c.next())
                v.tensor_tensor(out=cum[:, :], in0=cum[:, :], in1=ohT[:, :], op=ALU.mult).then_inc(s["ch"], 1)
                e.wait_ge(s["ch"], c.next())
                v.tensor_reduce(out=tk[:, 2, :], in_=et(cum), axis=AX.X, op=ALU.add).then_inc(s["ch"], 1)
                e.wait_ge(s["ch"], c.next())
                v.tensor_scalar(tk[:, 3, :], tk[:, 2, :], float(CAP0), None, ALU.is_le).then_inc(s["ch"], 1)
                e.wait_ge(s["ch"], c.next())
                v.tensor_tensor(out=wgt[:, :], in0=tk[:, 0, :], in1=tk[:, 3, :], op=ALU.mult).then_inc(s["ch"], 1)
                e.wait_ge(s["ch"], c.next())
                v.tensor_scalar(tk[:, 4, :], tk[:, 2, :], float(CAP0), -1.0, ALU.min, ALU.add).then_inc(s["ch"], 1)
                e.wait_ge(s["ch"], c.next())
                v.scalar_tensor_tensor(tk[:, 4, :], tk[:, 1, :], float(ER), tk[:, 4, :], ALU.mult, ALU.add).then_inc(s["ch"], 1)
                e.wait_ge(s["ch"], c.next())
                v.tensor_copy(back_idx[:, :], tk[:, 4, :]).then_inc(s["ch"], 1)
                e.wait_ge(s["ch"], c.next())
                v.tensor_scalar(tk[:, 5, :], tk[:, 3, :], -OOB, OOB, ALU.mult, ALU.add).then_inc(s["ch"], 1)
                e.wait_ge(s["ch"], c.next())
                v.tensor_tensor(out=tk[:, 5, :], in0=tk[:, 5, :], in1=tk[:, 4, :], op=ALU.add).then_inc(s["ch"], 1)
                e.wait_ge(s["ch"], c.next())
                v.tensor_copy(slot_idx[:, :], tk[:, 5, :]).then_inc(s["ch"], 1)
                e.wait_ge(s["ch"], c.next())
                e.wait_ge(S["xs_free"][0], 1)
                e.sem_inc(S["xs_free"][0], -1)
                e.wait_ge(S["xs_free"][1], 1)
                e.sem_inc(S["xs_free"][1], -1)
                e.sem_inc(s["slots"], 1)
                c.reset()

            @block.scalar
            def _(e):
                def body(n, par):
                    e.wait_ge(S["pT_ready"][par], 1)
                    e.sem_inc(S["pT_ready"][par], -1)
                    nc.scalar.activation(xT[:, par, :], pT[par][:, 0:4 * P], ACT.Copy).then_inc(S["xT_ready"][par], 1)
                    nc.scalar.activation(XN[:, bass.ds(n * (2 * D), 2 * D)], xs[:, par, :], ACT.Copy).then_inc(S["xs_free"][par], 1)
                steps(e, T // 2, body)
                e.wait_ge(s["lg_sub"], 1)
                e.sem_inc(s["lg_sub"], -1)
                nc.scalar.activation(pr[:, :], lg[:, :], ACT.Exp).then_inc(s["ex_done"], 1)

            @block.tensor
            def _(e):
                t_ = nc.tensor
                e.sem_inc(S["pl_free"][0], 1)
                e.sem_inc(S["pl_free"][1], 1)

                def transposes(par):
                    e.wait_ge(S["xn_ready"][par], 1)
                    e.sem_inc(S["xn_ready"][par], -1)
                    for q in range(2):
                        for b in range(2):
                            ins = t_.transpose(pT[par][:, (q * 2 + b) * P:(q * 2 + b + 1) * P], xs[:, par, q * D + b * 128:q * D + (b + 1) * 128], const.ident[:P, :P])
                    ins.then_inc(S["pT_ready"][par], 1)

                def body(par, last=False):
                    if not last:
                        transposes(1 - par)
                    e.wait_ge(S["xT_ready"][par], 1)
                    e.sem_inc(S["xT_ready"][par], -1)
                    e.wait_ge(S["pl_free"][par], 1)
                    e.sem_inc(S["pl_free"][par], -1)
                    for q in range(2):
                        for b in range(2):
                            ins = t_.matmul(pl[par][:P, q * NE:(q + 1) * NE], xT[:, par, (q * 2 + b) * P:(q * 2 + b + 1) * P], gw[:, b, :], start=b == 0, stop=b == 1)
                    ins.then_inc(S["pl_ready"][par], 1)
                transposes(0)
                with e.Fori(0, (T // 2 - 1) // 2) as i:
                    body(0)
                    body(1)
                body(0, last=True)
                e.wait_ge(s["tot_ready"], 1)
                e.sem_inc(s["tot_ready"], -1)
                t_.matmul(poff[:P, 0:NE], const.tri[:P, :P], tot[:, :], start=True, stop=True).then_inc(s["off_ready"], 1)

            @block.gpsimd
            def _(e):
                e.wait_ge(s["slots"], 1)
                e.sem_inc(s["slots"], -1)
                for t in range(T):
                    e.indirect_dma_start(out=bufx[:, :], out_offset=bass.IndirectOffsetOnAxis(ap=slot_idx[:, t:t + 1], axis=0),
                                         in_=XN[:, t * D:(t + 1) * D], in_offset=None, bounds_check=NE * ER - 1, oob_is_err=False).then_inc(s["sc"], 16)
                e.wait_ge(s["sc"], 16 * T)


def moe_experts(nc, const, bufx, bufy, w1, w2, b1, b2):
    NF = F0 // 128
    R = 4 * P
    with Mem(nc, "me") as m:
        w1s = m.sb("w1", [128, 2, 2 * F0])
        w2s = m.sb("w2", [128, 2, NF * D])
        b1s = m.sb("b1", [128, NE * NF])
        b2s = m.sb("b2", [P, NE * D])
        xr = m.sb("xr", [P, 2, 4 * D])
        xT = m.sb("xT", [128, 2, R])
        hT = m.sb("hT", [128, NF, R])
        yr = m.sb("yr", [P, 2, 4 * D])
        pT = [m.ps("pT0"), m.ps("pT1")]
        ph = [m.ps(f"ph{i}") for i in range(3)]
        py = [m.ps(f"py{i}") for i in range(2)]
        S = {n: [m.sem(n + "0"), m.sem(n + "1")] for n in ("w_ld", "w_free", "x_ld", "x_free", "y_ready", "y_free", "py_ready", "py_free", "pT_ready")}
        S["y_st"] = [m.counter("y_st0"), m.counter("y_st1")]
        ph_ready, ph_free = [m.sem(f"ph_ready{i}") for i in range(3)], [m.sem(f"ph_free{i}") for i in range(3)]
        xT_ready, bld = m.sem("xT_ready"), m.sem("bld")
        xv = bufx.rearrange("(s p q) d -> (s p) (q d)", s=2 * NE, q=4)
        yv = bufy.rearrange("(s p q) d -> (s p) (q d)", s=2 * NE, q=4)
        with nc.Block() as block:

            @block.sync
            def _(e):
                for b in range(2):
                    e.sem_inc(S["w_free"][b], 1)
                    e.sem_inc(S["x_free"][b], 1)

                def weights(x, p):
                    e.wait_ge(S["w_free"][p], 1)
                    e.sem_inc(S["w_free"][p], -1)
                    e.dma_start(w1s[:, p, :].rearrange("p (b f) -> p b f", b=2), w1[bass.ds(x * D, D), :].rearrange("(b i) f -> i b f", b=2)).then_inc(S["w_ld"][p], 16)
                    e.dma_start(w2s[:, p, :].rearrange("p (g d) -> p g d", d=D), w2[bass.ds(x * F0, F0), :].rearrange("(g f) d -> f g d", f=128)).then_inc(S["w_ld"][p], 16)

                def body(x, p, last=False):
                    for h in range(2):
                        e.wait_ge(S["x_free"][h], 1)
                        e.sem_inc(S["x_free"][h], -1)
                        e.dma_start(xr[:, h, :], xv[bass.ds((x * 2 + h) * P, P), :]).then_inc(S["x_ld"][h], 16)
                    if not last:
                        weights(x + 1, 1 - p)
                weights(0, 0)
                e.dma_start(b1s[:, :], b1).then_inc(bld, 16)
                e.dma_start(b2s[:, :], b2.rearrange("e d -> (e d)").partition_broadcast(P)).then_inc(bld, 16)
                with e.Fori(0, NE // 2 - 1) as i:
                    body(i * 2, 0)
                    body(i * 2 + 1, 1)
                body(NE - 2, 0)
                body(NE - 1, 1, last=True)

            @block.tensor
            def _(e):
                t = nc.tensor
                for q in S["py_free"] + ph_free:
                    e.sem_inc(q, 1)

                def transposes(h):
                    e.wait_ge(S["x_ld"][h], 16)
                    e.sem_inc(S["x_ld"][h], -16)
                    for b in range(2):
                        for q in range(4):
                            ins = t.transpose(pT[b][:, q * P:(q + 1) * P], xr[:, h, q * D + b * 128:q * D + b * 128 + 128], const.ident[:P, :P])
                        ins.then_inc(S["pT_ready"][b], 1)

                def half(p, h, first=False, last=False):
                    e.wait_ge(xT_ready, 2)
                    e.sem_inc(xT_ready, -2)
                    for f in range(NF):
                        if f >= 3 or first:
                            e.wait_ge(ph_free[f % 3], 1)
                            e.sem_inc(ph_free[f % 3], -1)
                        for b in range(2):
                            ins = t.matmul(ph[f % 3][:, 0:R], w1s[:, p, b * F0 + f * 128:b * F0 + f * 128 + 128], xT[:, b, :], start=b == 0, stop=b == 1)
                        ins.then_inc(ph_ready[f % 3], 1)
                    if not last:
                        transposes(1 - h)
                    for q in range(4):
                        e.wait_ge(S["py_free"][q % 2], 1)
                        e.sem_inc(S["py_free"][q % 2], -1)
                        for f in range(NF):
                            if q == 0 and f >= NF - 3:
                                e.wait_ge(ph_free[f % 3], 1)
                                e.sem_inc(ph_free[f % 3], -1)
                            ins = t.matmul(py[q % 2][:P, 0:D], hT[:, f, q * P:(q + 1) * P], w2s[:, p, f * D:(f + 1) * D], start=f == 0, stop=f == NF - 1)
                        ins.then_inc(S["py_ready"][q % 2], 1)

                def expert(p, first=False, last=False):
                    e.wait_ge(S["w_ld"][p], 32)
                    e.sem_inc(S["w_ld"][p], -32)
                    half(p, 0, first=first)
                    half(p, 1, last=last)
                transposes(0)
                expert(0, first=True)
                expert(1)
                with e.Fori(0, NE // 2 - 2) as i:
                    expert(0)
                    expert(1)
                expert(0)
                expert(1, last=True)

            @block.scalar
            def _(e):
                a = nc.scalar

                def transposed(h):
                    for b in range(2):
                        e.wait_ge(S["pT_ready"][b], 1)
                        e.sem_inc(S["pT_ready"][b], -1)
                        if b == 1:
                            e.sem_inc(S["x_free"][h], 1)
                        a.activation(xT[:, b, :], pT[b][:, 0:R], ACT.Copy).then_inc(xT_ready, 1)

                def half(x, h, last=False):
                    for f in range(NF):
                        e.wait_ge(ph_ready[f % 3], 1)
                        e.sem_inc(ph_ready[f % 3], -1)
                        a.activation(hT[:, f, :], ph[f % 3][:, 0:R], ACT.Relu, bias=b1s[:, bass.ds(x * NF + f, 1)]).then_inc(ph_free[f % 3], 1)
                    if not last:
                        transposed(1 - h)
                transposed(0)
                e.wait_ge(bld, 32)
                with e.Fori(0, NE - 1) as x:
                    half(x, 0)
                    half(x, 1)
                half(NE - 1, 0)
                half(NE - 1, 1, last=True)

            @block.vector
            def _(e):
                v = nc.vector
                e.wait_ge(bld, 32)
                for b in range(2):
                    e.sem_inc(S["y_free"][b], 1)

                def body(x, p):
                    for h in range(2):
                        e.wait_ge(S["y_free"][h], 1)
                        e.sem_inc(S["y_free"][h], -1)
                        for q in range(4):
                            e.wait_ge(S["py_ready"][q % 2], 1)
                            e.sem_inc(S["py_ready"][q % 2], -1)
                            if q == 3 and h == 1:
                                e.sem_inc(S["w_free"][p], 1)
                            ins = v.tensor_tensor(out=yr[:, h, q * D:(q + 1) * D], in0=py[q % 2][:P, 0:D], in1=b2s[:, bass.ds(x * D, D)], op=ALU.add)
                            ins.then_inc(S["py_free"][q % 2], 1)
                        e.drain().then_inc(S["y_ready"][h], 1)
                steps(e, NE, body)

            @block.gpsimd
            def _(e):
                def body(x, p):
                    for h in range(2):
                        e.wait_ge(S["y_ready"][h], 1)
                        e.sem_inc(S["y_ready"][h], -1)
                        e.dma_start(yv[bass.ds((x * 2 + h) * P, P), :], yr[:, h, :]).then_inc(S["y_st"][h], 16)
                        e.wait_ge(S["y_st"][h], x * 16 + 16)
                        e.sem_inc(S["y_free"][h], 1)
                steps(e, NE, body)


def moe_return(nc, X, bufy, back_idx, wgt, row_stats):
    G = 5
    SL = 5
    with Mem(nc, "mr") as m:
        y = m.sb("y", [P, SL, G * D])
        mk = m.sb("mk", [P, G * D])
        over = m.sb("over", [P, G * D])
        under = m.sb("under", [P, G * D])
        idx = m.sb("idx", [P, SL, G], I32)
        ch = m.sem("ch")
        ready = [m.sem(f"ready{b}") for b in range(SL)]
        weighed = [m.sem(f"weighed{b}") for b in range(SL)]
        ga = [m.counter(f"ga{b}") for b in range(SL)]
        n_turns = T // G // SL
        with nc.Block() as block:

            @block.gpsimd
            def _(e):
                with e.Fori(0, n_turns) as i:
                    for b in range(SL):
                        e.wait_ge(ready[b], 1)
                        e.sem_inc(ready[b], -1)
                        for k in range(G):
                            e.indirect_dma_start(out=y[:, b, k * D:(k + 1) * D], out_offset=None, in_=bufy[:, :],
                                                 in_offset=bass.IndirectOffsetOnAxis(ap=idx[:, b, k:k + 1], axis=0)).then_inc(ga[b], 16)

            @block.scalar
            def _(e):
                with e.Fori(0, n_turns) as i:
                    for b in range(SL):
                        e.wait_ge(ga[b], i * (16 * G) + 16 * G)
                        for k in range(G):
                            rows = y[:, b, k * D:(k + 1) * D]
                            ins = nc.scalar.activation(rows, rows, ACT.Copy, scale=wgt[:, bass.ds(i * (SL * G) + b * G + k, 1)])
                        ins.then_inc(weighed[b], 1)

            @block.vector
            def _(e):
                v = nc.vector
                c = Count(e, ch)

                def stage(s, b):
                    v.tensor_copy(idx[:, b, :], back_idx[:, bass.ds(s * G, G)]).then_inc(ready[b], 1)

                def body(i, b, last):
                    s = i * SL + b
                    e.wait_ge(weighed[b], 1)
                    e.sem_inc(weighed[b], -1)
                    yb = y[:, b, :]
                    v.tensor_scalar(over[:, :], yb, FLT_MAX, None, ALU.is_gt)
                    v.tensor_scalar(mk[:, :], yb, 0.0, 0.0, ALU.mult, ALU.is_equal)
                    v.tensor_scalar(under[:, :], yb, -FLT_MAX, -10000.0, ALU.is_lt, ALU.mult).then_inc(ch, 1)
                    e.wait_ge(ch, c.next())
                    v.scalar_tensor_tensor(over[:, :], over[:, :], 10000.0, under[:, :], ALU.mult, ALU.add).then_inc(ch, 1)
                    e.wait_ge(ch, c.next())
                    v.copy_predicated(over[:, :], mk[:, :].bitcast(I32), yb).then_inc(ch, 1)
                    e.wait_ge(ch, c.next())
                    if not last:
                        stage(s + SL, b)
                    xs = X[:, bass.ds(s * (G * D), G * D)]
                    v.tensor_tensor(out=xs, in0=xs, in1=over[:, :], op=ALU.add).then_inc(ch, 1)
                    e.wait_ge(ch, c.next())
                    for k in range(G):
                        v.bn_stats(out=row_stats[:, bass.ds(s * (G * 6) + k * 6, 6)], in_=X[:, bass.ds(s * (G * D) + k * D, D)])
                    c.reset()
                for b in range(SL):
                    stage(b, b)
                with e.Fori(0, n_turns - 1) as i:
                    for b in range(SL):
                        body(i, b, False)
                for b in range(SL):
                    body(n_turns - 1, b, True)


VW = D + 1


def dense1(nc, const, ed, X, mean, rstd, wz, wk, wv, bkv, zt, edt, edn, edge_ed, KS, VS, kmax, xT_dram):
    with Mem(nc, "d1") as m:
        xn = m.sb("xn", [P, 2, D])
        xT = m.sb("xT", [128, 2, 2 * P])
        zr = m.sb("zr", [P, 2, ZW + HEADS])
        xo = m.sb("xo", [128, 2, 2 * P])
        pT = m.ps("pT")
        pz, pkv = m.ps("pz"), [m.ps("pkv0"), m.ps("pkv1")]
        S = {n: [m.sem(n + "0"), m.sem(n + "1")] for n in
             ("xn_ready", "xn_free", "zr_ready", "zr_free", "zr_stored", "pkv_ready", "pkv_free", "xo_ready", "xo_stored", "xo_free")}
        pT_ready, xT_ready, ch, pz_ready, pz_free, ed_done, edst, row_ready = (
            m.sem(x) for x in ("pT_ready", "xT_ready", "ch", "pz_ready", "pz_free", "ed_done", "edst", "row_ready"))
        scattered = m.counter("scattered")
        zt_v = zt.rearrange("(p t) w -> p (t w)", t=T)
        with nc.Block() as block:

            @block.vector
            def _(e):
                v = nc.vector
                c = Count(e, ch)
                v.memset(VS[:, :].rearrange("p (t w) -> p t w", w=VW)[:, :, D:VW], 1.0).then_inc(ch, 1)
                e.wait_ge(ch, c.next())
                v.memset(kmax[:, :], -FLT_MAX).then_inc(ch, 1)
                e.wait_ge(ch, c.next())
                for par in range(2):
                    e.sem_inc(S["xn_free"][par], 1)
                c.reset()

                def norm(t, par):
                    e.wait_ge(S["xn_free"][par], 1)
                    e.sem_inc(S["xn_free"][par], -1)
                    v.tensor_scalar(xn[:, par, :], X[:, bass.ds(t * D, D)], mean[:, bass.ds(t, 1)], rstd[:, bass.ds(t, 1)],
                                    ALU.subtract, ALU.mult).then_inc(S["xn_ready"][par], 1)

                def keep(t, par):
                    e.wait_ge(S["pkv_ready"][par], 1)
                    e.sem_inc(S["pkv_ready"][par], -1)
                    k = KS[:, bass.ds(t * D, D)]
                    v.tensor_tensor(out=k, in0=pkv[par][:P, 0:D], in1=bkv[:, 0:D], op=ALU.add).then_inc(ch, 1)
                    e.wait_ge(ch, c.next())
                    v.tensor_tensor(out=VS[:, bass.ds(t * VW, D)], in0=pkv[par][:P, D:2 * D], in1=bkv[:, D:2 * D], op=ALU.add).then_inc(S["pkv_free"][par], 1)
                    v.tensor_tensor(out=kmax[:, :], in0=kmax[:, :], in1=k, op=ALU.max).then_inc(ch, 1)
                    e.wait_ge(ch, c.next())
                    c.reset()
                norm(0, 0)
                norm(1, 1)
                with e.Fori(0, T // 2 - 1) as i:
                    for par in range(2):
                        norm(i * 2 + par + 2, par)
                        keep(i * 2 + par, par)
                keep(T - 2, 0)
                keep(T - 1, 1)

            @block.scalar
            def _(e):
                a = nc.scalar

                def transposed(par):
                    e.wait_ge(pT_ready, 1)
                    e.sem_inc(pT_ready, -1)
                    e.sem_inc(S["xn_free"][par], 1)
                    e.wait_ge(S["xo_free"][par], 1)
                    e.sem_inc(S["xo_free"][par], -1)
                    a.activation(xo[:, par, :], pT[:, 0:2 * P], ACT.Copy).then_inc(S["xo_ready"][par], 1)
                    a.activation(xT[:, par, :], pT[:, 0:2 * P], ACT.Copy).then_inc(xT_ready, 1)

                def body(t, par, last=False):
                    if not last:
                        transposed(1 - par)
                    e.wait_ge(pz_ready, 1)
                    e.sem_inc(pz_ready, -1)
                    e.wait_ge(S["zr_free"][par], 1)
                    e.sem_inc(S["zr_free"][par], -1)
                    a.activation(zr[:, par, :], pz[:P, 0:ZW + HEADS], ACT.Copy).then_inc(S["zr_ready"][par], 1)
                    a.activation(edn[:, bass.ds(t * HEADS, HEADS)], pz[:P, ZW:ZW + HEADS], ACT.Copy).then_inc(pz_free, 1)
                    e.drain().then_inc(row_ready, 1)
                for par in range(2):
                    e.sem_inc(S["zr_free"][par], 1)
                    e.sem_inc(S["xo_free"][par], 1)
                transposed(0)
                with e.Fori(0, T // 2 - 1) as i:
                    body(i * 2, 0)
                    body(i * 2 + 1, 1)
                body(T - 2, 0)
                body(T - 1, 1, last=True)
                e.drain().then_inc(ed_done, 1)

            @block.gpsimd
            def _(e):
                scatter_edge_inputs(e, ed, edn, edge_ed, row_ready, scattered)

            @block.sync
            def _(e):
                def input_out(t, par):
                    e.wait_ge(S["xo_ready"][par], 1)
                    e.sem_inc(S["xo_ready"][par], -1)
                    e.dma_start(xT_dram[bass.ds(t * 128, 128), :], xo[:, par, :]).then_inc(S["xo_stored"][par], 16)

                def input_stored(par):
                    e.wait_ge(S["xo_stored"][par], 16)
                    e.sem_inc(S["xo_stored"][par], -16)
                    e.sem_inc(S["xo_free"][par], 1)

                def rows_out(t, par):
                    e.wait_ge(S["zr_ready"][par], 1)
                    e.sem_inc(S["zr_ready"][par], -1)
                    e.dma_start(zt_v[:, bass.ds(t * ZW, ZW)], zr[:, par, 0:ZW]).then_inc(S["zr_stored"][par], 16)

                def rows_stored(par):
                    e.wait_ge(S["zr_stored"][par], 16)
                    e.sem_inc(S["zr_stored"][par], -16)
                    e.sem_inc(S["zr_free"][par], 1)

                def step(t, par):
                    input_out(t + 1, 1 - par)
                    input_stored(par)
                    rows_out(t, par)
                    rows_stored(1 - par)
                input_out(0, 0)
                input_out(1, 1)
                input_stored(0)
                rows_out(0, 0)
                with e.Fori(0, T // 2 - 1) as i:
                    step(i * 2 + 1, 1)
                    step(i * 2 + 2, 0)
                input_stored(1)
                rows_out(T - 1, 1)
                rows_stored(0)
                rows_stored(1)
                e.wait_ge(ed_done, 1)
                e.sem_inc(ed_done, -1)
                e.dma_start(edt.rearrange("(p t) w -> p (t w)", t=T), edn[:, :]).then_inc(edst, 16)
                e.wait_ge(edst, 16)
                e.sem_inc(edst, -16)

            @block.tensor
            def _(e):
                t_ = nc.tensor
                e.sem_inc(pz_free, 1)
                for par in range(2):
                    e.sem_inc(S["pkv_free"][par], 1)

                def transposes(par):
                    e.wait_ge(S["xn_ready"][par], 1)
                    e.sem_inc(S["xn_ready"][par], -1)
                    for b in range(2):
                        ins = t_.transpose(pT[:, b * P:(b + 1) * P], xn[:, par, b * 128:(b + 1) * 128], const.ident[:P, :P])
                    ins.then_inc(pT_ready, 1)

                def body(par, last=False):
                    e.wait_ge(xT_ready, 1)
                    e.sem_inc(xT_ready, -1)
                    if not last:
                        transposes(1 - par)
                    e.wait_ge(pz_free, 1)
                    e.sem_inc(pz_free, -1)
                    for b in range(2):
                        ins = t_.matmul(pz[:P, 0:ZW + HEADS], xT[:, par, b * P:(b + 1) * P], wz[:, b, :], start=b == 0, stop=b == 1)
                    ins.then_inc(pz_ready, 1)
                    e.wait_ge(S["pkv_free"][par], 1)
                    e.sem_inc(S["pkv_free"][par], -1)
                    for n, w in enumerate((wk, wv)):
                        for b in range(2):
                            ins = t_.matmul(pkv[par][:P, n * D:(n + 1) * D], xT[:, par, b * P:(b + 1) * P], w[:, b, :], start=b == 0, stop=b == 1)
                    ins.then_inc(S["pkv_ready"][par], 1)
                transposes(0)
                with e.Fori(0, T // 2 - 1) as i:
                    body(0)
                    body(1)
                body(0)
                body(1, last=True)


def attend1(nc, const, KS, VS, kmax, gbeta, bn):
    with Mem(nc, "a1") as m:
        mT = m.sb("mT", [128, 2])
        dg = m.sb("dg", [128, 2, 128])
        mb = m.sb("mb", [P, D])
        kd = m.sb("kd", [P, 2, 2, D])
        ke = m.sb("ke", [P, 2, 2, D])
        lam = m.sb("lam", [128, 2, D])
        st = m.sb("st", [128, 2, 6])
        ag = m.sb("ag", [128, 2, 2])
        rs = m.sb("rs", [128, 2, 3])
        pm = m.ps("pm")
        pb = m.ps("pb")
        pl = [m.ps("pl0"), m.ps("pl1")]
        ch, mt_ready, dg_ready, mb_ready, lam_ready, var_ready, sd_ready = (m.sem(x) for x in ("ch", "mt_ready", "dg_ready", "mb_ready", "lam_ready", "var_ready", "sd_ready"))
        S = {n: [m.sem(n + "0"), m.sem(n + "1")] for n in ("kd_ready", "kd_free", "ke_ready", "ke_free")}
        with nc.Block() as block:

            @block.tensor
            def _(e):
                t = nc.tensor
                for b in range(2):
                    ins = t.transpose(pm[:, b * P:(b + 1) * P], kmax[:, b * 128:(b + 1) * 128], const.ident[:P, :P])
                ins.then_inc(mt_ready, 1)
                e.wait_ge(dg_ready, 1)
                e.sem_inc(dg_ready, -1)
                for b in range(2):
                    ins = t.matmul(pb[:P, b * 128:(b + 1) * 128], const.ones[:, 0:P], dg[:, b, :], start=True, stop=True)
                ins.then_inc(mb_ready, 1)

                def body(n, par, first=False, last=False):
                    e.wait_ge(S["ke_ready"][par], 1)
                    e.sem_inc(S["ke_ready"][par], -1)
                    for q in range(2):
                        for b in range(2):
                            ins = t.matmul(pl[b][:, 0:VW], ke[:, par, q, b * 128:(b + 1) * 128], VS[:, bass.ds(n * (2 * VW) + q * VW, VW)],
                                           start=first and q == 0, stop=last and q == 1)
                    ins.then_inc(lam_ready if last else S["ke_free"][par], 1)
                body(0, 0, first=True)
                with e.Fori(0, (T // 2 - 3) // 2) as i:
                    body(i * 2 + 1, 1)
                    body(i * 2 + 2, 0)
                body(T // 2 - 2, 1)
                body(T // 2 - 1, 0, last=True)

            @block.scalar
            def _(e):
                e.sem_inc(S["ke_free"][0], 1)
                e.sem_inc(S["ke_free"][1], 1)

                def body(t, par):
                    e.wait_ge(S["kd_ready"][par], 1)
                    e.sem_inc(S["kd_ready"][par], -1)
                    e.wait_ge(S["ke_free"][par], 1)
                    e.sem_inc(S["ke_free"][par], -1)
                    nc.scalar.activation(ke[:, par, :, :], kd[:, par, :, :], ACT.Exp).then_inc(S["ke_ready"][par], 1)
                    e.drain().then_inc(S["kd_free"][par], 1)
                steps(e, T // 2, body)
                e.wait_ge(var_ready, 1)
                e.sem_inc(var_ready, -1)
                nc.scalar.activation(rs[:, :, 1], rs[:, :, 0], ACT.Sqrt).then_inc(sd_ready, 1)

            @block.vector
            def _(e):
                v = nc.vector
                c = Count(e, ch)
                e.wait_ge(mt_ready, 1)
                e.sem_inc(mt_ready, -1)
                v.tensor_reduce(out=mT[:, :], in_=pm[:, 0:2 * P].rearrange("p (b n) -> p b n", b=2), axis=AX.X, op=ALU.max).then_inc(ch, 1)
                e.wait_ge(ch, c.next())
                for b in range(2):
                    v.tensor_scalar(dg[:, b, :], const.ident[:, :], mT[:, b:b + 1], None, ALU.mult).then_inc(ch, 1)
                    e.wait_ge(ch, c.next())
                e.sem_inc(dg_ready, 1)
                e.wait_ge(mb_ready, 1)
                e.sem_inc(mb_ready, -1)
                v.tensor_copy(mb[:, :], pb[:P, 0:D]).then_inc(ch, 1)
                e.wait_ge(ch, c.next())
                for par in range(2):
                    e.sem_inc(S["kd_free"][par], 1)

                def body(t, par):
                    e.wait_ge(S["kd_free"][par], 1)
                    e.sem_inc(S["kd_free"][par], -1)
                    v.tensor_tensor(out=kd[:, par, :, :], in0=KS[:, bass.ds(t * (2 * D), 2 * D)].rearrange("p (q w) -> p q w", w=D),
                                    in1=mb[:, :].unsqueeze(1).to_broadcast([P, 2, D]), op=ALU.subtract).then_inc(S["kd_ready"][par], 1)
                steps(e, T // 2, body)
                e.wait_ge(lam_ready, 1)
                e.sem_inc(lam_ready, -1)
                for b in range(2):
                    v.reciprocal(rs[:, b, 2:3], pl[b][:, D:VW]).then_inc(ch, 1)
                    e.wait_ge(ch, c.next())
                    v.tensor_scalar(lam[:, b, :], pl[b][:, 0:D], rs[:, b, 2:3], None, ALU.mult).then_inc(ch, 1)
                    e.wait_ge(ch, c.next())
                    v.bn_stats(out=st[:, b, :], in_=lam[:, b, :]).then_inc(ch, 1)
                    e.wait_ge(ch, c.next())
                    v.bn_aggr(out=ag[:, b, :], in_=st[:, b, :]).then_inc(ch, 1)
                    e.wait_ge(ch, c.next())
                    v.tensor_scalar(rs[:, b, 0:1], ag[:, b, 1:2], 1e-5, None, ALU.add).then_inc(ch, 1)
                    e.wait_ge(ch, c.next())
                e.sem_inc(var_ready, 1)
                e.wait_ge(sd_ready, 1)
                e.sem_inc(sd_ready, -1)
                for b in range(2):
                    v.reciprocal(rs[:, b, 2:3], rs[:, b, 1:2]).then_inc(ch, 1)
                    e.wait_ge(ch, c.next())
                    v.tensor_scalar(lam[:, b, :], lam[:, b, :], ag[:, b, 0:1], rs[:, b, 2:3], ALU.subtract, ALU.mult).then_inc(ch, 1)
                    e.wait_ge(ch, c.next())
                    v.tensor_scalar(bn[:, b, :], lam[:, b, :], gbeta[:, b:b + 1], gbeta[:, 2 + b:3 + b], ALU.mult, ALU.add).then_inc(ch, 1)
                    e.wait_ge(ch, c.next())
                c.reset()


def query1(nc, const, X, bn, wq_t, bq, xT_dram, bias):
    with Mem(nc, "q1") as m:
        qs = m.sb("qs", [128, 2, 4 * P])
        bs = m.sb("bs", [P, D])
        bqb = m.sb("bqb", [128, 2, P])
        wb = m.sb("wb", [128, 2, D])
        pw = m.ps("pw")
        pb = m.ps("pb")
        ch, bias_ld, bqb_ready, pw_ready, wb_ready = (m.sem(x) for x in ("ch", "bias_ld", "bqb_ready", "pw_ready", "wb_ready"))
        po = [m.ps("po0"), m.ps("po1")]
        S = {n: [m.sem(n + "0"), m.sem(n + "1")] for n in ("q_ld", "q_free", "po_ready", "po_free")}
        with nc.Block() as block:

            @block.sync
            def _(e):
                e.dma_start(bs[:, :], bias.partition_broadcast(P)).then_inc(bias_ld, 16)
                for b in range(2):
                    e.sem_inc(S["q_free"][b], 1)

                def body(n, par):
                    e.wait_ge(S["q_free"][par], 1)
                    e.sem_inc(S["q_free"][par], -1)
                    for t in range(2):
                        e.dma_start(qs[:, par, t * 2 * P:(t + 1) * 2 * P], xT_dram[bass.ds(n * 256 + t * 128, 128), :]).then_inc(S["q_ld"][par], 16)
                steps(e, T // 2, body)

            @block.tensor
            def _(e):
                e.wait_ge(bqb_ready, 1)
                e.sem_inc(bqb_ready, -1)
                for b in range(2):
                    nc.tensor.matmul(pb[:P, 0:D], bqb[:, b, :], bn[:, b, :], start=b == 0, stop=b == 1)
                for o in range(2):
                    for b in range(2):
                        ins = nc.tensor.matmul(pw[:, o * D:(o + 1) * D], wq_t[:, b, o * 128:(o + 1) * 128], bn[:, b, :], start=b == 0, stop=b == 1)
                ins.then_inc(pw_ready, 1)
                e.wait_ge(wb_ready, 1)
                e.sem_inc(wb_ready, -1)
                for b in range(2):
                    e.sem_inc(S["po_free"][b], 1)

                def body(n, par):
                    e.wait_ge(S["q_ld"][par], 32)
                    e.sem_inc(S["q_ld"][par], -32)
                    e.wait_ge(S["po_free"][par], 1)
                    e.sem_inc(S["po_free"][par], -1)
                    for t in range(2):
                        for b in range(2):
                            ins = nc.tensor.matmul(po[par][:P, t * D:(t + 1) * D], qs[:, par, (t * 2 + b) * P:(t * 2 + b + 1) * P], wb[:, b, :], start=b == 0, stop=b == 1)
                    ins.then_inc(S["po_ready"][par], 1)
                steps(e, T // 2, body)

            @block.vector
            def _(e):
                v = nc.vector
                c = Count(e, ch)
                for b in range(2):
                    v.tensor_scalar(bqb[:, b, :], const.ones[:, 0:P], bq[:, b:b + 1], None, ALU.mult).then_inc(ch, 1)
                    e.wait_ge(ch, c.next())
                e.sem_inc(bqb_ready, 1)
                e.wait_ge(bias_ld, 16)
                e.sem_inc(bias_ld, -16)
                e.wait_ge(pw_ready, 1)
                e.sem_inc(pw_ready, -1)
                v.tensor_copy(wb[:, :, :], pw[:, 0:2 * D].rearrange("p (o w) -> p o w", w=D)).then_inc(wb_ready, 1)
                v.tensor_tensor(out=bs[:, :], in0=bs[:, :], in1=pb[:P, 0:D], op=ALU.add).then_inc(ch, 1)
                e.wait_ge(ch, c.next())
                c.reset()

                def body(n, par):
                    xt = X[:, bass.ds(n * (2 * D), 2 * D)]
                    x3 = xt.rearrange("p (q w) -> p q w", w=D)
                    v.tensor_tensor(out=x3, in0=x3, in1=bs[:, :].unsqueeze(1).to_broadcast([P, 2, D]), op=ALU.add).then_inc(ch, 1)
                    e.wait_ge(ch, c.next())
                    e.wait_ge(S["po_ready"][par], 1)
                    e.sem_inc(S["po_ready"][par], -1)
                    e.sem_inc(S["q_free"][par], 1)
                    v.tensor_tensor(out=xt, in0=xt, in1=po[par][:P, 0:2 * D], op=ALU.add).then_inc(S["po_free"][par], 1)
                    c.reset()
                steps(e, T // 2, body)


def route1(nc, const, X, mean, rstd, XN, a, w1, w2, b1, b2):
    with Mem(nc, "r1") as m:
        wr = m.sb("wr", [128, 2, NE])
        br = m.sb("br", [1, NE])
        mrow = m.sb("mrow", [1, D])
        mT = m.sb("mT", [128, 2])
        r = m.sb("r", [1, 8, NE])
        sc = m.sb("sc", [1, 16])
        ids = m.sb("ids", [1, 2], I32)
        wb = m.sb("wb", [128, 2])
        b2s = m.sb("b2s", [P, 2, D])
        pmn = m.ps("pmn")
        pt = m.ps("pt")
        pl = m.ps("pl")
        names = ("ch", "ld", "xn_ready", "sum_ready", "row_ready", "mt_ready", "mts_ready", "lg_ready", "x1", "e1", "x2", "e2", "x3", "e3", "ids_ready", "w_ready", "wb_ready", "wld")
        s = {n: m.sem(n) for n in names}
        with nc.Block() as block:

            @block.sync
            def _(e):
                e.dma_start(wr[:, :, :], a["L1_ffn_Wr"].rearrange("(b i) x -> i b x", b=2)).then_inc(s["ld"], 16)
                e.dma_start(br[:, :], a["L1_ffn_br"].rearrange("(o x) -> o x", o=1)).then_inc(s["ld"], 16)
                e.wait_ge(s["ids_ready"], 1)
                e.sem_inc(s["ids_ready"], -1)
                for n in range(2):
                    i = nc.sync.value_load(ids[0:1, n:n + 1], min_val=0, max_val=NE - 1)
                    e.dma_start(w1[:, n, :, :], a["L1_ffn_W1"].rearrange("x d f -> (x d) f")[bass.ds(i * D, D), :].rearrange("(b i) f -> i b f", b=2)).then_inc(s["wld"], 16)
                    e.dma_start(w2[:, n, :, :], a["L1_ffn_W2"].rearrange("x f d -> (x f) d")[bass.ds(i * F1, F1), :].rearrange("(g f) d -> f g d", f=128)).then_inc(s["wld"], 16)
                    e.dma_start(b1[:, n, :], a["ffn1_b1"][bass.ds(i * 128, 128), :]).then_inc(s["wld"], 16)
                    e.dma_start(b2s[:, n, :], a["ffn1_b2"][bass.ds(i, 1), :].to_broadcast([P, D])).then_inc(s["wld"], 16)

            @block.tensor
            def _(e):
                t = nc.tensor
                def total(t10, first=False, last=False):
                    e.wait_ge(s["xn_ready"], 1)
                    e.sem_inc(s["xn_ready"], -1)
                    for k in range(10):
                        ins = t.matmul(pmn[0:1, 0:D], const.ones[:P, 0:1], XN[:, bass.ds(t10 * (10 * D) + k * D, D)], start=first and k == 0, stop=last and k == 9)
                    return ins
                total(0, first=True)
                with e.Fori(1, T // 10 - 1) as i:
                    total(i)
                total(T // 10 - 1, last=True).then_inc(s["sum_ready"], 1)
                e.wait_ge(s["row_ready"], 1)
                e.sem_inc(s["row_ready"], -1)
                for b in range(2):
                    ins = t.matmul(pt[:, b:b + 1], mrow[0:1, b * 128:(b + 1) * 128], const.ones[0:1, 0:1], start=True, stop=True)
                ins.then_inc(s["mt_ready"], 1)
                e.wait_ge(s["mts_ready"], 1)
                e.sem_inc(s["mts_ready"], -1)
                for b in range(2):
                    ins = t.matmul(pl[0:1, 0:NE], mT[:, b:b + 1], wr[:, b, :], start=b == 0, stop=b == 1)
                ins.then_inc(s["lg_ready"], 1)
                e.wait_ge(s["w_ready"], 1)
                e.sem_inc(s["w_ready"], -1)
                t.matmul(pt[:, 2:4], const.ones[0:1, 0:128], sc[0:1, 8:10], start=True, stop=True).then_inc(s["wb_ready"], 1)

            @block.scalar
            def _(e):
                A = nc.scalar
                e.wait_ge(s["x1"], 1)
                e.sem_inc(s["x1"], -1)
                A.activation(r[:, 1, :], r[:, 0, :], ACT.Exp).then_inc(s["e1"], 1)
                e.wait_ge(s["x2"], 1)
                e.sem_inc(s["x2"], -1)
                A.activation(r[:, 1, :], r[:, 0, :], ACT.Exp).then_inc(s["e2"], 1)
                e.wait_ge(s["x3"], 1)
                e.sem_inc(s["x3"], -1)
                A.activation(sc[:, 5:6], sc[:, 4:5], ACT.Exp).then_inc(s["e3"], 1)

            @block.vector
            def _(e):
                v = nc.vector
                c = Count(e, s["ch"])
                with e.Fori(0, T // 10) as i:
                    for k in range(10):
                        t = i * 10 + k
                        ins = v.tensor_scalar(XN[:, bass.ds(t * D, D)], X[:, bass.ds(t * D, D)], mean[:, bass.ds(t, 1)], rstd[:, bass.ds(t, 1)], ALU.subtract, ALU.mult)
                    ins.then_inc(s["xn_ready"], 1)
                v.memset(sc[:, :], 0.0).then_inc(s["ch"], 1)
                e.wait_ge(s["ch"], c.next())
                e.wait_ge(s["sum_ready"], 1)
                e.sem_inc(s["sum_ready"], -1)
                v.tensor_scalar(mrow[:, :], pmn[0:1, 0:D], 1.0 / N, None, ALU.mult).then_inc(s["ch"], 1)
                e.wait_ge(s["ch"], c.next())
                e.sem_inc(s["row_ready"], 1)
                e.wait_ge(s["mt_ready"], 1)
                e.sem_inc(s["mt_ready"], -1)
                v.tensor_copy(mT[:, :], pt[:, 0:2]).then_inc(s["ch"], 1)
                e.wait_ge(s["ch"], c.next())
                e.wait_ge(s["ld"], 32)
                e.sem_inc(s["ld"], -32)
                e.sem_inc(s["mts_ready"], 1)
                e.wait_ge(s["lg_ready"], 1)
                e.sem_inc(s["lg_ready"], -1)
                v.tensor_tensor(out=r[:, 0, :], in0=pl[0:1, 0:NE], in1=br[:, :], op=ALU.add).then_inc(s["ch"], 1)
                e.wait_ge(s["ch"], c.next())

                def softmax(x, done):
                    v.tensor_reduce(out=sc[:, 0:1], in_=r[:, 0, :], axis=AX.X, op=ALU.max).then_inc(s["ch"], 1)
                    e.wait_ge(s["ch"], c.next())
                    v.tensor_scalar(r[:, 0, :], r[:, 0, :], sc[:, 0:1], None, ALU.subtract).then_inc(s["ch"], 1)
                    e.wait_ge(s["ch"], c.next())
                    e.sem_inc(x, 1)
                    e.wait_ge(done, 1)
                    e.sem_inc(done, -1)
                    v.tensor_reduce(out=sc[:, 1:2], in_=r[:, 1, :], axis=AX.X, op=ALU.add).then_inc(s["ch"], 1)
                    e.wait_ge(s["ch"], c.next())
                    v.reciprocal(sc[:, 1:2], sc[:, 1:2]).then_inc(s["ch"], 1)
                    e.wait_ge(s["ch"], c.next())
                    v.tensor_scalar(r[:, 2, :], r[:, 1, :], sc[:, 1:2], None, ALU.mult).then_inc(s["ch"], 1)
                    e.wait_ge(s["ch"], c.next())
                softmax(s["x1"], s["e1"])
                v.tensor_scalar(r[:, 3, :], r[:, 2, :], float(N), None, ALU.mult).then_inc(s["ch"], 1)
                e.wait_ge(s["ch"], c.next())
                v.tensor_scalar(r[:, 5, :], r[:, 3, :], float(CAP0), None, ALU.is_gt).then_inc(s["ch"], 1)
                e.wait_ge(s["ch"], c.next())
                v.tensor_scalar(r[:, 3, :], r[:, 3, :], float(CAP0), None, ALU.max).then_inc(s["ch"], 1)
                e.wait_ge(s["ch"], c.next())
                v.reciprocal(r[:, 4, :], r[:, 3, :]).then_inc(s["ch"], 1)
                e.wait_ge(s["ch"], c.next())
                v.tensor_scalar(r[:, 4, :], r[:, 4, :], float(CAP0), -1.0, ALU.mult, ALU.add).then_inc(s["ch"], 1)
                e.wait_ge(s["ch"], c.next())
                v.tensor_tensor(out=r[:, 4, :], in0=r[:, 4, :], in1=r[:, 5, :], op=ALU.mult).then_inc(s["ch"], 1)
                e.wait_ge(s["ch"], c.next())
                v.tensor_scalar(r[:, 4, :], r[:, 4, :], 1.0, None, ALU.add).then_inc(s["ch"], 1)
                e.wait_ge(s["ch"], c.next())
                v.tensor_tensor(out=r[:, 0, :], in0=r[:, 2, :], in1=r[:, 4, :], op=ALU.mult).then_inc(s["ch"], 1)
                e.wait_ge(s["ch"], c.next())
                softmax(s["x2"], s["e2"])
                for n in range(2):
                    v.tensor_reduce(out=sc[:, 2 + n:3 + n], in_=r[:, 2, :], axis=AX.X, op=ALU.max).then_inc(s["ch"], 1)
                    e.wait_ge(s["ch"], c.next())
                    v.tensor_scalar(r[:, 3, :], r[:, 2, :], sc[:, 2 + n:3 + n], None, ALU.is_equal).then_inc(s["ch"], 1)
                    e.wait_ge(s["ch"], c.next())
                    v.tensor_scalar(r[:, 3, :], r[:, 3, :], -float(NE), float(NE), ALU.mult, ALU.add).then_inc(s["ch"], 1)
                    e.wait_ge(s["ch"], c.next())
                    v.tensor_tensor(out=r[:, 3, :], in0=r[:, 3, :], in1=const.iota[0:1, 0:NE], op=ALU.add).then_inc(s["ch"], 1)
                    e.wait_ge(s["ch"], c.next())
                    v.tensor_reduce(out=sc[:, 6 + n:7 + n], in_=r[:, 3, :], axis=AX.X, op=ALU.min).then_inc(s["ch"], 1)
                    e.wait_ge(s["ch"], c.next())
                    if n == 0:
                        v.tensor_scalar(r[:, 3, :], const.iota[0:1, 0:NE], sc[:, 6:7], None, ALU.is_equal).then_inc(s["ch"], 1)
                        e.wait_ge(s["ch"], c.next())
                        v.scalar_tensor_tensor(r[:, 2, :], r[:, 3, :], -2.0, r[:, 2, :], ALU.mult, ALU.add).then_inc(s["ch"], 1)
                        e.wait_ge(s["ch"], c.next())
                v.tensor_copy(ids[:, :], sc[:, 6:8]).then_inc(s["ch"], 1)
                e.wait_ge(s["ch"], c.next())
                e.sem_inc(s["ids_ready"], 1)
                v.tensor_tensor(out=sc[:, 4:5], in0=sc[:, 3:4], in1=sc[:, 2:3], op=ALU.subtract).then_inc(s["ch"], 1)
                e.wait_ge(s["ch"], c.next())
                e.sem_inc(s["x3"], 1)
                e.wait_ge(s["e3"], 1)
                e.sem_inc(s["e3"], -1)
                v.tensor_scalar(sc[:, 10:11], sc[:, 5:6], 1.0, None, ALU.add).then_inc(s["ch"], 1)
                e.wait_ge(s["ch"], c.next())
                v.reciprocal(sc[:, 8:9], sc[:, 10:11]).then_inc(s["ch"], 1)
                e.wait_ge(s["ch"], c.next())
                v.tensor_tensor(out=sc[:, 9:10], in0=sc[:, 5:6], in1=sc[:, 8:9], op=ALU.mult).then_inc(s["ch"], 1)
                e.wait_ge(s["ch"], c.next())
                e.sem_inc(s["w_ready"], 1)
                e.wait_ge(s["wb_ready"], 1)
                e.sem_inc(s["wb_ready"], -1)
                v.tensor_copy(wb[:, :], pt[:, 2:4]).then_inc(s["ch"], 1)
                e.wait_ge(s["ch"], c.next())
                e.wait_ge(s["wld"], 128)
                e.sem_inc(s["wld"], -128)
                for n in range(2):
                    v.tensor_scalar(w2[:, n, :, :], w2[:, n, :, :], wb[:, n:n + 1], None, ALU.mult).then_inc(s["ch"], 1)
                    e.wait_ge(s["ch"], c.next())
                    v.tensor_scalar(b2s[:, n, :], b2s[:, n, :], wb[:P, n:n + 1], None, ALU.mult).then_inc(s["ch"], 1)
                    e.wait_ge(s["ch"], c.next())
                v.tensor_tensor(out=b2[:, :], in0=b2s[:, 0, :], in1=b2s[:, 1, :], op=ALU.add).then_inc(s["ch"], 1)
                e.wait_ge(s["ch"], c.next())
                c.reset()


def ffn1(nc, const, X, XN, w1, w2, b1, b2, a, out):
    NF = F1 // 128
    with Mem(nc, "x1") as m:
        gb = m.sb("gb", [P, 2, D])
        xs = m.sb("xs", [P, 4 * D])
        xT = m.sb("xT", [128, 2, 4 * P])
        hT = m.sb("hT", [128, 2 * NF, 4 * P])
        u = m.sb("u", [P, 4, D])
        o = m.sb("o", [P, 2, 4 * D])
        half = m.sb("half", [P, 4])
        stat = m.sb("stat", [P, 4, 6])
        ms = m.sb("ms", [P, 4, 3])
        pT = [m.ps("pT0"), m.ps("pT1")]
        ph = [m.ps(f"ph{i}") for i in range(3)]
        py = [m.ps("py0"), m.ps("py1")]
        names = ("ch", "ld", "xs_ready", "xs_free", "xT_ready", "norm_ready", "norm_done", "g")
        s = {n: m.sem(n) for n in names}
        S = {n: [m.sem(n + "0"), m.sem(n + "1")] for n in ("pT_ready", "py_ready", "py_free", "o_ready", "o_free", "o_st")}
        ph_ready, ph_free = [m.sem(f"ph_ready{i}") for i in range(3)], [m.sem(f"ph_free{i}") for i in range(3)]
        out_v = out.rearrange("(p t) d -> p (t d)", t=T)
        full, rest = T // 4, T % 4

        def tile_steps(e, body):
            steps(e, full, lambda i, par: body(i * 4, par, 4))
            body(full * 4, full % 2, rest)
        with nc.Block() as block:

            @block.gpsimd
            def _(e):
                g = nc.gpsimd
                g.memset(half[:, :], -0.5).then_inc(s["g"], 1)
                e.wait_ge(s["g"], 1)
                e.sem_inc(s["g"], -1)

                def rows(t, n):
                    e.wait_ge(s["xs_free"], 1)
                    e.sem_inc(s["xs_free"], -1)
                    g.tensor_copy(xs[:, 0:n * D], XN[:, bass.ds(t * D, n * D)]).then_inc(s["xs_ready"], 1)

                def deviation():
                    e.wait_ge(s["norm_ready"], 1)
                    e.sem_inc(s["norm_ready"], -1)
                    g.tensor_scalar(ms[:, :, 1], ms[:, :, 1], 1e-5, None, ALU.add).then_inc(s["g"], 1)
                    e.wait_ge(s["g"], 1)
                    e.sem_inc(s["g"], -1)
                    g.tensor_tensor(out=ms[:, :, 2], in0=ms[:, :, 1], in1=half[:, :], op=ALU.pow).then_inc(s["norm_done"], 1)
                rows(0, 4)
                with e.Fori(0, full - 1) as i:
                    rows(i * 4 + 4, 4)
                    deviation()
                rows(full * 4, rest)
                deviation()
                deviation()

            @block.tensor
            def _(e):
                t_ = nc.tensor
                for q in S["py_free"] + ph_free:
                    e.sem_inc(q, 1)
                e.sem_inc(s["xs_free"], 1)

                def transposes(n):
                    e.wait_ge(s["xs_ready"], 1)
                    e.sem_inc(s["xs_ready"], -1)
                    for b in range(2):
                        for q in range(n):
                            ins = t_.transpose(pT[b][:, q * P:(q + 1) * P], xs[:, q * D + b * 128:q * D + b * 128 + 128], const.ident[:P, :P])
                        ins.then_inc(S["pT_ready"][b], 1)

                def body(n, after, first=False):
                    e.wait_ge(s["xT_ready"], 2)
                    e.sem_inc(s["xT_ready"], -2)
                    e.sem_inc(s["xs_free"], 1)
                    for f in range(2 * NF):
                        if f >= 3 or first:
                            e.wait_ge(ph_free[f % 3], 1)
                            e.sem_inc(ph_free[f % 3], -1)
                        x, g = f // NF, f % NF
                        for b in range(2):
                            ins = t_.matmul(ph[f % 3][:, 0:n * P], w1[:, x, b, g * 128:(g + 1) * 128], xT[:, b, 0:n * P], start=b == 0, stop=b == 1)
                        ins.then_inc(ph_ready[f % 3], 1)
                    if after:
                        transposes(after)
                    for q in range(n):
                        e.wait_ge(S["py_free"][q % 2], 1)
                        e.sem_inc(S["py_free"][q % 2], -1)
                        for f in range(2 * NF):
                            if q == 0 and f >= 2 * NF - 3:
                                e.wait_ge(ph_free[f % 3], 1)
                                e.sem_inc(ph_free[f % 3], -1)
                            ins = t_.matmul(py[q % 2][:P, 0:D], hT[:, f, q * P:(q + 1) * P], w2[:, f // NF, f % NF, :], start=f == 0, stop=f == 2 * NF - 1)
                        ins.then_inc(S["py_ready"][q % 2], 1)
                transposes(4)
                body(4, 4, first=True)
                with e.Fori(0, full - 2) as i:
                    body(4, 4)
                body(4, rest)
                body(rest, 0)

            @block.scalar
            def _(e):
                A = nc.scalar

                def transposed(n):
                    for b in range(2):
                        e.wait_ge(S["pT_ready"][b], 1)
                        e.sem_inc(S["pT_ready"][b], -1)
                        A.activation(xT[:, b, 0:n * P], pT[b][:, 0:n * P], ACT.Copy).then_inc(s["xT_ready"], 1)

                def body(n, after):
                    for f in range(2 * NF):
                        e.wait_ge(ph_ready[f % 3], 1)
                        e.sem_inc(ph_ready[f % 3], -1)
                        A.activation(hT[:, f, 0:n * P], ph[f % 3][:, 0:n * P], ACT.Gelu, bias=b1[:, f // NF, f % NF:f % NF + 1]).then_inc(ph_free[f % 3], 1)
                    if after:
                        transposed(after)
                transposed(4)
                with e.Fori(0, full - 1) as i:
                    body(4, 4)
                body(4, rest)
                body(rest, 0)

            @block.vector
            def _(e):
                v = nc.vector
                c = Count(e, s["ch"])
                for b in range(2):
                    e.sem_inc(S["o_free"][b], 1)
                e.wait_ge(s["ld"], 32)
                e.sem_inc(s["ld"], -32)
                v.memset(ms[:, :, :], 1.0).then_inc(s["ch"], 1)
                e.wait_ge(s["ch"], c.next())

                def body(t, par, n):
                    v.tensor_tensor(out=u[:, 0:n, :], in0=XN[:, bass.ds(t * D, n * D)].rearrange("p (k w) -> p k w", w=D),
                                    in1=b2[:, :].unsqueeze(1).to_broadcast([P, n, D]), op=ALU.add).then_inc(s["ch"], 1)
                    e.wait_ge(s["ch"], c.next())
                    for q in range(n):
                        e.wait_ge(S["py_ready"][q % 2], 1)
                        e.sem_inc(S["py_ready"][q % 2], -1)
                        v.tensor_tensor(out=u[:, q, :], in0=py[q % 2][:P, 0:D], in1=u[:, q, :], op=ALU.add).then_inc(s["ch"], 1)
                        e.wait_ge(s["ch"], c.next())
                        e.sem_inc(S["py_free"][q % 2], 1)
                        v.bn_stats(out=stat[:, q, :], in_=u[:, q, :]).then_inc(s["ch"], 1)
                        e.wait_ge(s["ch"], c.next())
                        v.bn_aggr(out=ms[:, q, 0:2], in_=stat[:, q, :]).then_inc(s["ch"], 1)
                        e.wait_ge(s["ch"], c.next())
                    e.sem_inc(s["norm_ready"], 1)
                    e.wait_ge(s["norm_done"], 1)
                    e.sem_inc(s["norm_done"], -1)
                    for q in range(n):
                        v.tensor_scalar(u[:, q, :], u[:, q, :], ms[:, q, 0:1], ms[:, q, 2:3], ALU.subtract, ALU.mult)
                    v.memset(stat[:, :, :], 0.0).then_inc(s["ch"], 1)
                    e.wait_ge(s["ch"], c.next())
                    v.tensor_tensor(out=u[:, 0:n, :], in0=u[:, 0:n, :], in1=gb[:, 0, :].unsqueeze(1).to_broadcast([P, n, D]), op=ALU.mult).then_inc(s["ch"], 1)
                    e.wait_ge(s["ch"], c.next())
                    v.tensor_tensor(out=u[:, 0:n, :], in0=u[:, 0:n, :], in1=gb[:, 1, :].unsqueeze(1).to_broadcast([P, n, D]), op=ALU.add).then_inc(s["ch"], 1)
                    e.wait_ge(s["ch"], c.next())
                    e.wait_ge(S["o_free"][par], 1)
                    e.sem_inc(S["o_free"][par], -1)
                    v.tensor_tensor(out=o[:, par, 0:n * D].rearrange("p (k w) -> p k w", w=D), in0=u[:, 0:n, :],
                                    in1=X[:, bass.ds(t * D, n * D)].rearrange("p (k w) -> p k w", w=D), op=ALU.add).then_inc(s["ch"], 1)
                    e.wait_ge(s["ch"], c.next())
                    e.sem_inc(S["o_ready"][par], 1)
                    c.reset()
                c.reset()
                tile_steps(e, body)

            @block.sync
            def _(e):
                for n, name in enumerate(("L1_ffn_gamma", "L1_ffn_beta")):
                    e.dma_start(gb[:, n, :], a[name].partition_broadcast(P)).then_inc(s["ld"], 16)

                def body(t, par, n):
                    e.wait_ge(S["o_ready"][par], 1)
                    e.sem_inc(S["o_ready"][par], -1)
                    e.dma_start(out_v[:, bass.ds(t * D, n * D)], o[:, par, 0:n * D]).then_inc(S["o_st"][par], 16)
                    e.wait_ge(S["o_st"][par], 16)
                    e.sem_inc(S["o_st"][par], -16)
                    e.sem_inc(S["o_free"][par], 1)
                tile_steps(e, body)


class Const:

    def __init__(self, m):
        self.all = m.sb("const", [128, 4 * 128 + CK])
        self.ident = self.all[:, 0:128]
        self.tri = self.all[:, 128:256]
        self.iota = self.all[:, 256:384]
        self.ones = self.all[:, 384:512]
        self.rowbase = self.all[:, 512:512 + CK]


def const_table():
    import numpy as np
    out = np.zeros((128, 4 * 128 + CK), np.float32)
    out[:, 0:128] = np.eye(128)
    out[:, 128:256] = np.triu(np.ones((128, 128)), 1)
    out[:, 256:384] = np.arange(128)[None, :]
    out[:, 384:512] = 1.0
    c = np.arange(CP)[:, None] * CK + np.arange(CK)[None, :]
    out[:CP, 512:] = (c // BC) * (P * BC) + c % BC
    return out


def network(nc, a, out):
    dram = lambda n, shape, dt=F32: nc.dram_tensor(n, list(shape), dt).ap()
    start_dram = dram("start_dram", [C, J])
    zt = dram("zt", [N, ZW])
    edt = dram("edt", [N, HEADS])
    edge_ed = dram("edge_ed", [E + BC * J, HEADS])
    sums = dram("sums", [NB * P * BC, GW])
    extras = dram("extras", [C, GW])
    bufx = dram("bufx", [NE * ER, D])
    bufy = dram("bufy", [NE * ER, D])
    xT_dram = dram("xT_dram", [T * 128, 2 * P])
    with Mem(nc, "g") as m:
        const = Const(m)
        ed = Edges(m)
        X = m.sb("X", [P, T * D])
        mean = m.sb("mean", [P, T])
        rstd = m.sb("rstd", [P, T])
        loaded = m.sem("loaded")
        with nc.Block() as block:
            @block.sync
            def _(e):
                e.dma_start(const.all[:, :], a["consts"][:, :]).then_inc(loaded, 16)
                e.wait_ge(loaded, 16)
                e.sem_inc(loaded, -16)
        zeros = [bufx.rearrange("(p r w) d -> p r (w d)", p=125, r=16), edge_ed.rearrange("(p r w) h -> p r (w h)", p=120, r=5)]
        edge_tables(nc, ed, const, a["src"], a["dst"], start_dram, X, a["x"], zeros)
        norm_stats(nc, "n0", X, mean, rstd, 1e-5)
        with Mem(nc, "l0") as l:
            edn = l.sb("edn", [P, T * HEADS])
            kv = l.sb("kv", [128, 2 * 132])
            with Mem(nc, "q") as mq:
                qT = mq.sb("qT", [128, T * 2 * P])
                wz = mq.sb("wz", [128, 2, ZW + HEADS])
                wkv = mq.sb("wkv", [128, 2, 2 * D])
                wq = mq.sb("wq", [128, 2, D])
                with nc.Block() as block:
                    @block.sync
                    def _(e):
                        w = a["mix_wqkv"].rearrange("(b i) o -> i b o", b=2)
                        e.dma_start(wq[:, :, :], w[:, :, 0:D]).then_inc(loaded, 16)
                        e.dma_start(wkv[:, :, :], w[:, :, D:3 * D]).then_inc(loaded, 16)
                        e.wait_ge(loaded, 32)
                        e.sem_inc(loaded, -32)
                gat_weights(nc, "gw0", a["gnn0_w_in"], a["gnn0_w_out"], a["gnn0_att"], wz)
                dense0(nc, const, ed, X, mean, rstd, wz, wkv, wq, zt, edt, edn, edge_ed, qT, kv)
                mix0(nc, const, X, mean, rstd, qT, kv, a)
            chunk_edge_inputs(nc, "gi0", ed, edt, edge_ed)
            gat_edges(nc, "ge0", const, ed, zt, edge_ed, sums, 0.01)
            with Mem(nc, "rs0") as r:
                row_stats = r.sb("row_stats", [P, T * 6])
                gat_merge(nc, "gm0", const, ed, X, sums, extras, row_stats)
                norm_stats(nc, "n1", X, mean, rstd, 1e-5, row_stats)
        with Mem(nc, "f0") as l:
            back_idx = l.sb("back_idx", [P, T], I32)
            wgt = l.sb("wgt", [P, T])
            with Mem(nc, "f0g") as g:
                XN = g.sb("XN", [P, T * D])
                slot_idx = g.sb("slot_idx", [P, T], I32)
                gw = g.sb("gw", [128, 2, NE])
                gb = g.sb("gb", [P, NE])
                with nc.Block() as block:
                    @block.sync
                    def _(e):
                        e.dma_start(gw[:, :, :], a["L0_ffn_gate_w"].rearrange("(b i) x -> i b x", b=2)).then_inc(loaded, 16)
                        e.dma_start(gb[:, :], a["L0_ffn_gate_b"].partition_broadcast(P)).then_inc(loaded, 16)
                        e.wait_ge(loaded, 32)
                        e.sem_inc(loaded, -32)
                moe_gate(nc, const, X, mean, rstd, XN, gw, gb, bufx, slot_idx, back_idx, wgt)
            moe_experts(nc, const, bufx, bufy, a["L0_ffn_w1"].rearrange("x d f -> (x d) f"), a["L0_ffn_w2"].rearrange("x f d -> (x f) d"),
                        a["ffn0_b1"], a["L0_ffn_b2"])
            row_stats = l.sb("row_stats", [P, T * 6])
            moe_return(nc, X, bufy, back_idx, wgt, row_stats)
            norm_stats(nc, "n2", X, mean, rstd, 1e-5, row_stats)
        with Mem(nc, "l1") as l:
            edn = l.sb("edn", [P, T * HEADS])
            with Mem(nc, "l1m") as g:
                VS = g.sb("VS", [P, T * VW])
                KS = g.sb("KS", [P, T * D])
                wz = g.sb("wz", [128, 2, ZW + HEADS])
                wq_t = g.sb("wq_t", [128, 2, D])
                wk = g.sb("wk", [128, 2, D])
                wv = g.sb("wv", [128, 2, D])
                bkv = g.sb("bkv", [P, 2 * D])
                bq = g.sb("bq", [128, 2])
                gbeta = g.sb("gbeta", [128, 4])
                kmax = g.sb("kmax", [P, D])
                bn = g.sb("bn", [128, 2, D])
                with nc.Block() as block:
                    @block.sync
                    def _(e):
                        e.dma_start(wq_t[:, :, :], a["mix1_wq_t"].rearrange("(b i) o -> i b o", b=2)).then_inc(loaded, 16)
                        e.dma_start(wk[:, :, :], a["L1_mix_W_qk"][1, :, :].rearrange("(b i) o -> i b o", b=2)).then_inc(loaded, 16)
                        e.dma_start(wv[:, :, :], a["L1_mix_W_v"].rearrange("(b i) o -> i b o", b=2)).then_inc(loaded, 16)
                        e.dma_start(bkv[:, 0:D], a["L1_mix_b_qk"][1, :].partition_broadcast(P)).then_inc(loaded, 16)
                        e.dma_start(bkv[:, D:2 * D], a["L1_mix_b_v"].partition_broadcast(P)).then_inc(loaded, 16)
                        e.dma_start(bq[:, :], a["mix1_bq"]).then_inc(loaded, 16)
                        e.dma_start(gbeta[:, :], a["mix1_gbeta"]).then_inc(loaded, 16)
                        e.wait_ge(loaded, 112)
                        e.sem_inc(loaded, -112)
                gat_weights(nc, "gw1", a["L1_gnn_W"], a["gnn1_w_out"], a["gnn1_att"], wz)
                dense1(nc, const, ed, X, mean, rstd, wz, wk, wv, bkv, zt, edt, edn, edge_ed, KS, VS, kmax, xT_dram)
                attend1(nc, const, KS, VS, kmax, gbeta, bn)
                query1(nc, const, X, bn, wq_t, bq, xT_dram, a["L1_gnn_bias"])
            chunk_edge_inputs(nc, "gi1", ed, edt, edge_ed)
            gat_edges(nc, "ge1", const, ed, zt, edge_ed, sums, 0.2)
            with Mem(nc, "rs1") as r:
                row_stats = r.sb("row_stats", [P, T * 6])
                gat_merge(nc, "gm1", const, ed, X, sums, extras, row_stats, zt=zt, edn=edn, slope=0.2)
                norm_stats(nc, "n3", X, mean, rstd, 1e-5, row_stats)
        with Mem(nc, "f1") as l:
            XN = l.sb("XN", [P, T * D])
            w1 = l.sb("w1", [128, 2, 2, F1])
            w2 = l.sb("w2", [128, 2, F1 // 128, D])
            b1 = l.sb("b1", [128, 2, F1 // 128])
            b2 = l.sb("b2", [P, D])
            route1(nc, const, X, mean, rstd, XN, a, w1, w2, b1, b2)
            ffn1(nc, const, X, XN, w1, w2, b1, b2, a, out)


def kernel(**inputs):
    import numpy as _np
    import concourse.bacc as _bacc
    from concourse.bass_utils import run_bass_kernel_spmd as _run

    nc = _bacc.Bacc("TRN2", target_bir_lowering=False, num_devices=1)
    data = {k: _np.asarray(v) for k, v in inputs.items()}
    data["consts"] = const_table()
    data["mix_wqkv"] = _np.transpose(data.pop("L0_mix_Wqkv"))
    data["mix_w1"] = _np.transpose(data.pop("L0_mix_W1"))
    data["mix_w2"] = _np.transpose(data.pop("L0_mix_W2"))
    data["mix_b1"] = _np.transpose(data.pop("L0_mix_b1").reshape(2, 128))
    data["ffn0_b1"] = _np.transpose(data.pop("L0_ffn_b1").reshape(NE * F0 // 128, 128))
    data["ffn1_b1"] = _np.transpose(data.pop("L1_ffn_b1").reshape(NE, F1 // 128, 128), (0, 2, 1)).reshape(NE * 128, F1 // 128)
    data["ffn1_b2"] = data.pop("L1_ffn_b2")
    data["mix1_wq_t"] = _np.transpose(data["L1_mix_W_qk"][0])
    data["mix1_bq"] = _np.transpose(data["L1_mix_b_qk"][0].reshape(2, 128))
    data["mix1_gbeta"] = _np.concatenate([_np.transpose(data.pop(n).reshape(2, 128)) for n in ("L1_mix_gamma", "L1_mix_beta")], 1)
    data["gnn1_w_out"] = _np.transpose(data["L1_gnn_W"].reshape(D, HEADS, DO), (2, 1, 0))
    att = [data.pop(n).reshape(HEADS, DO) for n in ("L1_gnn_att_src", "L1_gnn_att_dst")]
    data["gnn1_att"] = _np.transpose(_np.concatenate(att, 0))
    w = data.pop("L0_gnn_W")
    data["gnn0_w_in"] = _np.transpose(w, (2, 0, 1)).reshape(D, D)
    data["gnn0_w_out"] = _np.transpose(w, (1, 0, 2))
    att = data.pop("L0_gnn_att").reshape(HEADS, 2, DO)
    data["gnn0_att"] = _np.transpose(att, (2, 1, 0)).reshape(DO, 2 * HEADS)
    arrays, args = {}, {}
    for name, x in data.items():
        x = _np.ascontiguousarray(x)
        arrays[f"in_{name}"] = x
        args[name] = nc.dram_tensor(f"in_{name}", x.shape, mybir.dt.from_np(x.dtype), kind="ExternalInput").ap()
    out = nc.dram_tensor("out", (N, D), F32, kind="ExternalOutput").ap()
    network(nc, args, out)
    r = _run(nc, [arrays], core_ids=[0])
    return r.results[0]["out"]
```
